# Optimizing a Trainium2 kernel written in Bass

```python
import numpy as np
import jax
import jax.numpy as jnp

def _softmax(x, axis=-1):
    return jax.nn.softmax(x, axis=axis)

def _gelu(x):
    return jax.nn.gelu(x, approximate=True)

def _silu(x):
    return jax.nn.silu(x)

def _sigmoid(x):
    return jax.nn.sigmoid(x)

def _layernorm(x, axis=-1, eps=1e-05):
    m = jnp.mean(x, axis=axis, keepdims=True)
    v = jnp.var(x, axis=axis, keepdims=True)
    return (x - m) / jnp.sqrt(v + eps)

def _scatter_add(tgt, idx, src, axis=0):
    return tgt.at[idx].add(src)

def _segment_sum(src, seg, n):
    return jax.ops.segment_sum(src, seg, n)
kernel_name = 'mk_gnn_preln_d4_gnn_r32_c52d49'

def setup_inputs(seed: int=0):
    np.random.seed(seed)
    _w = jnp.asarray

    def _rec_inputs():
        import jax
        import jax.numpy as jnp
        _gk = jax.random.key(seed)
        x = 3.989e-05 + 0.1 * jax.random.normal(jax.random.fold_in(_gk, 1), (3125, 64), jnp.float32)
        _s = jax.random.randint(jax.random.fold_in(_gk, 2), (25000,), 0, 3125, jnp.int32)
        _d = jax.random.randint(jax.random.fold_in(_gk, 3), (25000,), 0, 3125, jnp.int32)
        _loop = jnp.arange(3125, dtype=jnp.int32)
        src = jnp.concatenate([_s, _d, _loop])
        dst = jnp.concatenate([_d, _s, _loop])
        _o = jnp.argsort(dst, stable=True)
        src = src[_o]
        dst = dst[_o]
        edge_attr_64 = 0.000241658 + 0.999772 * jax.random.normal(jax.random.fold_in(_gk, 12), (53125, 64), jnp.float32)
        edge_attr_8 = 0.000113954 + 0.49997 * jax.random.normal(jax.random.fold_in(_gk, 13), (53125, 8), jnp.float32)
        edge_type_64 = jax.random.randint(jax.random.fold_in(_gk, 15), (53125,), 0, 64, jnp.int32)
        edge_weight = jax.random.uniform(jax.random.fold_in(_gk, 16), (53125,), jnp.float32, 0.0, 1.39999)
        return (x, src, dst, edge_attr_64, edge_attr_8, edge_type_64, edge_weight)
    x, src, dst, edge_attr_64, edge_attr_8, edge_type_64, edge_weight = _rec_inputs()

    def _L0_gnn_setup():
        import jax, jax.numpy as jnp
        import numpy as np
        N_HOPS = 2
        NEG_SLOPE = 0.2

        def _hop(emb, head, tail, rel_e, W, N):
            a_input = jnp.concatenate([emb[head], emb[tail]], axis=-1)
            e = jnp.sum(a_input @ W * rel_e, axis=-1)
            e = jax.nn.leaky_relu(e, NEG_SLOPE)
            seg_max = jax.ops.segment_max(e, head, num_segments=N)
            ex = jnp.exp(e - seg_max[head])
            denom = jax.ops.segment_sum(ex, head, num_segments=N)
            alpha = ex / denom[head]
            agg = jax.ops.segment_sum(emb[tail] * alpha[:, None], head, num_segments=N)
            return agg + emb
        key = jax.random.key(seed)
        k1, k2, k3, k4, k5 = jax.random.split(key, 5)
        N, E, D, R = (3125, 50000, 64, 64)
        edge_index = jax.random.randint(k1, (2, E), 0, N, dtype=jnp.int64)
        edge_type = jax.random.randint(k2, (E,), 0, R, dtype=jnp.int64)
        entity_emb = jax.random.normal(k3, (N, D), dtype=jnp.float32) * 0.1
        relation_emb = jax.random.normal(k4, (R, D), dtype=jnp.float32) * 0.1
        W = jax.random.normal(k5, (2 * D, D), dtype=jnp.float32) * 0.1
        return {'edge_index': edge_index, 'edge_type': edge_type, 'entity_emb': entity_emb, 'relation_emb': relation_emb, 'W': W}
    _L0_gnn_all = _L0_gnn_setup()
    _L0_gnn_in = {k: v for k, v in _L0_gnn_all.items() if k in ('relation_emb', 'W')}
    del _L0_gnn_all

    def _L1_gnn_setup():
        import jax, jax.numpy as jnp
        import numpy as np
        N, K, D, S, B, H = (256, 16, 64, 8, 64, 4)
        E = N * K
        F = D * (1 + S)
        HID = 64

        def _mlp(x, W1, W2, W3):
            h = jax.nn.gelu(x @ W1)
            h = jax.nn.gelu(h @ W2)
            return h @ W3
        key = jax.random.key(seed)
        ks = jax.random.split(key, 12)

        def w(k, shape):
            return jax.random.normal(k, shape, jnp.float32) / np.sqrt(shape[0])
        node_feat = jax.random.normal(ks[0], (N, D), jnp.float32)
        edge_sh = jax.random.normal(ks[1], (E, S), jnp.float32) * 0.5
        edge_inv = jax.random.normal(ks[2], (E, B), jnp.float32)
        edge_weight_cutoff = jax.random.uniform(ks[3], (E,), jnp.float32, 0.05, 1.4)
        edge_src = jax.random.randint(ks[4], (E,), 0, N, jnp.int32)
        edge_dst = jnp.repeat(jnp.arange(N, dtype=jnp.int32), K)
        return {'node_feat': node_feat, 'edge_sh': edge_sh, 'edge_inv': edge_inv, 'edge_weight_cutoff': edge_weight_cutoff, 'Wk1': w(ks[5], (B, HID)), 'Wk2': w(ks[6], (HID, HID)), 'Wk3': w(ks[7], (HID, F)), 'Wv1': w(ks[8], (B, HID)), 'Wv2': w(ks[9], (HID, HID)), 'Wv3': w(ks[10], (HID, F)), 'W_logit': jax.random.normal(ks[11], (2 * D, H), jnp.float32) / np.sqrt(2 * D), 'W_out': jax.random.normal(jax.random.fold_in(key, 99), (F, D), jnp.float32) / np.sqrt(F), 'edge_src': edge_src, 'edge_dst': edge_dst}
    _L1_gnn_all = _L1_gnn_setup()
    _L1_gnn_in = {k: v for k, v in _L1_gnn_all.items() if k in ('Wk1', 'Wk2', 'Wk3', 'Wv1', 'Wv2', 'Wv3', 'W_logit', 'W_out')}
    del _L1_gnn_all

    def _L2_gnn_setup():
        import jax, jax.numpy as jnp
        import numpy as np
        N = 3125
        E = 50000
        D = 64
        EPS = 1e-05

        def _gcn_conv(x, W, b, src, dst, edge_weight, n):
            h = x @ W
            loop = jnp.arange(n, dtype=src.dtype)
            s = jnp.concatenate([src, loop])
            d = jnp.concatenate([dst, loop])
            w = jnp.concatenate([edge_weight, jnp.ones((n,), x.dtype)])
            deg = jax.ops.segment_sum(w, d, num_segments=n)
            dinv = jnp.where(deg > 0, jax.lax.rsqrt(deg), 0.0)
            norm = dinv[s] * w * dinv[d]
            msg = h[s] * norm[:, None]
            out = jax.ops.segment_sum(msg, d, num_segments=n)
            return out + b
        key = jax.random.key(seed)
        ks = jax.random.split(key, 6)
        x = jax.random.normal(ks[0], (N, D), dtype=jnp.float32)
        edge_index = jax.random.randint(ks[1], (2, E), 0, N, dtype=jnp.int32)
        edge_feature = jax.random.uniform(ks[2], (E,), dtype=jnp.float32)
        scale = 1.0 / np.sqrt(D)
        W1 = jax.random.normal(ks[3], (D, D), dtype=jnp.float32) * scale
        b1 = jnp.zeros((D,), jnp.float32)
        gamma = jnp.ones((D,), jnp.float32)
        beta = jnp.zeros((D,), jnp.float32)
        W2 = jax.random.normal(ks[4], (D, D), dtype=jnp.float32) * scale
        b2 = jnp.zeros((D,), jnp.float32)
        return {'x': x, 'edge_index': edge_index, 'edge_feature': edge_feature, 'W1': W1, 'b1': b1, 'gamma': gamma, 'beta': beta, 'W2': W2, 'b2': b2}
    _L2_gnn_all = _L2_gnn_setup()
    _L2_gnn_in = {k: v for k, v in _L2_gnn_all.items() if k in ('W1', 'b1', 'gamma', 'beta', 'W2', 'b2')}
    del _L2_gnn_all

    def _L3_gnn_setup():
        import jax, jax.numpy as jnp
        import numpy as np
        N_NODES = 3125
        N_EDGES = 50000
        D = 64
        key = jax.random.key(seed)
        ks = jax.random.split(key, 9)
        x = jax.random.normal(ks[0], (N_NODES, D), dtype=jnp.float32)
        edge_index = jax.random.randint(ks[1], (2, N_EDGES), 0, N_NODES, dtype=jnp.int64)
        W_self = jax.random.normal(ks[2], (D, D), dtype=jnp.float32) * D ** (-0.5)
        b_self = jax.random.normal(ks[3], (D,), dtype=jnp.float32) * 0.01
        W_neigh = jax.random.normal(ks[4], (D, D), dtype=jnp.float32) * D ** (-0.5)
        b_neigh = jax.random.normal(ks[5], (D,), dtype=jnp.float32) * 0.01
        W_var = jax.random.normal(ks[6], (D, D), dtype=jnp.float32) * D ** (-0.5)
        b_var = jax.random.normal(ks[7], (D,), dtype=jnp.float32) * 0.01
        return {'x': x, 'edge_index': edge_index, 'W_self': W_self, 'b_self': b_self, 'W_neigh': W_neigh, 'b_neigh': b_neigh, 'W_var': W_var, 'b_var': b_var}
    _L3_gnn_all = _L3_gnn_setup()
    _L3_gnn_in = {k: v for k, v in _L3_gnn_all.items() if k in ('W_self', 'b_self', 'W_neigh', 'b_neigh', 'W_var', 'b_var')}
    del _L3_gnn_all
    return {'x': x, 'src': src, 'dst': dst, 'edge_attr_64': edge_attr_64, 'edge_attr_8': edge_attr_8, 'edge_type_64': edge_type_64, 'edge_weight': edge_weight, 'L0_gnn_relation_emb': _L0_gnn_in['relation_emb'], 'L0_gnn_W': _L0_gnn_in['W'], 'L1_gnn_Wk1': _L1_gnn_in['Wk1'], 'L1_gnn_Wk2': _L1_gnn_in['Wk2'], 'L1_gnn_Wk3': _L1_gnn_in['Wk3'], 'L1_gnn_Wv1': _L1_gnn_in['Wv1'], 'L1_gnn_Wv2': _L1_gnn_in['Wv2'], 'L1_gnn_Wv3': _L1_gnn_in['Wv3'], 'L1_gnn_W_logit': _L1_gnn_in['W_logit'], 'L1_gnn_W_out': _L1_gnn_in['W_out'], 'L2_gnn_W1': _L2_gnn_in['W1'], 'L2_gnn_b1': _L2_gnn_in['b1'], 'L2_gnn_gamma': _L2_gnn_in['gamma'], 'L2_gnn_beta': _L2_gnn_in['beta'], 'L2_gnn_W2': _L2_gnn_in['W2'], 'L2_gnn_b2': _L2_gnn_in['b2'], 'L3_gnn_W_self': _L3_gnn_in['W_self'], 'L3_gnn_b_self': _L3_gnn_in['b_self'], 'L3_gnn_W_neigh': _L3_gnn_in['W_neigh'], 'L3_gnn_b_neigh': _L3_gnn_in['b_neigh'], 'L3_gnn_W_var': _L3_gnn_in['W_var'], 'L3_gnn_b_var': _L3_gnn_in['b_var']}

def reference(x, src, dst, edge_attr_64, edge_attr_8, edge_type_64, edge_weight, L0_gnn_relation_emb, L0_gnn_W, L1_gnn_Wk1, L1_gnn_Wk2, L1_gnn_Wk3, L1_gnn_Wv1, L1_gnn_Wv2, L1_gnn_Wv3, L1_gnn_W_logit, L1_gnn_W_out, L2_gnn_W1, L2_gnn_b1, L2_gnn_gamma, L2_gnn_beta, L2_gnn_W2, L2_gnn_b2, L3_gnn_W_self, L3_gnn_b_self, L3_gnn_W_neigh, L3_gnn_b_neigh, L3_gnn_W_var, L3_gnn_b_var):
    import jax
    import jax.numpy as jnp

    def _L0_gnn_ref(edge_index, edge_type, entity_emb, relation_emb, W):
        import jax, jax.numpy as jnp
        import numpy as np
        N_HOPS = 2
        NEG_SLOPE = 0.2

        def _hop(emb, head, tail, rel_e, W, N):
            a_input = jnp.concatenate([emb[head], emb[tail]], axis=-1)
            e = jnp.sum(a_input @ W * rel_e, axis=-1)
            e = jax.nn.leaky_relu(e, NEG_SLOPE)
            seg_max = jax.ops.segment_max(e, head, num_segments=N)
            ex = jnp.exp(e - seg_max[head])
            denom = jax.ops.segment_sum(ex, head, num_segments=N)
            alpha = ex / denom[head]
            agg = jax.ops.segment_sum(emb[tail] * alpha[:, None], head, num_segments=N)
            return agg + emb
        head, tail = (edge_index[0], edge_index[1])
        N = entity_emb.shape[0]
        rel_e = relation_emb[edge_type]
        res = entity_emb
        emb = entity_emb
        for _ in range(N_HOPS):
            emb = _hop(emb, head, tail, rel_e, W, N)
            norm = jnp.maximum(jnp.linalg.norm(emb, axis=-1, keepdims=True), 1e-12)
            emb = emb / norm
            res = 0.5 * res + emb
        return res

    def _L1_gnn_ref(node_feat, edge_sh, edge_inv, edge_weight_cutoff, Wk1, Wk2, Wk3, Wv1, Wv2, Wv3, W_logit, W_out, edge_src, edge_dst):
        import jax, jax.numpy as jnp
        import numpy as np
        N, K, D, S, B, H = (256, 16, 64, 8, 64, 4)
        E = N * K
        F = D * (1 + S)
        HID = 64

        def _mlp(x, W1, W2, W3):
            h = jax.nn.gelu(x @ W1)
            h = jax.nn.gelu(h @ W2)
            return h @ W3
        n_nodes = node_feat.shape[0]
        n_edges, d = (edge_src.shape[0], node_feat.shape[1])
        s = edge_sh.shape[1]
        x_src = node_feat[edge_src]

        def f(W1, W2, W3):
            tp = (x_src[:, :, None] * edge_sh[:, None, :]).reshape(n_edges, d * s)
            out1 = jnp.concatenate([x_src, tp], axis=-1)
            out2 = _mlp(edge_inv, W1, W2, W3)
            return out1 * out2
        edge_key = f(Wk1, Wk2, Wk3)
        q = node_feat[edge_dst]
        k0 = edge_key[:, :d]
        k1 = edge_key[:, d:].reshape(n_edges, d, s)
        scal = jnp.concatenate([q * k0, jnp.einsum('ed,eds,es->ed', q, k1, edge_sh)], axis=-1)
        edge_logit = scal @ W_logit
        node_logit_max = jax.ops.segment_max(edge_logit, edge_dst, num_segments=n_nodes)
        exp = edge_weight_cutoff[:, None] * jnp.exp(edge_logit - node_logit_max[edge_dst])
        z = jax.ops.segment_sum(exp, edge_dst, num_segments=n_nodes)
        z = jnp.where(z == 0.0, 1.0, z)
        alpha = exp / z[edge_dst]
        edge_v = f(Wv1, Wv2, Wv3)
        edge_v = edge_v.reshape(n_edges, H, F // H) * jnp.sqrt(jax.nn.relu(alpha))[:, :, None]
        edge_v = edge_v.reshape(n_edges, F)
        node_out = jax.ops.segment_sum(edge_v, edge_dst, num_segments=n_nodes)
        return node_out @ W_out

    def _L2_gnn_ref(x, edge_index, edge_feature, W1, b1, gamma, beta, W2, b2):
        import jax, jax.numpy as jnp
        import numpy as np
        N = 3125
        E = 50000
        D = 64
        EPS = 1e-05

        def _gcn_conv(x, W, b, src, dst, edge_weight, n):
            h = x @ W
            loop = jnp.arange(n, dtype=src.dtype)
            s = jnp.concatenate([src, loop])
            d = jnp.concatenate([dst, loop])
            w = jnp.concatenate([edge_weight, jnp.ones((n,), x.dtype)])
            deg = jax.ops.segment_sum(w, d, num_segments=n)
            dinv = jnp.where(deg > 0, jax.lax.rsqrt(deg), 0.0)
            norm = dinv[s] * w * dinv[d]
            msg = h[s] * norm[:, None]
            out = jax.ops.segment_sum(msg, d, num_segments=n)
            return out + b
        src, dst = (edge_index[0], edge_index[1])
        n = x.shape[0]
        h = _gcn_conv(x, W1, b1, src, dst, edge_feature, n)
        mu = jnp.mean(h, axis=0)
        var = jnp.var(h, axis=0)
        h = gamma * (h - mu) * jax.lax.rsqrt(var + EPS) + beta
        h = jax.nn.relu(h)
        return _gcn_conv(h, W2, b2, src, dst, edge_feature, n)

    def _L3_gnn_ref(x, edge_index, W_self, b_self, W_neigh, b_neigh, W_var, b_var):
        import jax, jax.numpy as jnp
        import numpy as np
        N_NODES = 3125
        N_EDGES = 50000
        D = 64
        N, d = x.shape
        scale = d ** (-0.5)
        src, dst = (edge_index[0], edge_index[1])
        x_src = x[src]
        x_dst = x[dst]
        logits = jnp.sum(x_src * x_dst, axis=-1) * scale
        seg_max = jax.ops.segment_max(logits, dst, num_segments=N)
        ex = jnp.exp(logits - seg_max[dst])
        denom = jax.ops.segment_sum(ex, dst, num_segments=N)
        attn = ex / denom[dst]
        msg = jax.ops.segment_sum(x_src * attn[:, None], dst, num_segments=N)
        out = x @ W_self.T + b_self + msg @ W_neigh.T + b_neigh
        cnt = jax.ops.segment_sum(jnp.ones_like(logits), dst, num_segments=N)
        cnt = jnp.maximum(cnt, 1.0)[:, None]
        msg_mean = jax.ops.segment_sum(x_src, dst, num_segments=N) / cnt
        diff_sq = (x_src - msg_mean[dst]) ** 2
        var = jax.ops.segment_sum(diff_sq, dst, num_segments=N) / cnt
        out = out + var @ W_var.T + b_var
        return out
    edge_index = jnp.stack([src, dst])
    h = jnp.maximum(_layernorm(x, axis=-1), 0.0)
    x = x + _L0_gnn_ref(edge_index, edge_type_64, h, L0_gnn_relation_emb, L0_gnn_W)
    h = jnp.maximum(_layernorm(x, axis=-1), 0.0)
    x = x + _L1_gnn_ref(h, edge_attr_8, edge_attr_64, edge_weight, L1_gnn_Wk1, L1_gnn_Wk2, L1_gnn_Wk3, L1_gnn_Wv1, L1_gnn_Wv2, L1_gnn_Wv3, L1_gnn_W_logit, L1_gnn_W_out, src, dst)
    h = jnp.maximum(_layernorm(x, axis=-1), 0.0)
    x = x + _L2_gnn_ref(h, edge_index, edge_weight, L2_gnn_W1, L2_gnn_b1, L2_gnn_gamma, L2_gnn_beta, L2_gnn_W2, L2_gnn_b2)
    h = jnp.maximum(_layernorm(x, axis=-1), 0.0)
    x = x + _L3_gnn_ref(h, edge_index, L3_gnn_W_self, L3_gnn_b_self, L3_gnn_W_neigh, L3_gnn_b_neigh, L3_gnn_W_var, L3_gnn_b_var)
    return x

_drawn_inputs = setup_inputs


def setup_inputs(seed=0):
    import zlib

    import numpy as np

    out = dict(_drawn_inputs(seed))
    spreads = {'L2_gnn_b1': (0.0, 0.8),
     'L2_gnn_gamma': (1.0, 0.2),
     'L2_gnn_beta': (0.0, 0.1),
     'L2_gnn_b2': (0.0, 0.1)}
    factors = {'L0_gnn_relation_emb': 3.162,
     'L0_gnn_W': 3.318,
     'L3_gnn_b_self': 5.984,
     'L3_gnn_b_neigh': 6.498,
     'L3_gnn_b_var': 7.048}
    for name, (base, spread) in spreads.items():
        noise = np.random.default_rng([zlib.crc32(name.encode()), seed]).standard_normal(out[name].shape)
        drawn = base * np.exp(spread * noise) if base else spread * noise
        out[name] = jnp.asarray(drawn.astype(out[name].dtype))
    for name, factor in factors.items():
        out[name] = (out[name] * factor).astype(out[name].dtype)
    return out
```

```python
import concourse.bass as bass
from concourse import mybir
from contextlib import ExitStack

F32 = mybir.dt.float32
I32 = mybir.dt.int32
ALU = mybir.AluOpType
ACT = mybir.ActivationFunctionType
AX = mybir.AxisListType
ds = bass.ds
PE, DVE, ACTIVATION, SP = (mybir.EngineType.PE, mybir.EngineType.DVE, mybir.EngineType.Activation,
                           mybir.EngineType.SP)

N, E, D = 3125, 53125, 64
P = 128
BLOCKS = -(-N // P)
NP = BLOCKS * P
TILES = -(-E // P)
STEPS = TILES + BLOCKS - 1
U = 4
GROUPS = STEPS // U
RING = 2
ITERS = GROUPS // RING
TGROUPS = TILES // U
TITERS = TGROUPS // RING
Q = 110
W = 4 * P
EPAD = E + P + 123
NONE = 16384
BIG = 1.0e30
AGG = 72
BANK = 512
EPS = 1e-5
F1 = 9 * D
assert STEPS % (U * RING) == 0 and TILES % (U * RING) == 0 and Q * 4 == STEPS


class Kernel:

    def __init__(self, sb, pb, sem, a, out, ctx):
        self.sb, self.pb, self.sem, self.a, self.out, self.ctx = sb, pb, sem, a, out, ctx


class Scratch:

    def __init__(self, s, w):
        self.s, self.w = s, w


class Chain:

    def __init__(self, eng, sem, base=0):
        self.eng, self.sem, self.base, self.n = eng, sem, base, 0

    def inc(self, ins):
        ins.then_inc(self.sem, 1)
        self.n += 1

    def link(self, ins):
        self.inc(ins)
        self.eng.wait_ge(self.sem, self.base + self.n)


def apart(eng, sem):
    eng.sem_inc(sem, 1)


def bc(ap, shape):
    return ap.broadcast_to(shape)


def four(nc, engine, row, at, max_val):
    return nc.values_load_multi_w_load_instructions(row[0:1, ds(at, 4)], engines=[engine], min_val=0,
                                                    max_val=max_val)[1]


def blocks_at(nc, engine, blk, g):
    return four(nc, engine, blk[:].rearrange("a g w u -> a (g w u)"), g * (2 * U), BLOCKS - 1)


def columns_at(nc, engine, blk, g):
    return four(nc, engine, blk[:].rearrange("a g w u -> a (g w u)"), g * (2 * U) + U, 4 * BANK - AGG)


def program(nc, a, out):
    with ExitStack() as ctx:
        def sb(name, shape, dt=F32, stack=ctx):
            return stack.enter_context(nc.sbuf_tensor(name, shape, dt))

        def pb(name, shape, stack):
            return stack.enter_context(nc.psum_tensor(name, shape, F32))

        used = []

        def sem(name):
            used.append(nc.alloc_semaphore(name))
            return used[-1]

        def renew():
            nc.all_engine_barrier()
            nc.clear_and_free_semaphores(used)
            nc.all_engine_barrier()
            used.clear()

        c = Kernel(sb=sb, pb=pb, sem=sem, a=a, out=out, ctx=ctx)
        c.s_apart = nc.alloc_semaphore("apart")
        c.iota = sb("iota", [P, P])
        c.iota_p = sb("iota_p", [P, 1])
        c.ident = sb("ident", [P, P])
        c.ones = sb("ones", [P, P])
        c.zeros = sb("zeros", [P, BANK])
        c.recS = sb("recS", [P, STEPS + U, 4], I32)
        c.locD = sb("locD", [P, STEPS + U])
        c.locS = sb("locS", [P, STEPS + U])
        c.penD = sb("penD", [Q, W + 1])
        c.penS = sb("penS", [Q, W + 1])
        c.edge0 = sb("edge0", [1, STEPS + U], I32)
        c.deg = sb("deg", [P, BLOCKS])
        c.tick = sb("tick", [P, 1])
        rows = nc.dram_tensor("rows", (NP, D), F32, kind="Internal").ap()
        c.rows_flat, c.rows = rows, rows.rearrange("(b p) d -> p b d", p=P)
        c.blkD = sb("blkD", [1, GROUPS + 1, 2, U], I32)
        c.blkS = sb("blkS", [1, GROUPS + 1, 2, U], I32)
        c.prevD = sb("prevD", [1, STEPS], I32)
        c.x = sb("x", [P, BLOCKS, D])
        c.src_dram = nc.dram_tensor("src_dram", (P, STEPS + U), I32, kind="Internal").ap()
        c.loc_dram = nc.dram_tensor("loc_dram", ((STEPS + U) * P,), F32, kind="Internal").ap()
        c.val_dram = nc.dram_tensor("val_dram", (P, STEPS * 9), F32, kind="Internal").ap()
        c.recS_dram = nc.dram_tensor("recS_dram", (P * STEPS, 4), I32, kind="Internal").ap()
        c.table = nc.dram_tensor("table", (NP, 2 * D), F32, kind="Internal").ap()
        prepare(nc, c)
        renew()
        for layer in (layer0, layer1, layer2, layer3):
            layer(nc, c)
            renew()
        finish(nc, c)


def layernorm_relu(v, V, act_root, x, h, t):
    full = [P, BLOCKS, D]
    v.link(V.tensor_reduce(t.s[:], x[:], AX.X, ALU.add))
    v.link(V.tensor_scalar(t.s[:], t.s[:], 1.0 / D, None, ALU.mult))
    v.link(V.tensor_tensor(h[:], x[:], bc(t.s[:].unsqueeze(2), full), ALU.subtract))
    v.link(V.tensor_tensor(t.w[:], h[:], h[:], ALU.mult))
    v.link(V.tensor_reduce(t.s[:], t.w[:], AX.X, ALU.add))
    act_root(V.tensor_scalar(t.s[:], t.s[:], 1.0 / D, EPS, ALU.mult, ALU.add))
    v.link(V.reciprocal(t.s[:], t.s[:]))
    v.link(V.tensor_tensor(h[:], h[:], bc(t.s[:].unsqueeze(2), full), ALU.mult))
    v.link(V.tensor_scalar(h[:], h[:], 0.0, None, ALU.max))


def blocks_of(ps, width):
    for j in range(4):
        n = min(7, BLOCKS - 7 * j)
        yield (slice(7 * j, 7 * j + n),
               ps[:, j * BANK:j * BANK + n * AGG].rearrange("p (b f) -> p b f", f=AGG)[:, :, 0:width])


def segment_exp(nc, c, name, L, pen, heads):
    st = ExitStack()
    sb, pb, sem = c.sb, c.pb, c.sem
    with st:
        X = sb(name + "X", [Q, W], F32, st)
        F = sb(name + "F", [Q, W], F32, st)
        B = sb(name + "B", [Q, W], F32, st)
        runs = sb(name + "runs", [Q, 2], F32, st)
        rrow = sb(name + "rrow", [1, 2, Q], F32, st)
        erow = sb(name + "erow", [1, 2, Q], F32, st)
        carry = sb(name + "carry", [1, 2, Q + 2], F32, st)
        ccol = sb(name + "ccol", [Q, 2], F32, st)
        ps_x = pb(name + "ps_x", [Q, W], st)
        ps_r = pb(name + "ps_r", [1, 2, Q], st)
        ps_e = pb(name + "ps_e", [1, 2, Q], st)
        ps_c = pb(name + "ps_c", [Q, 2], st)
        ps_b = pb(name + "ps_b", [P, 4, Q], st)
        s_v = sem(name + "v"); s_run = sem(name + "run"); s_rr = sem(name + "rr")
        s_x = sem(name + "x"); s_e = sem(name + "e"); s_er = sem(name + "er"); s_cr = sem(name + "cr")
        s_cc = sem(name + "cc"); s_m = sem(name + "m"); s_ex = sem(name + "ex"); s_b = sem(name + "b")
        s_done = sem(name + "done")
        block = st.enter_context(nc.Block(name))

        @block.vector
        def _(dve):
            V = nc.vector
            v = Chain(dve, s_v)
            v.link(V.tensor_reduce(runs[:, 0:1], pen[:, 0:W], AX.X, ALU.min))
            v.link(V.tensor_reduce(runs[:, 1:2], pen[:, 1:W + 1], AX.X, ALU.min))
            v.link(V.memset(carry[:], -BIG))
            V.tensor_copy(ccol[:], runs[:]).then_inc(s_run, 1)
            dve.wait_ge(s_rr, 1)
            v.link(V.tensor_copy(rrow[:], ps_r[:]))
            for n in range(heads):
                dve.wait_ge(s_x, n + 1)
                v.link(V.tensor_copy(X[:], ps_x[:]))
                v.link(V.tensor_tensor_scan(F[:], pen[:, 0:W], X[:], -BIG, ALU.add, ALU.max))
                v.link(V.tensor_tensor_scan(B[:, ::-1], pen[:, 1:W + 1][:, ::-1], X[:, ::-1], -BIG, ALU.add, ALU.max))
                dve.sem_inc(s_e, 1)
                dve.wait_ge(s_er, n + 1)
                v.link(V.tensor_copy(erow[:], ps_e[:]))
                v.link(V.tensor_tensor_scan(carry[:, 0, 1:Q + 1], rrow[:, 0, :], erow[:, 0, :], -BIG, ALU.add, ALU.max))
                v.link(V.tensor_tensor_scan(carry[:, 1, 1:Q + 1][:, ::-1], rrow[:, 1, :][:, ::-1],
                                            erow[:, 1, :][:, ::-1], -BIG, ALU.add, ALU.max))
                dve.sem_inc(s_cr, 1)
                dve.wait_ge(s_cc, n + 1)
                v.link(V.tensor_copy(ccol[:], ps_c[:]))
                v.link(V.tensor_tensor_scan(F[:], pen[:, 0:W], X[:], ccol[:, 0:1], ALU.add, ALU.max))
                v.link(V.tensor_tensor_scan(B[:, ::-1], pen[:, 1:W + 1][:, ::-1], X[:, ::-1], ccol[:, 1:2],
                                            ALU.add, ALU.max))
                v.link(V.tensor_tensor(F[:], F[:], B[:], ALU.max))
                V.tensor_tensor(X[:], X[:], F[:], ALU.subtract).then_inc(s_m, 1)
                dve.wait_ge(s_b, n + 1)
                V.tensor_copy(L[:, 0:STEPS, n].rearrange("p (q j) -> p j q", j=4), ps_b[:]).then_inc(s_done, 1)
                dve.wait_ge(s_done, n + 1)

        @block.scalar
        def _(act):
            for n in range(heads):
                act.wait_ge(s_m, n + 1)
                nc.scalar.activation(X[:], X[:], ACT.Exp).then_inc(s_ex, 1)

        @block.tensor
        def _(pe):
            T = nc.tensor
            pe.wait_ge(s_run, 1)
            for o in range(2):
                last = T.transpose(ps_r[:, o, :], runs[:, o:o + 1], c.ident[0:Q, 0:Q])
            last.then_inc(s_rr, 1)
            for n in range(heads):
                for j in range(4):
                    last = T.transpose(ps_x[:, j * P:(j + 1) * P], L[:, j:STEPS:4, n], c.ident[:])
                last.then_inc(s_x, 1)
                pe.wait_ge(s_e, n + 1)
                T.transpose(ps_e[:, 0, :], F[:, W - 1:W], c.ident[0:Q, 0:Q])
                T.transpose(ps_e[:, 1, :], B[:, 0:1], c.ident[0:Q, 0:Q]).then_inc(s_er, 1)
                pe.wait_ge(s_cr, n + 1)
                T.transpose(ps_c[:, 0:1], carry[:, 0, 0:Q], c.ident[0:1, 0:1])
                T.transpose(ps_c[:, 1:2], carry[:, 1, 2:Q + 2], c.ident[0:1, 0:1]).then_inc(s_cc, 1)
                pe.wait_ge(s_ex, n + 1)
                for j in range(4):
                    last = T.transpose(ps_b[:, j, :], X[:, j * P:(j + 1) * P], c.ident[0:Q, 0:Q])
                last.then_inc(s_b, 1)


def weighted_sums(nc, c, name, order, G, EX, ps, squares=False):
    st = ExitStack()
    sb, sem = c.sb, c.sem
    loc, blk = (c.locD, c.blkD) if order == "dst" else (c.locS, c.blkS)
    with st:
        H = [sb(f"{name}H{h}", [P, U, P], F32, st) for h in range(RING)]
        Y = [sb(f"{name}Y{h}", [P, U, D + 1], F32, st) for h in range(RING)]
        Y2 = [sb(f"{name}Y2{h}", [P, U, D], F32, st) for h in range(RING)] if squares else None
        s_y = sem(name + "y"); s_used = sem(name + "used")
        each = 3 + squares
        block = st.enter_context(nc.Block(name))

        @block.vector
        def _(dve):
            V = nc.vector
            with dve.Fori(0, ITERS) as i:
                for h in range(RING):
                    at = (i * RING + h) * U
                    dve.wait_ge(s_used, i * RING + h + 1)
                    V.tensor_tensor(H[h][:], bc(c.iota[:, None, :], [P, U, P]),
                                    bc(loc[:, ds(at, U)].unsqueeze(2), [P, U, P]), ALU.is_equal).then_inc(s_y, 1)
                    V.tensor_tensor(Y[h][:, :, 0:D], G[:, ds(at, U), :], bc(EX[:, ds(at, U), :], [P, U, D]),
                                    ALU.mult).then_inc(s_y, 1)
                    V.tensor_scalar(Y[h][:, :, D:D + 1], EX[:, ds(at, U), :], 1.0, None, ALU.mult).then_inc(s_y, 1)
                    if squares:
                        V.tensor_tensor(Y2[h][:], G[:, ds(at, U), :], G[:, ds(at, U), :], ALU.mult).then_inc(s_y, 1)

        @block.tensor
        def _(pe):
            T = nc.tensor
            for j in range(8 if squares else 4):
                T.matmul(ps[:, j * BANK:(j + 1) * BANK], c.zeros[:, 0:P], c.zeros[:], start=True, stop=True)
            pe.sem_inc(s_used, RING)
            with pe.Fori(0, ITERS) as i:
                for h in range(RING):
                    g = i * RING + h
                    cols = columns_at(nc, PE, blk, g)
                    pe.wait_ge(s_y, (g + 1) * each)
                    for k in range(U):
                        if squares:
                            T.matmul(ps[:, ds(cols[k] + 4 * BANK, D)], H[h][:, k, :], Y2[h][:, k, :], start=False,
                                     stop=True, skip_group_check=True)
                        last = T.matmul(ps[:, ds(cols[k], D + 1)], H[h][:, k, :], Y[h][:, k, :], start=False, stop=True,
                                        skip_group_check=True)
                    last.then_inc(s_used, 1)


def layer0(nc, c):
    sb, pb, sem, a = c.sb, c.pb, c.sem, c.a
    st = ExitStack()
    full = [P, BLOCKS, D]
    with st:
        G = sb("l0G", [P, STEPS, D], F32, st)
        L = sb("l0L", [P, STEPS, 1], F32, st)
        emb = sb("l0emb", full, F32, st)
        res = sb("l0res", full, F32, st)
        T1 = sb("l0T1", full, F32, st)
        RW = sb("l0RW", [D, 2 * D], F32, st)
        typ = sb("l0typ", [P, STEPS], F32, st)
        t = Scratch(s=sb("l0s", [P, BLOCKS], F32, st), w=sb("l0w", full, F32, st))
        WT = sb("l0WT", [D, 2 * D], F32, st)
        relT = sb("l0relT", [D, D], F32, st)

        s_w = sem("l0_weights"); s_v = sem("l0_v"); s_q = sem("l0_var"); s_r = sem("l0_root"); s_rw = sem("l0_rw")
        with nc.psum_tensor("l0ps_rw", [D, 2 * D], F32) as ps_rw, nc.Block("l0_start") as block:
            @block.sync
            def _(sp):
                sp.dma_start(WT[:], a["l0_WT"]).then_inc(s_w, 16)
                sp.dma_start(relT[:], a["l0_relT"]).then_inc(s_w, 16)

            @block.vector
            def _(dve):
                V = nc.vector
                v = Chain(dve, s_v)

                def root(ins):
                    ins.then_inc(s_q, 1)
                    dve.wait_ge(s_r, 1)
                v.link(V.tensor_copy(typ[:], c.recS[:, 0:STEPS, 2]))
                layernorm_relu(v, V, root, c.x, emb, t)
                v.link(V.tensor_copy(res[:], emb[:]))
                dve.wait_ge(s_rw, 1)
                v.link(V.tensor_copy(RW[:], ps_rw[:]))

            @block.scalar
            def _(act):
                act.wait_ge(s_q, 1)
                nc.scalar.activation(t.s[:], t.s[:], ACT.Sqrt).then_inc(s_r, 1)

            @block.tensor
            def _(pe):
                pe.wait_ge(s_w, 32)
                nc.tensor.matmul(ps_rw[:, 0:D], WT[:, 0:D], relT[:], start=True, stop=True)
                nc.tensor.matmul(ps_rw[:, D:2 * D], WT[:, D:2 * D], relT[:], start=True, stop=True).then_inc(s_rw, 1)

        for hop in range(2):
            layer0_tables(nc, c, f"l0t{hop}", emb, T1, RW)
            layer0_logits(nc, c, f"l0a{hop}", G, L, T1, typ)
            segment_exp(nc, c, f"l0e{hop}", L, c.penS, 1)
            with nc.psum_tensor(f"l0ps{hop}", [P, 4 * BANK], F32) as ps:
                weighted_sums(nc, c, f"l0s{hop}", "src", G, L, ps)
                s_v = sem(f"l0u{hop}"); s_q = sem(f"l0q{hop}"); s_r = sem(f"l0r{hop}")
                with nc.sbuf_tensor(f"l0agg{hop}", [P, BLOCKS, D + 1], F32) as agg, nc.Block(f"l0_update{hop}") as block:
                    @block.vector
                    def _(dve):
                        V = nc.vector
                        v = Chain(dve, s_v)
                        for b, view in blocks_of(ps, D + 1):
                            v.link(V.tensor_copy(agg[:, b, :], view))
                        den = agg[:, :, D:D + 1]
                        v.link(V.tensor_scalar(t.s[:].unsqueeze(2), den, 0.0, None, ALU.is_equal))
                        v.link(V.tensor_tensor(t.s[:].unsqueeze(2), den, t.s[:].unsqueeze(2), ALU.add))
                        v.link(V.reciprocal(t.s[:], t.s[:]))
                        v.link(V.tensor_tensor(agg[:, :, 0:D], agg[:, :, 0:D], bc(t.s[:].unsqueeze(2), full), ALU.mult))
                        v.link(V.tensor_tensor(emb[:], emb[:], agg[:, :, 0:D], ALU.add))
                        v.link(V.tensor_tensor(t.w[:], emb[:], emb[:], ALU.mult))
                        v.link(V.tensor_reduce(t.s[:], t.w[:], AX.X, ALU.add))
                        V.tensor_scalar(t.s[:], t.s[:], 1e-30, None, ALU.max).then_inc(s_q, 1)
                        dve.wait_ge(s_r, 1)
                        v.link(V.tensor_scalar(t.s[:], t.s[:], 1e-12, None, ALU.max))
                        v.link(V.reciprocal(t.s[:], t.s[:]))
                        v.link(V.tensor_tensor(emb[:], emb[:], bc(t.s[:].unsqueeze(2), full), ALU.mult))
                        v.link(V.scalar_tensor_tensor(res[:], res[:], 0.5, emb[:], ALU.mult, ALU.add))
                        if hop == 1:
                            v.link(V.tensor_tensor(c.x[:], c.x[:], res[:], ALU.add))

                    @block.scalar
                    def _(act):
                        act.wait_ge(s_q, 1)
                        nc.scalar.activation(t.s[:], t.s[:], ACT.Sqrt).then_inc(s_r, 1)


def layer0_tables(nc, c, name, emb, T1, RW):
    sb, pb, sem = c.sb, c.pb, c.sem
    with ExitStack() as st:
        rows = sb(name + "rows", [P, BLOCKS, 2 * D], F32, st)
        eT = [sb(f"{name}eT{j}", [D, W], F32, st) for j in range(2)]
        ps_t = [pb(f"{name}ps_t{j}", [D, W], st) for j in range(2)]
        ps_m = [pb(f"{name}ps_m{j}", [P, W], st) for j in range(2)]
        s_t = sem(name + "t"); s_c = sem(name + "c"); s_m = sem(name + "m"); s_v = sem(name + "v"); s_o = sem(name + "o")
        groups = [(b, min(4, BLOCKS - b)) for b in range(0, BLOCKS, 4)]
        block = st.enter_context(nc.Block(name))

        @block.tensor
        def _(pe):
            for j, (b, n) in enumerate(groups):
                if j >= 2:
                    pe.wait_ge(s_c, j - 1)
                for k in range(n):
                    last = nc.tensor.transpose(ps_t[j % 2][:, k * P:(k + 1) * P], emb[:, b + k, :], c.ident[:])
                last.then_inc(s_t, 1)
                pe.wait_ge(s_c, j + 1)
                if j >= 2:
                    pe.wait_ge(s_v, 1 + 2 * (j - 1))
                for k in range(n):
                    last = nc.tensor.matmul(ps_m[j % 2][:, k * P:(k + 1) * P], eT[j % 2][:, k * P:(k + 1) * P], RW[:],
                                            start=True, stop=True)
                last.then_inc(s_m, 1)

        @block.scalar
        def _(act):
            for j, (b, n) in enumerate(groups):
                act.wait_ge(s_t, j + 1)
                if j >= 2:
                    act.wait_ge(s_m, j - 1)
                nc.scalar.copy(eT[j % 2][:, 0:n * P], ps_t[j % 2][:, 0:n * P]).then_inc(s_c, 1)

        @block.vector
        def _(dve):
            V = nc.vector
            v = Chain(dve, s_v)
            v.link(V.tensor_copy(rows[:, :, 0:D], emb[:]))
            for j, (b, n) in enumerate(groups):
                dve.wait_ge(s_m, j + 1)
                m = ps_m[j % 2][:, 0:n * P].rearrange("p (b f) -> p b f", f=P)
                v.link(V.tensor_copy(T1[:, b:b + n, :], m[:, :, 0:D]))
                v.link(V.tensor_copy(rows[:, b:b + n, D:], m[:, :, D:]))

        @block.sync
        def _(sp):
            sp.wait_ge(s_v, 1 + 2 * len(groups))
            sp.dma_start(c.table.rearrange("(b p) f -> p b f", p=P), rows[:]).then_inc(s_o, 16)
            sp.wait_ge(s_o, 16)


def layer0_logits(nc, c, name, G, L, T1, typ):
    sb, pb, sem = c.sb, c.pb, c.sem
    with ExitStack() as st:
        R = [sb(f"{name}R{h}", [P, U, 2 * D], F32, st) for h in range(RING)]
        H = [sb(f"{name}H{h}", [P, U, P], F32, st) for h in range(RING)]
        HT = [sb(f"{name}HT{h}", [P, W], F32, st) for h in range(RING)]
        idx = [sb(f"{name}idx{h}", [P, U], I32, st) for h in range(RING)]
        S = sb(name + "S", [P, U, D], F32, st)
        one = sb(name + "one", [P, U, D], F32, st)
        e = sb(name + "e", [P, U], F32, st)
        ps_h = [pb(f"{name}ps_h{h}", [P, W], st) for h in range(RING)]
        ps_s = [pb(f"{name}ps_s{h}", [P, BANK], st)[:, 0:U * D].rearrange("p (u d) -> p u d", u=U) for h in range(RING)]
        s_idx = sem(name + "idx"); s_g = [sem(f"{name}g{h}") for h in range(RING)]
        s_h = sem(name + "h"); s_t = sem(name + "t"); s_tc = sem(name + "tc"); s_s = sem(name + "s")
        s_used = sem(name + "used"); s_keep = sem(name + "keep"); s_v = sem(name + "v")
        block = st.enter_context(nc.Block(name))

        @block.gpsimd
        def _(pool):
            with pool.Fori(0, ITERS) as i:
                for h in range(RING):
                    pool.wait_ge(s_idx, i * RING + h + 1)
                    apart(pool, c.s_apart)
                    for k in range(U):
                        nc.gpsimd.indirect_dma_start(
                            out=R[h][:, k, :], out_offset=None, in_=c.table,
                            in_offset=bass.IndirectOffsetOnAxis(ap=idx[h][:, k:k + 1], axis=0)).then_inc(s_g[h], 16)

        @block.scalar
        def _(act):
            A = nc.scalar

            def indices(g, h):
                act.wait_ge(s_used, g + 1)
                act.wait_ge(s_keep, g + 1)
                apart(act, c.s_apart)
                A.copy(idx[h][:], c.recS[:, ds(g * U, U), 1]).then_inc(s_idx, 1)

            act.sem_inc(s_keep, RING)
            indices(0, 0)
            with act.Fori(0, ITERS) as i:
                for h in range(RING):
                    g = i * RING + h
                    indices(g + 1, (h + 1) % RING)
                    act.wait_ge(s_t, g + 1)
                    A.copy(HT[h][:], ps_h[h][:]).then_inc(s_tc, 1)
                    act.wait_ge(s_g[h], (i + 1) * (16 * U))
                    apart(act, c.s_apart)
                    A.copy(G[:, ds(g * U, U), :], R[h][:, :, 0:D]).then_inc(s_keep, 1)

        @block.vector
        def _(dve):
            V = nc.vector

            def onehot(g, h):
                V.tensor_tensor(H[h][:], bc(c.iota[:, None, :], [P, U, P]),
                                bc(c.locS[:, ds(g * U, U)].unsqueeze(2), [P, U, P]), ALU.is_equal).then_inc(s_h, 1)

            dve.sem_inc(s_used, RING)
            onehot(0, 0)
            with dve.Fori(0, ITERS) as i:
                for h in range(RING):
                    g = i * RING + h
                    onehot(g + 1, (h + 1) % RING)
                    v = Chain(dve, s_v, g * 4)
                    v.link(V.tensor_tensor(one[:], bc(c.iota[:, None, 0:D], [P, U, D]),
                                           bc(typ[:, ds(g * U, U)].unsqueeze(2), [P, U, D]), ALU.is_equal))
                    dve.wait_ge(s_s, g + 1)
                    dve.wait_ge(s_g[h], (i + 1) * (16 * U))
                    V.tensor_tensor(S[:], ps_s[h], R[h][:, :, D:], ALU.add).then_inc(s_used, 1)
                    dve.wait_ge(s_used, g + RING + 1)
                    v.link(V.tensor_tensor(S[:], S[:], one[:], ALU.mult))
                    v.link(V.tensor_reduce(e[:], S[:], AX.X, ALU.add))
                    v.link(V.scalar_tensor_tensor(L[:, ds(g * U, U), 0], e[:], 0.2, e[:], ALU.mult, ALU.max))

        @block.tensor
        def _(pe):
            T = nc.tensor
            with pe.Fori(0, ITERS) as i:
                for h in range(RING):
                    g = i * RING + h
                    pe.wait_ge(s_h, g + 1)
                    for k in range(U):
                        last = T.transpose(ps_h[h][:, k * P:(k + 1) * P], H[h][:, k, :], c.ident[:])
                    last.then_inc(s_t, 1)
                    blk = blocks_at(nc, PE, c.blkS, g)
                    pe.wait_ge(s_tc, g + 1)
                    pe.wait_ge(s_used, g + 1)
                    for k in range(U):
                        last = T.matmul(ps_s[h][:, k, :], HT[h][:, k * P:(k + 1) * P], T1[:, ds(blk[k], 1), :]
                                        .rearrange("p a d -> p (a d)"), start=True, stop=True)
                    last.then_inc(s_s, 1)


def node_linear(nc, c, name, terms, dest, bias, add):
    sb, pb, sem = c.sb, c.pb, c.sem
    n_t = len(terms)
    with ExitStack() as st:
        eT = [sb(f"{name}eT{j}", [D, n_t, W], F32, st) for j in range(2)]
        ps_t = [pb(f"{name}ps_t{j}", [D, W], st) for j in range(2)]
        ps_m = [pb(f"{name}ps_m{j}", [P, BANK], st) for j in range(2)]
        s_t = sem(name + "t"); s_c = sem(name + "c"); s_m = sem(name + "m"); s_v = sem(name + "v")
        groups = [(b, min(4, BLOCKS - b)) for b in range(0, BLOCKS, 4)]
        block = st.enter_context(nc.Block(name))

        @block.tensor
        def _(pe):
            q = 0
            for j, (b, n) in enumerate(groups):
                for X, _ in terms:
                    if q >= 2:
                        pe.wait_ge(s_c, q - 1)
                    for k in range(n):
                        last = nc.tensor.transpose(ps_t[q % 2][:, k * P:(k + 1) * P], X[:, b + k, 0:D], c.ident[:])
                    last.then_inc(s_t, 1)
                    q += 1
                pe.wait_ge(s_c, n_t * (j + 1))
                if j >= 2:
                    pe.wait_ge(s_v, 2 * (j - 1))
                for k in range(n):
                    for i, (_, w) in enumerate(terms):
                        last = nc.tensor.matmul(ps_m[j % 2][:, k * D:(k + 1) * D], eT[j % 2][:, i, k * P:(k + 1) * P],
                                                w[:], start=(i == 0), stop=(i == n_t - 1))
                last.then_inc(s_m, 1)

        @block.scalar
        def _(act):
            q = 0
            for j, (b, n) in enumerate(groups):
                if j >= 2:
                    act.wait_ge(s_m, j - 1)
                for i in range(n_t):
                    act.wait_ge(s_t, q + 1)
                    nc.scalar.copy(eT[j % 2][:, i, 0:n * P], ps_t[q % 2][:, 0:n * P]).then_inc(s_c, 1)
                    q += 1

        @block.vector
        def _(dve):
            V = nc.vector
            v = Chain(dve, s_v)
            for j, (b, n) in enumerate(groups):
                dve.wait_ge(s_m, j + 1)
                m = ps_m[j % 2][:, 0:n * D].rearrange("p (b f) -> p b f", f=D)
                part = dest[:, b:b + n, :]
                if add:
                    v.link(V.tensor_tensor(part, part, m, ALU.add))
                    v.link(V.tensor_tensor(part, part, bc(bias[:, None, :], [P, n, D]), ALU.add))
                else:
                    v.link(V.tensor_tensor(part, m, bc(bias[:, None, :], [P, n, D]), ALU.add))
                    v.link(V.tensor_copy(c.tick[:], c.ones[:, 0:1]))


def norm_and_table(nc, c, name, h, t, scale=None, width=D):
    sem = c.sem
    s_v = sem(name + "v"); s_q = sem(name + "q"); s_r = sem(name + "r"); s_h = sem(name + "h"); s_o = sem(name + "o")
    with nc.Block(name) as block:
        @block.vector
        def _(dve):
            V = nc.vector
            v = Chain(dve, s_v)

            def root(ins):
                ins.then_inc(s_q, 1)
                dve.wait_ge(s_r, 1)
            layernorm_relu(v, V, root, c.x, h, t)
            if scale is not None:
                v.link(V.tensor_tensor(h[:], h[:], bc(scale[:].unsqueeze(2), [P, BLOCKS, D]), ALU.mult))
            V.tensor_copy(c.tick[:], c.ones[:, 0:1]).then_inc(s_h, 1)

        @block.scalar
        def _(act):
            act.wait_ge(s_q, 1)
            nc.scalar.activation(t.s[:], t.s[:], ACT.Sqrt).then_inc(s_r, 1)

        @block.sync
        def _(sp):
            sp.wait_ge(s_h, 1)
            sp.dma_start(c.rows, h[:]).then_inc(s_o, 16)
            sp.wait_ge(s_o, 16)


def layer2(nc, c):
    sb, sem, a = c.sb, c.sem, c.a
    full = [P, BLOCKS, D]
    st = ExitStack()
    with st:
        src = sb("l2src", [P, STEPS + U], I32, st)
        val = sb("l2val", [P, STEPS, 9], F32, st)
        h = sb("l2h", full, F32, st)
        y = sb("l2y", full, F32, st)
        dinv = sb("l2dinv", [P, BLOCKS], F32, st)
        t = Scratch(s=sb("l2s", [P, BLOCKS], F32, st), w=sb("l2w", full, F32, st))
        real = sb("l2real", [P, 1], F32, st)
        Wt = [sb(f"l2W{i}", [D, D], F32, st) for i in range(2)]
        row = sb("l2row", [P, 4, D], F32, st)
        sums = sb("l2sums", [P, D], F32, st)
        mean = sb("l2mean", [P, D], F32, st)
        s_in = sem("l2_in"); s_v = sem("l2_v"); s_q = sem("l2_q"); s_r = sem("l2_r")
        with nc.Block("l2_start") as block:
            @block.sync
            def _(sp):
                sp.dma_start(src[:], c.src_dram).then_inc(s_in, 16)
                sp.dma_start(val[:].rearrange("p s f -> p (s f)"), c.val_dram).then_inc(s_in, 16)
                for i in range(2):
                    sp.dma_start(Wt[i][:], a[f"l2_W{i + 1}"]).then_inc(s_in, 16)
                for i, k in enumerate(("l2_b1", "l2_gamma", "l2_beta", "l2_b2")):
                    sp.dma_start(row[:, i, :], a[k].partition_broadcast(P)).then_inc(s_in, 16)
                sp.wait_ge(s_in, 16 * 8)

            @block.vector
            def _(dve):
                V = nc.vector
                v = Chain(dve, s_v)
                v.link(V.tensor_scalar(t.s[:], c.deg[:], 1.0, None, ALU.add))
                v.link(V.tensor_scalar(dinv[:], t.s[:], 0.0, None, ALU.is_gt))
                V.tensor_scalar(t.s[:], t.s[:], 1e-30, None, ALU.max).then_inc(s_q, 1)
                dve.wait_ge(s_r, 1)
                v.link(V.reciprocal(t.s[:], t.s[:]))
                v.link(V.tensor_tensor(dinv[:], dinv[:], t.s[:], ALU.mult))
                v.link(V.tensor_scalar(real[:], c.iota_p[:], float(N - (BLOCKS - 1) * P), None, ALU.is_lt))

            @block.scalar
            def _(act):
                act.wait_ge(s_q, 1)
                nc.scalar.activation(t.s[:], t.s[:], ACT.Sqrt).then_inc(s_r, 1)

        norm_and_table(nc, c, "l2n", h, t, scale=dinv)
        for conv in range(2):
            n = f"l2c{conv}"
            with nc.psum_tensor(n + "ps", [P, 4 * BANK], F32) as ps:
                gathered_sums(nc, c, n, src, val, ps)
                s_v = sem(n + "v")
                with nc.Block(n + "_node") as block:
                    @block.vector
                    def _(dve):
                        V = nc.vector
                        v = Chain(dve, s_v)
                        for b, view in blocks_of(ps, D):
                            v.link(V.tensor_tensor(y[:, b, :], view, h[:, b, :], ALU.add))
                        v.link(V.tensor_tensor(y[:], y[:], bc(dinv[:].unsqueeze(2), full), ALU.mult))
            if conv == 1:
                node_linear(nc, c, n + "w", [(y, Wt[1])], c.x, row[:, 3, :], True)
                break
            node_linear(nc, c, n + "w", [(y, Wt[0])], h, row[:, 0, :], False)
            s_v = sem("l2b_v"); s_s = sem("l2b_s"); s_m = sem("l2b_m"); s_q = sem("l2b_q"); s_r = sem("l2b_r")
            s_h = sem("l2b_h"); s_o = sem("l2b_o")
            with nc.psum_tensor("l2b_ps", [P, 2, D], F32) as ps, nc.Block("l2_batch_norm") as block:
                @block.vector
                def _(dve):
                    V = nc.vector
                    v = Chain(dve, s_v)
                    edge = h[:, BLOCKS - 1, :]
                    v.link(V.tensor_scalar(edge, edge, real[:, 0:1], None, ALU.mult))
                    V.tensor_reduce(sums[:], h[:].rearrange("p b d -> p d b"), AX.X, ALU.add).then_inc(s_s, 1)
                    dve.wait_ge(s_m, 1)
                    v.link(V.tensor_scalar(mean[:], ps[:, 0, :], 1.0 / N, None, ALU.mult))
                    v.link(V.tensor_tensor(h[:], h[:], bc(mean[:, None, :], full), ALU.subtract))
                    v.link(V.tensor_scalar(edge, edge, real[:, 0:1], None, ALU.mult))
                    v.link(V.tensor_tensor(t.w[:], h[:], h[:], ALU.mult))
                    V.tensor_reduce(sums[:], t.w[:].rearrange("p b d -> p d b"), AX.X, ALU.add).then_inc(s_s, 1)
                    dve.wait_ge(s_m, 2)
                    V.tensor_scalar(mean[:], ps[:, 1, :], 1.0 / N, EPS, ALU.mult, ALU.add).then_inc(s_q, 1)
                    dve.wait_ge(s_r, 1)
                    v.link(V.reciprocal(mean[:], mean[:]))
                    v.link(V.tensor_tensor(mean[:], mean[:], row[:, 1, :], ALU.mult))
                    v.link(V.tensor_tensor(h[:], h[:], bc(mean[:, None, :], full), ALU.mult))
                    v.link(V.tensor_tensor(h[:], h[:], bc(row[:, 2:3, :], full), ALU.add))
                    v.link(V.tensor_scalar(h[:], h[:], 0.0, None, ALU.max))
                    V.tensor_tensor(h[:], h[:], bc(dinv[:].unsqueeze(2), full), ALU.mult).then_inc(s_h, 1)

                @block.scalar
                def _(act):
                    act.wait_ge(s_q, 1)
                    nc.scalar.activation(mean[:], mean[:], ACT.Sqrt).then_inc(s_r, 1)

                @block.tensor
                def _(pe):
                    for j in range(2):
                        pe.wait_ge(s_s, j + 1)
                        nc.tensor.matmul(ps[:, j, :], c.ones[:], sums[:], start=True, stop=True).then_inc(s_m, 1)

                @block.sync
                def _(sp):
                    sp.wait_ge(s_h, 1)
                    sp.dma_start(c.rows, h[:]).then_inc(s_o, 16)
                    sp.wait_ge(s_o, 16)


def gathered_sums(nc, c, name, src, val, ps):
    sb, sem = c.sb, c.sem
    with ExitStack() as st:
        R = [sb(f"{name}R{h}", [P, U, D], F32, st) for h in range(RING)]
        H = [sb(f"{name}H{h}", [P, U, P], F32, st) for h in range(RING)]
        Y = [sb(f"{name}Y{h}", [P, U, D], F32, st) for h in range(RING)]
        idx = [sb(f"{name}idx{h}", [P, U], I32, st) for h in range(RING)]
        s_idx = sem(name + "idx"); s_g = [sem(f"{name}g{h}") for h in range(RING)]
        s_y = sem(name + "y"); s_taken = sem(name + "taken"); s_used = sem(name + "used")
        block = st.enter_context(nc.Block(name))

        @block.gpsimd
        def _(pool):
            gather(nc, c, pool, c.rows_flat, R, idx, s_idx, s_g)

        @block.scalar
        def _(act):
            with act.Fori(0, ITERS) as i:
                for h in range(RING):
                    g = i * RING + h
                    act.wait_ge(s_taken, g + 1)
                    apart(act, c.s_apart)
                    nc.scalar.copy(idx[h][:], src[:, ds(g * U, U)]).then_inc(s_idx, 1)

        @block.vector
        def _(dve):
            V = nc.vector
            dve.sem_inc(s_taken, RING)
            with dve.Fori(0, ITERS) as i:
                for h in range(RING):
                    g = i * RING + h
                    dve.wait_ge(s_used, g + 1)
                    V.tensor_tensor(H[h][:], bc(c.iota[:, None, :], [P, U, P]),
                                    bc(c.locD[:, ds(g * U, U)].unsqueeze(2), [P, U, P]), ALU.is_equal).then_inc(s_y, 1)
                    dve.wait_ge(s_g[h], (i + 1) * (16 * U))
                    V.tensor_tensor(Y[h][:], R[h][:], bc(val[:, ds(g * U, U), 0:1], [P, U, D]),
                                    ALU.mult).then_inc(s_taken, 1)

        @block.tensor
        def _(pe):
            T = nc.tensor
            for j in range(4):
                T.matmul(ps[:, j * BANK:(j + 1) * BANK], c.zeros[:, 0:P], c.zeros[:], start=True, stop=True)
            pe.sem_inc(s_used, RING)
            with pe.Fori(0, ITERS) as i:
                for h in range(RING):
                    g = i * RING + h
                    cols = columns_at(nc, PE, c.blkD, g)
                    pe.wait_ge(s_y, g + 1)
                    pe.wait_ge(s_taken, g + RING + 1)
                    for k in range(U):
                        last = T.matmul(ps[:, ds(cols[k], D)], H[h][:, k, :], Y[h][:, k, :], start=False, stop=True,
                                        skip_group_check=True)
                    last.then_inc(s_used, 1)


def gather(nc, c, pool, table, R, idx, s_idx, s_g):
    with pool.Fori(0, ITERS) as i:
        for h in range(RING):
            pool.wait_ge(s_idx, i * RING + h + 1)
            apart(pool, c.s_apart)
            for k in range(U):
                nc.gpsimd.indirect_dma_start(
                    out=R[h][:, k, 0:D], out_offset=None, in_=table,
                    in_offset=bass.IndirectOffsetOnAxis(ap=idx[h][:, k:k + 1], axis=0)).then_inc(s_g[h], 16)


def layer3(nc, c):
    sb, sem, a = c.sb, c.sem, c.a
    full = [P, BLOCKS, D]
    st = ExitStack()
    with st:
        src = sb("l3src", [P, STEPS + U], I32, st)
        h = sb("l3h", full, F32, st)
        G = sb("l3G", [P, STEPS, D], F32, st)
        L = sb("l3L", [P, STEPS, 1], F32, st)
        Wt = [sb(f"l3W{i}", [D, D], F32, st) for i in range(3)]
        row = sb("l3row", [P, 3, D], F32, st)
        t = Scratch(s=sb("l3s", [P, BLOCKS], F32, st), w=sb("l3w", full, F32, st))
        mean = sb("l3mean", [P, BLOCKS, D + 1], F32, st)
        agg = sb("l3agg", [P, BLOCKS, D + 1], F32, st)
        s_in = sem("l3_in"); s_v = sem("l3_v")
        with nc.Block("l3_start") as block:
            @block.sync
            def _(sp):
                sp.dma_start(src[:], c.src_dram).then_inc(s_in, 16)
                for i, k in enumerate(("self", "neigh", "var")):
                    sp.dma_start(Wt[i][:], a[f"l3_WT_{k}"]).then_inc(s_in, 16)
                    sp.dma_start(row[:, i, :], a[f"l3_b_{k}"].partition_broadcast(P)).then_inc(s_in, 16)
                sp.wait_ge(s_in, 16 * 7)

            @block.vector
            def _(dve):
                v = Chain(dve, s_v)
                dve.wait_ge(s_in, 16 * 7)
                for i in (1, 2):
                    v.link(nc.vector.tensor_tensor(row[:, 0, :], row[:, 0, :], row[:, i, :], ALU.add))
        norm_and_table(nc, c, "l3n", h, t)
        with nc.psum_tensor("l3ps1", [P, 4 * BANK], F32) as ps:
            layer3_logits(nc, c, src, h, G, L, ps)
            s_v = sem("l3m_v")
            with nc.Block("l3_counts") as block:
                @block.vector
                def _(dve):
                    v = Chain(dve, s_v)
                    for b, view in blocks_of(ps, D + 1):
                        v.link(nc.vector.tensor_copy(mean[:, b, :], view))
        segment_exp(nc, c, "l3e", L, c.penD, 1)
        with nc.psum_tensor("l3ps2", [P, 8 * BANK], F32) as ps:
            weighted_sums(nc, c, "l3s", "dst", G, L, ps, squares=True)
            s_v = sem("l3f_v")
            with nc.Block("l3_node") as block:
                @block.vector
                def _(dve):
                    V = nc.vector
                    v = Chain(dve, s_v)
                    v.link(V.tensor_scalar(t.s[:].unsqueeze(2), mean[:, :, D:D + 1], 1.0, None, ALU.max))
                    v.link(V.reciprocal(t.s[:], t.s[:]))
                    v.link(V.tensor_tensor(mean[:, :, 0:D], mean[:, :, 0:D], bc(t.s[:].unsqueeze(2), full), ALU.mult))
                    for b, view in blocks_of(ps[:, 4 * BANK:], D):
                        v.link(V.tensor_copy(agg[:, b, 0:D], view))
                    v.link(V.tensor_tensor(agg[:, :, 0:D], agg[:, :, 0:D], bc(t.s[:].unsqueeze(2), full), ALU.mult))
                    v.link(V.tensor_tensor(t.w[:], mean[:, :, 0:D], mean[:, :, 0:D], ALU.mult))
                    v.link(V.tensor_tensor(t.w[:], agg[:, :, 0:D], t.w[:], ALU.subtract))
                    for b, view in blocks_of(ps, D + 1):
                        v.link(V.tensor_copy(agg[:, b, :], view))
                    den = agg[:, :, D:D + 1]
                    v.link(V.tensor_scalar(t.s[:].unsqueeze(2), den, 0.0, None, ALU.is_equal))
                    v.link(V.tensor_tensor(t.s[:].unsqueeze(2), den, t.s[:].unsqueeze(2), ALU.add))
                    v.link(V.reciprocal(t.s[:], t.s[:]))
                    v.link(V.tensor_tensor(agg[:, :, 0:D], agg[:, :, 0:D], bc(t.s[:].unsqueeze(2), full), ALU.mult))
        node_linear(nc, c, "l3w", [(h, Wt[0]), (agg, Wt[1]), (t.w, Wt[2])], c.x, row[:, 0, :], True)


def layer3_logits(nc, c, src, x, G, L, ps):
    sb, pb, sem = c.sb, c.pb, c.sem
    name = "l3a"
    with ExitStack() as st:
        R = [sb(f"{name}R{h}", [P, U, D + 1], F32, st) for h in range(RING)]
        H = [sb(f"{name}H{h}", [P, U, P], F32, st) for h in range(RING)]
        HT = [sb(f"{name}HT{h}", [P, W], F32, st) for h in range(RING)]
        idx = [sb(f"{name}idx{h}", [P, U], I32, st) for h in range(RING)]
        S = sb(name + "S", [P, U, D], F32, st)
        e = sb(name + "e", [P, U], F32, st)
        ps_h = [pb(f"{name}ps_h{h}", [P, W], st) for h in range(RING)]
        ps_q = [pb(f"{name}ps_q{h}", [P, BANK], st)[:, 0:U * D].rearrange("p (u d) -> p u d", u=U) for h in range(RING)]
        s_idx = sem(name + "idx"); s_g = [sem(f"{name}g{h}") for h in range(RING)]
        s_h = sem(name + "h"); s_t = sem(name + "t"); s_tc = sem(name + "tc"); s_q = sem(name + "q")
        s_used = sem(name + "used"); s_keep = sem(name + "keep"); s_v = sem(name + "v"); s_sum = sem(name + "sum")
        s_one = sem(name + "one")
        block = st.enter_context(nc.Block(name))

        @block.gpsimd
        def _(pool):
            gather(nc, c, pool, c.rows_flat, R, idx, s_idx, s_g)

        @block.scalar
        def _(act):
            A = nc.scalar

            def indices(g, h):
                act.wait_ge(s_used, g + 1)
                act.wait_ge(s_keep, g + 1)
                act.wait_ge(s_sum, g + 1)
                apart(act, c.s_apart)
                A.copy(idx[h][:], src[:, ds(g * U, U)]).then_inc(s_idx, 1)

            act.sem_inc(s_keep, RING)
            indices(0, 0)
            with act.Fori(0, ITERS) as i:
                for h in range(RING):
                    g = i * RING + h
                    indices(g + 1, (h + 1) % RING)
                    act.wait_ge(s_t, g + 1)
                    A.copy(HT[h][:], ps_h[h][:]).then_inc(s_tc, 1)
                    act.wait_ge(s_g[h], (i + 1) * (16 * U))
                    apart(act, c.s_apart)
                    A.copy(G[:, ds(g * U, U), :], R[h][:, :, 0:D]).then_inc(s_keep, 1)

        @block.vector
        def _(dve):
            V = nc.vector

            def onehot(g, h):
                V.tensor_tensor(H[h][:], bc(c.iota[:, None, :], [P, U, P]),
                                bc(c.locD[:, ds(g * U, U)].unsqueeze(2), [P, U, P]), ALU.is_equal).then_inc(s_h, 1)

            for h in range(RING):
                V.memset(R[h][:, :, D:D + 1], 1.0).then_inc(s_one, 1)
            dve.sem_inc(s_used, RING)
            onehot(0, 0)
            with dve.Fori(0, ITERS) as i:
                for h in range(RING):
                    g = i * RING + h
                    dve.wait_ge(s_sum, g + RING)
                    onehot(g + 1, (h + 1) % RING)
                    v = Chain(dve, s_v, g * 2)
                    dve.wait_ge(s_q, g + 1)
                    dve.wait_ge(s_g[h], (i + 1) * (16 * U))
                    V.tensor_tensor(S[:], ps_q[h], R[h][:, :, 0:D], ALU.mult).then_inc(s_used, 1)
                    dve.wait_ge(s_used, g + RING + 1)
                    v.link(V.tensor_reduce(e[:], S[:], AX.X, ALU.add))
                    v.link(V.tensor_scalar(L[:, ds(g * U, U), 0], e[:], D ** -0.5, None, ALU.mult))

        @block.tensor
        def _(pe):
            T = nc.tensor
            for j in range(4):
                T.matmul(ps[:, j * BANK:(j + 1) * BANK], c.zeros[:, 0:P], c.zeros[:], start=True, stop=True)
            pe.wait_ge(s_one, RING)
            pe.sem_inc(s_sum, RING)
            with pe.Fori(0, ITERS) as i:
                for h in range(RING):
                    g = i * RING + h
                    pe.wait_ge(s_h, g + 1)
                    for k in range(U):
                        last = T.transpose(ps_h[h][:, k * P:(k + 1) * P], H[h][:, k, :], c.ident[:])
                    last.then_inc(s_t, 1)
                    blk = blocks_at(nc, PE, c.blkD, g)
                    pe.wait_ge(s_tc, g + 1)
                    pe.wait_ge(s_used, g + 1)
                    for k in range(U):
                        last = T.matmul(ps_q[h][:, k, :], HT[h][:, k * P:(k + 1) * P], x[:, ds(blk[k], 1), :]
                                        .rearrange("p a d -> p (a d)"), start=True, stop=True)
                    last.then_inc(s_q, 1)
                    cols = columns_at(nc, PE, c.blkD, g)
                    pe.wait_ge(s_g[h], (i + 1) * (16 * U))
                    for k in range(U):
                        last = T.matmul(ps[:, ds(cols[k], D + 1)], H[h][:, k, :], R[h][:, k, :], start=False, stop=True,
                                        skip_group_check=True)
                    last.then_inc(s_sum, 1)


HEADS = 4
HEAD_D = [(max(0, (F1 // HEADS * n - D) // 8), (F1 // HEADS * (n + 1) - D) // 8) for n in range(HEADS)]
OUTER = 8 * D


def layer1(nc, c):
    sb, sem, a = c.sb, c.sem, c.a
    full = [P, BLOCKS, D]
    G = nc.dram_tensor("l1_G", (P, STEPS * D), F32, kind="Internal").ap()
    hidden = nc.dram_tensor("l1_hidden", (D, STEPS * P), F32, kind="Internal").ap()
    st = ExitStack()
    with st:
        src = sb("l1src", [P, STEPS + U], I32, st)
        val = sb("l1val", [P, STEPS, 9], F32, st)
        L = sb("l1L", [P, STEPS, HEADS], F32, st)
        WE = sb("l1WE", [P, STEPS, HEADS + 1], F32, st)
        W1 = sb("l1W1", [D, P], F32, st)
        W2 = sb("l1W2", [P, P], F32, st)
        K3, V3 = (sb(f"l1{k}", [D, F1], F32, st) for k in ("K3", "V3"))
        Wl = sb("l1Wl", [P, HEADS], F32, st)
        s_in = sem("l1_in"); s_w2 = sem("l1_w2")
        with nc.Block("l1_start") as block:
            @block.sync
            def _(sp):
                sp.dma_start(src[:], c.src_dram).then_inc(s_in, 16)
                sp.dma_start(val[:].rearrange("p s f -> p (s f)"), c.val_dram).then_inc(s_in, 16)
                sp.wait_ge(s_w2, 1)
                for t_, k in ((W1[:, 0:D], "Wk1"), (W2[0:D, 0:D], "Wk2"), (K3[:], "Wk3"), (W1[:, D:P], "Wv1"),
                              (W2[D:P, D:P], "Wv2"), (V3[:], "Wv3"), (Wl[:], "W_logit")):
                    sp.dma_start(t_, a["l1_" + k]).then_inc(s_in, 16)
                sp.wait_ge(s_in, 16 * 9)

            @block.vector
            def _(dve):
                nc.vector.memset(W2[:], 0.0).then_inc(s_w2, 1)

        with ExitStack() as keys:
            h = sb("l1h", full, F32, keys)
            sh2 = sb("l1sh2", [P, STEPS, 8], F32, keys)
            t = Scratch(s=sb("l1s", [P, BLOCKS], F32, keys), w=sb("l1w", full, F32, keys))
            norm_and_table(nc, c, "l1n", h, t)
            with nc.Block("l1_squares") as block:
                @block.vector
                def _(dve):
                    nc.vector.tensor_tensor(sh2[:], val[:, :, 1:9], val[:, :, 1:9], ALU.mult)
            layer1_logits(nc, c, src, h, sh2, L, G, hidden, W1, W2, K3, Wl)
        segment_exp(nc, c, "l1e", L, c.penD, HEADS)
        s_v = sem("l1w_v"); s_q = sem("l1w_q"); s_r = sem("l1w_r")
        with nc.sbuf_tensor("l1pos", [P, STEPS, HEADS], F32) as pos, nc.Block("l1_weights") as block:
            @block.vector
            def _(dve):
                V = nc.vector
                v = Chain(dve, s_v)
                v.link(V.tensor_tensor(WE[:, :, 0:HEADS], L[:], bc(val[:, :, 0:1], [P, STEPS, HEADS]), ALU.mult))
                v.link(V.tensor_copy(WE[:, :, HEADS:HEADS + 1], val[:, :, 0:1]))
                v.link(V.tensor_scalar(pos[:], WE[:, :, 0:HEADS], 0.0, None, ALU.is_gt))
                V.tensor_scalar(L[:], WE[:, :, 0:HEADS], 1e-34, None, ALU.max).then_inc(s_q, 1)
                dve.wait_ge(s_r, 1)
                v.link(V.tensor_tensor(L[:], L[:], pos[:], ALU.mult))

            @block.scalar
            def _(act):
                act.wait_ge(s_q, 1)
                nc.scalar.activation(L[:], L[:], ACT.Sqrt).then_inc(s_r, 1)

        acc = sb("l1acc", [P, BLOCKS, F1 + HEADS + 1], F32, st)
        layer1_values(nc, c, val, L, WE, G, hidden, V3, acc)
        layer1_output(nc, c, acc)


def layer1_logits(nc, c, src, x, sh2, L, G, hidden, W1, W2, K3, Wl):
    sb, pb, sem, a = c.sb, c.pb, c.sem, c.a
    name = "l1a"
    with ExitStack() as st:
        R = [sb(f"{name}R{h}", [P, U, D], F32, st) for h in range(RING)]
        loc = [sb(f"{name}loc{h}", [P, W], F32, st) for h in range(RING)]
        HT = [sb(f"{name}HT{h}", [P, W], F32, st) for h in range(RING)]
        idx = [sb(f"{name}idx{h}", [P, U], I32, st) for h in range(RING)]
        ea = [sb(f"{name}ea{h}", [D, W], F32, st) for h in range(RING)]
        g1 = sb(name + "g1", [P, W], F32, st)
        g2 = [sb(f"{name}g2{h}", [P, W], F32, st) for h in range(RING)]
        z = [sb(f"{name}z{h}", [P, U, D], F32, st) for h in range(RING)]
        m = [sb(f"{name}m{j}", [P, D, 8], F32, st) for j in range(2)]
        scal = [sb(f"{name}scal{h}", [P, U, P], F32, st) for h in range(RING)]
        k1 = sb(name + "k1", [P, U, D], F32, st)
        scT = sb(name + "scT", [P, W], F32, st)
        ps_m = pb(name + "ps_m", [P, W], st)
        ps_q = pb(name + "ps_q", [P, BANK], st)[:, 0:U * D].rearrange("p (u d) -> p u d", u=U)
        ps_d = [pb(f"{name}ps_d{j}", [P, OUTER], st) for j in range(2)]
        ps_0 = pb(name + "ps_0", [P, BANK], st)[:, 0:U * D].rearrange("p (u d) -> p u d", u=U)
        ps_s = pb(name + "ps_s", [P, W], st)
        ps_l = pb(name + "ps_l", [P, BANK], st)[:, 0:U * HEADS].rearrange("p (u n) -> p u n", u=U)
        s_idx = sem(name + "idx"); s_g = [sem(f"{name}g{h}") for h in range(RING)]
        s_G = [sem(f"{name}G{h}") for h in range(RING)]; s_ea = [sem(f"{name}ea{h}") for h in range(RING)]
        s_loc = [sem(f"{name}loc{h}") for h in range(RING)]
        s_h = sem(name + "h"); s_q = sem(name + "q")
        s_z = sem(name + "z"); s_m1 = sem(name + "m1"); s_m2 = sem(name + "m2"); s_a1 = sem(name + "a1")
        s_a2 = sem(name + "a2"); s_k = sem(name + "k"); s_0 = sem(name + "0"); s_d = sem(name + "d"); s_v = sem(name + "v")
        s_scal0 = sem(name + "scal0"); s_scal = sem(name + "scal"); s_st = sem(name + "st")
        s_stc = sem(name + "stc"); s_l = sem(name + "l")
        s_L = sem(name + "L"); s_hid = [sem(f"{name}hid{h}") for h in range(RING)]
        block = st.enter_context(nc.Block(name))

        @block.gpsimd
        def _(pool):
            gather(nc, c, pool, c.rows_flat, R, idx, s_idx, s_g)

        @block.sync
        def _(sp):
            def edges(g, h):
                sp.wait_ge(s_m1, g + 1)
                e0 = four(nc, SP, c.edge0, g * U, E)
                for k in range(U):
                    sp.dma_start(ea[h][:, k * P:(k + 1) * P], a["l1_edges"][:, ds(e0[k], P)]).then_inc(s_ea[h], 16)
                sp.wait_ge(s_h, g + 1)
                sp.dma_start(loc[h][:], c.loc_dram[ds(g * W, W)].partition_broadcast(P)).then_inc(s_loc[h], 16)

            edges(0, 0)
            with sp.Fori(0, ITERS) as i:
                for h in range(RING):
                    g = i * RING + h
                    edges(g + 1, (h + 1) % RING)
                    sp.wait_ge(s_g[h], (i + 1) * (16 * U))
                    sp.dma_start(G[:, ds(g * (U * D), U * D)], R[h][:].rearrange("p u d -> p (u d)")
                                 ).then_inc(s_G[h], 16)
                    sp.wait_ge(s_a2, g + 1)
                    sp.dma_start(hidden[:, ds(g * W, W)], g2[h][D:P, :]).then_inc(s_hid[h], 16)
            for h in range(RING):
                sp.wait_ge(s_G[h], 16 * ITERS)
                sp.wait_ge(s_hid[h], 16 * ITERS)
            sp.wait_ge(s_ea[0], 16 * U * (ITERS + 1))
            sp.wait_ge(s_loc[0], 16 * (ITERS + 1))

        @block.scalar
        def _(act):
            A = nc.scalar

            def groups(i):
                for h in range(RING):
                    g = i * RING + h
                    start = isinstance(i, int) and h == 0
                    act.wait_ge(s_z, g + RING)
                    if not start:
                        act.wait_ge(s_G[(h + 1) % RING], (i + h) * 16)
                    apart(act, c.s_apart)
                    A.copy(idx[(h + 1) % RING][:], src[:, ds((g + 1) * U, U)]).then_inc(s_idx, 1)
                    act.wait_ge(s_m1, g + RING + 2)
                    A.activation(g1[:], ps_m[:], ACT.Gelu_apprx_tanh).then_inc(s_a1, 1)
                    if not start:
                        act.wait_ge(s_st, g)
                        A.copy(scT[:], ps_s[:]).then_inc(s_stc, 1)
                        act.wait_ge(s_hid[(h + 1) % RING], (i + h) * 16)
                        apart(act, c.s_apart)
                    act.wait_ge(s_m2, g + 2)
                    A.activation(g2[(h + 1) % RING][:], ps_m[:], ACT.Gelu_apprx_tanh).then_inc(s_a2, 1)

            A.copy(idx[0][:], src[:, 0:U]).then_inc(s_idx, 1)
            act.wait_ge(s_m1, RING + 1)
            A.activation(g1[:], ps_m[:], ACT.Gelu_apprx_tanh).then_inc(s_a1, 1)
            act.wait_ge(s_m2, 1)
            A.activation(g2[0][:], ps_m[:], ACT.Gelu_apprx_tanh).then_inc(s_a2, 1)
            groups(0)
            with act.Fori(1, ITERS) as i:
                groups(i)
            act.wait_ge(s_st, GROUPS)
            A.copy(scT[:], ps_s[:]).then_inc(s_stc, 1)

        @block.vector
        def _(dve):
            V = nc.vector

            def onehot(g, h, loads):
                dve.wait_ge(s_loc[h], loads * 16)
                V.tensor_scalar(HT[h][:], loc[h][:], c.iota_p[:, 0:1], None, ALU.is_equal).then_inc(s_h, 1)

            def logits(g):
                dve.wait_ge(s_l, g + 1)
                V.tensor_scalar(L[:, ds(g * U, U), :], ps_l, 1.0, None, ALU.mult).then_inc(s_L, 1)

            def groups(i):
                for h in range(RING):
                    g = i * RING + h
                    dve.wait_ge(s_q, g + 1)
                    dve.wait_ge(s_g[h], (i + 1) * (16 * U))
                    V.tensor_tensor(z[h][:], ps_q, R[h][:], ALU.mult).then_inc(s_z, 1)
                    onehot(g + 1, (h + 1) % RING, i + 1 + (h + 1) // RING)
                    dve.wait_ge(s_z, g + RING + 1)
                    dve.wait_ge(s_0, g + 1)
                    V.tensor_tensor(scal[h][:, :, 0:D], z[h][:], ps_0, ALU.mult).then_inc(s_scal0, 1)
                    if not (isinstance(i, int) and h == 0):
                        dve.wait_ge(s_scal, g)
                    for k in range(U + 1):
                        s = g * U + k
                        if k < U:
                            dve.wait_ge(s_k, s + 1)
                            if not (isinstance(i, int) and h == 0 and k < 2):
                                dve.wait_ge(s_v, s - 1)
                            V.tensor_tensor(m[k % 2][:], ps_d[k % 2][:].rearrange("p (d s) -> p d s", s=8),
                                            bc(sh2[:, ds(s, 1), :], [P, D, 8]), ALU.mult).then_inc(s_d, 1)
                        if k:
                            dve.wait_ge(s_d, s + 2)
                            V.tensor_reduce(k1[:, k - 1, :], m[(k - 1) % 2][:], AX.X, ALU.add).then_inc(s_v, 1)
                    if not (isinstance(i, int) and h == 0):
                        logits(g - 1)
                    dve.wait_ge(s_v, (g + 1) * U)
                    V.tensor_tensor(scal[h][:, :, D:P], z[h][:], k1[:], ALU.mult).then_inc(s_scal, 1)

            dve.sem_inc(s_z, RING)
            dve.sem_inc(s_d, 2)
            onehot(0, 0, 1)
            groups(0)
            with dve.Fori(1, ITERS) as i:
                groups(i)
            logits(GROUPS - 1)

        @block.tensor
        def _(pe):
            T = nc.tensor

            def first_layer(h, loads):
                pe.wait_ge(s_ea[h], loads * (16 * U))
                T.matmul(ps_m[:], W1[:], ea[h][:], start=True, stop=True).then_inc(s_m1, 1)

            def second_layer(g):
                pe.wait_ge(s_a1, g + 1)
                T.matmul(ps_m[:], W2[:], g1[:], start=True, stop=True).then_inc(s_m2, 1)

            def dst_rows(g, h):
                blk = blocks_at(nc, PE, c.blkD, g)
                pe.wait_ge(s_h, g + RING + 1)
                pe.wait_ge(s_z, g + RING)
                for k in range(U):
                    last = T.matmul(ps_q[:, k, :], HT[h][:, k * P:(k + 1) * P], x[:, ds(blk[k], 1), :]
                                    .rearrange("p a d -> p (a d)"), start=True, stop=True)
                last.then_inc(s_q, 1)

            def plain_channels(g, h, read):
                pe.wait_ge(s_a2, g + 1)
                if read:
                    pe.wait_ge(s_scal0, g)
                for k in range(U):
                    last = T.matmul(ps_0[:, k, :], g2[h][0:D, k * P:(k + 1) * P], K3[:, 0:D], start=True, stop=True)
                last.then_inc(s_0, 1)

            def channels(s, k, h):
                pe.wait_ge(s_d, s + 1)
                T.matmul(ps_d[k % 2][:], g2[h][0:D, k * P:(k + 1) * P], K3[:, D:F1], start=True, stop=True
                         ).then_inc(s_k, 1)

            def turn(g, h):
                pe.wait_ge(s_scal, g + 1)
                for k in range(U):
                    last = T.transpose(ps_s[:, k * P:(k + 1) * P], scal[h][:, k, :], c.ident[:])
                last.then_inc(s_st, 1)

            def logits(g, read):
                pe.wait_ge(s_stc, g + 1)
                if read:
                    pe.wait_ge(s_L, g)
                for k in range(U):
                    last = T.matmul(ps_l[:, k, :], scT[:, k * P:(k + 1) * P], Wl[:], start=True, stop=True)
                last.then_inc(s_l, 1)

            def groups(i):
                for h in range(RING):
                    g = i * RING + h
                    after_first = not (isinstance(i, int) and h == 0)
                    hn = (h + 1) % RING
                    channels(g * U, 0, h)
                    first_layer(hn, i + 1 + (h + 1) // RING)
                    channels(g * U + 1, 1, h)
                    if after_first:
                        turn(g - 1, hn)
                    second_layer(g + 1)
                    channels(g * U + 2, 2, h)
                    dst_rows(g + 1, hn)
                    channels(g * U + 3, 3, h)
                    if after_first:
                        logits(g - 1, not (isinstance(i, int) and h == 1))
                    plain_channels(g + 1, hn, True)

            pe.sem_inc(s_m1, RING)
            pe.sem_inc(s_h, RING)
            first_layer(0, 1)
            second_layer(0)
            dst_rows(0, 0)
            plain_channels(0, 0, False)
            groups(0)
            with pe.Fori(1, ITERS) as i:
                groups(i)
            turn(GROUPS - 1, 1)
            logits(GROUPS - 1, True)


def layer1_values(nc, c, val, A, WE, G, hidden, V3, acc):
    sb, pb, sem, a = c.sb, c.pb, c.sem, c.a
    name = "l1v"
    M = D + HEADS + 1
    with ExitStack() as st:
        R = [sb(f"{name}R{h}", [P, U, D], F32, st) for h in range(RING)]
        H = [sb(f"{name}H{h}", [P, U, P], F32, st) for h in range(RING)]
        g2 = [sb(f"{name}g2{h}", [D, W], F32, st) for h in range(RING)]
        xa = [sb(f"{name}xa{h}", [P, U, D], F32, st) for h in range(RING)]
        xs = [sb(f"{name}xs{k}", [P, D, 8], F32, st) for k in range(U)]
        x0 = [sb(f"{name}x0{h}", [P, U, D], F32, st) for h in range(RING)]
        Yd = [sb(f"{name}Yd{k}", [P, D, 8], F32, st) for k in range(U)]
        Y0 = [sb(f"{name}Y0{h}", [P, U, M], F32, st) for h in range(RING)]
        ps_d = [pb(f"{name}ps_d{j}", [P, OUTER], st) for j in range(2)]
        ps_0 = pb(name + "ps_0", [P, BANK], st)[:, 0:U * D].rearrange("p (u d) -> p u d", u=U)
        ps_sd = [pb(f"{name}ps_sd{j}", [P, OUTER], st) for j in range(2)]
        ps_s0 = [pb(f"{name}ps_s0{j}", [P, BANK], st)[:, 0:M] for j in range(2)]
        s_R = [sem(f"{name}R{h}") for h in range(RING)]; s_g2 = [sem(f"{name}g2{h}") for h in range(RING)]
        s_h = sem(name + "h"); s_hu = sem(name + "hu"); s_k = sem(name + "k"); s_0 = sem(name + "0"); s_v = sem(name + "v")
        s_y0 = sem(name + "y0"); s_d = sem(name + "d"); s_seg = sem(name + "seg")
        s_acc = sem(name + "acc"); s_x = sem(name + "x"); s_z = sem(name + "z"); s_xs = sem(name + "xs")
        block = st.enter_context(nc.Block(name))

        @block.gpsimd
        def _(pool):
            pool.sem_inc(s_x, RING)
            with pool.Fori(0, ITERS) as i:
                for h in range(RING):
                    g = i * RING + h
                    at = g * U
                    pool.wait_ge(s_R[h], (i + 1) * 16)
                    pool.wait_ge(s_y0, g * 2 + 2)
                    for n, (d0, d1) in enumerate(HEAD_D):
                        nc.gpsimd.tensor_tensor(xa[h][:, :, d0:d1], R[h][:, :, d0:d1],
                                                bc(A[:, ds(at, U), n:n + 1], [P, U, d1 - d0]), ALU.mult).then_inc(s_v, 1)
                    nc.gpsimd.tensor_tensor(x0[h][:], R[h][:], bc(A[:, ds(at, U), 0:1], [P, U, D]),
                                            ALU.mult).then_inc(s_x, 1)
                    pool.wait_ge(s_v, (g + 1) * HEADS)
                    for k in range(U):
                        s = at + k
                        pool.wait_ge(s_d, s + 1)
                        nc.gpsimd.tensor_tensor(xs[k][:], bc(xa[h][:, k, :].unsqueeze(2), [P, D, 8]),
                                                bc(val[:, ds(s, 1), 1:9], [P, D, 8]), ALU.mult).then_inc(s_xs, 1)
                    pool.wait_ge(s_xs, (g + 1) * U)

        @block.sync
        def _(sp):
            with sp.Fori(0, ITERS) as i:
                for h in range(RING):
                    g = i * RING + h
                    sp.wait_ge(s_hu, g + 1)
                    sp.dma_start(g2[h][:], hidden[:, ds(g * W, W)]).then_inc(s_g2[h], 16)
                    sp.wait_ge(s_x, g + 1)
                    sp.dma_start(R[h][:].rearrange("p u d -> p (u d)"), G[:, ds(g * (U * D), U * D)]
                                 ).then_inc(s_R[h], 16)

        @block.vector
        def _(dve):
            V = nc.vector

            def add(s, j, blk):
                dve.wait_ge(s_seg, s + 1)
                d = acc[:, ds(blk, 1), 0:OUTER].rearrange("p a f -> p (a f)")
                V.tensor_tensor(d, d, ps_sd[j][:], ALU.add).then_inc(s_acc, 1)
                d = acc[:, ds(blk, 1), OUTER:].rearrange("p a f -> p (a f)")
                V.tensor_tensor(d, d, ps_s0[j], ALU.add).then_inc(s_acc, 1)
                dve.wait_ge(s_acc, 2 * s + 2 + 4)

            def groups(i):
                for h in range(RING):
                    g = i * RING + h
                    at = g * U
                    V.tensor_tensor(H[h][:], bc(c.iota[:, None, :], [P, U, P]),
                                    bc(c.locD[:, ds(at, U)].unsqueeze(2), [P, U, P]), ALU.is_equal).then_inc(s_h, 1)
                    V.tensor_scalar(Y0[h][:, :, D:M], WE[:, ds(at, U), :], 1.0, None, ALU.mult).then_inc(s_y0, 1)
                    dve.wait_ge(s_x, g + RING + 1)
                    dve.wait_ge(s_0, g + 1)
                    V.tensor_tensor(Y0[h][:, :, 0:D], ps_0, x0[h][:], ALU.mult).then_inc(s_y0, 1)
                    before = four(nc, DVE, c.prevD, at, BLOCKS - 1)
                    for k in range(U):
                        s = at + k
                        first = isinstance(i, int) and h == 0 and k == 0
                        dve.wait_ge(s_k, s + 1)
                        dve.wait_ge(s_xs, s + 1)
                        V.tensor_tensor(Yd[k][:], ps_d[k % 2][:].rearrange("p (d s) -> p d s", s=8),
                                        xs[k][:], ALU.mult).then_inc(s_d, 1)
                        if not first:
                            add(s - 1, (k + 1) % 2, before[k])

            dve.sem_inc(s_y0, 2 * RING)
            dve.sem_inc(s_d, U)
            V.memset(acc[:], 0.0).then_inc(s_z, 1)
            dve.wait_ge(s_z, 1)
            dve.sem_inc(s_acc, 4)
            groups(0)
            with dve.Fori(1, ITERS) as i:
                groups(i)
            blk = dve.value_load(c.blkD[0:1, GROUPS - 1, 0, U - 1:U], min_val=0, max_val=BLOCKS - 1)
            add(STEPS - 1, 1, blk)

        @block.tensor
        def _(pe):
            T = nc.tensor

            def segment(s, k, h):
                pe.wait_ge(s_d, s + 1 + U)
                pe.wait_ge(s_acc, 2 * s + 2)
                T.matmul(ps_sd[k % 2][:], H[h][:, k, :], Yd[k][:].rearrange("p d s -> p (d s)"), start=True, stop=True)
                T.matmul(ps_s0[k % 2], H[h][:, k, :], Y0[h][:, k, :], start=True, stop=True).then_inc(s_seg, 1)

            def groups(i):
                for h in range(RING):
                    g = i * RING + h
                    pe.wait_ge(s_g2[h], (i + 1) * 16)
                    if not (isinstance(i, int) and h == 0):
                        pe.wait_ge(s_y0, 2 * g + 2 * RING)
                    for k in range(U):
                        last = T.matmul(ps_0[:, k, :], g2[h][:, k * P:(k + 1) * P], V3[:, 0:D], start=True, stop=True)
                    last.then_inc(s_0, 1)
                    for k in range(U):
                        s = g * U + k
                        pe.wait_ge(s_d, s + U - 1)
                        last = T.matmul(ps_d[k % 2][:], g2[h][:, k * P:(k + 1) * P], V3[:, D:F1], start=True, stop=True)
                        last.then_inc(s_k, 1)
                        if k == 1:
                            pe.wait_ge(s_h, g + 1)
                            pe.wait_ge(s_y0, 2 * g + 2 + 2 * RING)
                        if k or not isinstance(i, int) or h:
                            segment(s - 1, (k - 1) % U, h if k else (h + 1) % RING)
                    pe.wait_ge(s_seg, g * U + U - 1)
                    pe.sem_inc(s_hu, 1)

            pe.sem_inc(s_hu, RING)
            groups(0)
            with pe.Fori(1, ITERS) as i:
                groups(i)
            segment(STEPS - 1, U - 1, 1)


def layer1_output(nc, c, acc):
    sb, pb, sem, a = c.sb, c.pb, c.sem, c.a
    name = "l1o"
    Z = OUTER + D
    with ExitStack() as st:
        z = sb(name + "z", [P, BLOCKS, HEADS], F32, st)
        zero = sb(name + "zero", [P, BLOCKS, HEADS], F32, st)
        Wo = sb(name + "Wo", [P, 5, D], F32, st)
        aT = [sb(f"{name}aT{j}", [P, 5, P], F32, st) for j in range(2)]
        ps_t = [pb(f"{name}ps_t{j}", [P, 4, P], st) for j in range(2)]
        ps_u = [pb(f"{name}ps_u{j}", [D, BANK], st)[:, 0:P] for j in range(2)]
        ps_o = [pb(f"{name}ps_o{j}", [P, BANK], st)[:, 0:D] for j in range(2)]
        s_in = sem(name + "in"); s_v = sem(name + "v"); s_q = sem(name + "q"); s_r = sem(name + "r")
        s_s = sem(name + "s"); s_t = sem(name + "t"); s_c = sem(name + "c"); s_o = sem(name + "o")
        s_x = sem(name + "x")
        block = st.enter_context(nc.Block(name))

        @block.sync
        def _(sp):
            sp.dma_start(Wo[:, 0:4, :], a["l1_W_out"][D:F1, :].rearrange("(c p) o -> p c o", p=P)).then_inc(s_in, 16)
            sp.dma_start(Wo[0:D, 4, :], a["l1_W_out"][0:D, :]).then_inc(s_in, 16)

        @block.vector
        def _(dve):
            V = nc.vector
            v = Chain(dve, s_v)
            v.link(V.tensor_scalar(zero[:], acc[:, :, Z:Z + HEADS], 0.0, None, ALU.is_equal))
            v.link(V.tensor_tensor(z[:], acc[:, :, Z:Z + HEADS], zero[:], ALU.add))
            v.link(V.tensor_copy(c.deg[:].unsqueeze(2), acc[:, :, Z + HEADS:Z + HEADS + 1]))
            V.reciprocal(z[:], z[:]).then_inc(s_q, 1)
            dve.wait_ge(s_r, 1)
            for n, (d0, d1) in enumerate(HEAD_D):
                part = acc[:, :, 8 * d0:8 * d1]
                v.link(V.tensor_tensor(part, part, bc(z[:, :, n:n + 1], [P, BLOCKS, 8 * (d1 - d0)]), ALU.mult))
            part = acc[:, :, OUTER:Z]
            V.tensor_tensor(part, part, bc(z[:, :, 0:1], [P, BLOCKS, D]), ALU.mult).then_inc(s_s, 1)
            for b in range(BLOCKS):
                dve.wait_ge(s_o, b + 1)
                V.tensor_tensor(c.x[:, b, :], c.x[:, b, :], ps_o[b % 2], ALU.add).then_inc(s_x, 1)

        @block.scalar
        def _(act):
            act.wait_ge(s_q, 1)
            nc.scalar.activation(z[:], z[:], ACT.Sqrt).then_inc(s_r, 1)
            for b in range(BLOCKS):
                act.wait_ge(s_t, b + 1)
                if b >= 2:
                    act.wait_ge(s_o, b - 1)
                nc.scalar.copy(aT[b % 2][:, 0:4, :], ps_t[b % 2][:]).then_inc(s_c, 1)
                nc.scalar.copy(aT[b % 2][0:D, 4, :], ps_u[b % 2]).then_inc(s_c, 1)

        @block.tensor
        def _(pe):
            T = nc.tensor
            pe.wait_ge(s_s, 1)
            pe.wait_ge(s_in, 32)
            for b in range(BLOCKS):
                if b >= 2:
                    pe.wait_ge(s_c, 2 * (b - 1))
                for j in range(4):
                    T.transpose(ps_t[b % 2][:, j, :], acc[:, b, j * P:(j + 1) * P], c.ident[:])
                T.transpose(ps_u[b % 2], acc[:, b, OUTER:Z], c.ident[:]).then_inc(s_t, 1)
                pe.wait_ge(s_c, 2 * (b + 1))
                if b >= 2:
                    pe.wait_ge(s_x, b - 1)
                for j in range(4):
                    T.matmul(ps_o[b % 2], aT[b % 2][:, j, :], Wo[:, j, :], start=(j == 0), stop=False)
                T.matmul(ps_o[b % 2], aT[b % 2][0:D, 4, :], Wo[0:D, 4, :], start=False, stop=True).then_inc(s_o, 1)


def finish(nc, c):
    s_out = c.sem("out")
    with nc.Block("finish") as block:
        @block.sync
        def _(sp):
            sp.dma_start(c.out.rearrange("(b p) d -> p b d", p=P), c.x[:]).then_inc(s_out, 16)
            sp.wait_ge(s_out, 16)


def prepare(nc, c):
    st, banks = ExitStack(), ExitStack()
    sb, pb, sem, a = c.sb, c.pb, c.sem, c.a
    NB = BLOCKS
    with st:
        recD = sb("recD", [P, STEPS + U, 4], I32, st)
        frecD = sb("frecD", [P, STEPS, 9], F32, st)
        srcI = sb("srcI", [P, TILES + U, 4], I32, st)
        dstI = sb("dstI", [P, TILES], I32, st)
        srcB = sb("srcB", [P, TILES + U], F32, st)
        srcL = sb("srcL", [P, TILES + U], F32, st)
        dstB = sb("dstB", [P, TILES], F32, st)
        tmpI = sb("tmpI", [P, TILES + U], I32, st)
        junk = sb("junk", [P, TILES + U], F32, st)
        junk2 = sb("junk2", [P, STEPS], F32, st)
        cntp = sb("cntp", [P, 2, 32], F32, st)
        cnt = sb("cnt", [P, 2, 32], F32, st)
        tilesI = sb("tilesI", [P, 2, 32], I32, st)
        tiles = sb("tiles", [P, 2, 32], F32, st)
        first = sb("first", [P, 2, 33], F32, st)
        shift = sb("shift", [P, 32], F32, st)
        steps = sb("steps", [P, STEPS], F32, st)
        blk = sb("blk", [P, 2, STEPS], F32, st)
        off = sb("off", [P, STEPS], F32, st)
        seven = sb("seven", [P, 2, STEPS], F32, st)
        before = sb("before", [P, P], F32, st)
        after = sb("after", [P, P], F32, st)
        prev = sb("prev", [P, P], F32, st)
        nxt = sb("nxt", [P, P], F32, st)
        Hr = [sb(f"Hr{h}", [P, U, P], F32, st) for h in range(RING)]
        Hb = [sb(f"Hb{h}", [P, U, NB], F32, st) for h in range(RING)]
        HT = [sb(f"HT{h}", [P, W], F32, st) for h in range(RING)]
        eq = sb("eq", [P, U, P], F32, st)
        low = sb("low", [P, W], I32, st)
        row = [sb(f"row{h}", [P, W], I32, st) for h in range(RING)]
        rank = sb("rank", [P, RING, U], F32, st)
        C = sb("C", [P, RING, U, NB], F32, st)
        Cc = sb("Cc", [P, NB], F32, st)
        sel = sb("sel", [P, U, NB], F32, st)
        pos = sb("pos", [P, U], F32, st)
        posI = sb("posI", [P, U], I32, st)
        posA = sb("posA", [P, U], I32, st)
        posB = sb("posB", [P, U], I32, st)
        posC = sb("posC", [P, U], I32, st)
        idx = [sb(f"idx{h}", [P, U], I32, st) for h in range(RING)]
        rbuf = [sb(f"rbuf{h}", [P, U, 4], I32, st) for h in range(RING)]
        ps_cnt = pb("ps_cnt", [P, BANK], banks)
        ps_hist = pb("ps_hist", [P, BANK], banks)
        ps_base = pb("ps_base", [P, BANK], banks)
        ps_new = [pb(f"ps_new{h}", [P, U, NB], banks) for h in range(RING)]
        ps_sel = pb("ps_sel", [P, U, NB], banks)

        s_const = sem("p_const"); s_cchain = sem("p_cchain")
        s_in = sem("p_in"); s_fill = sem("p_fill"); s_fill0 = sem("p_fill0")
        s_v = sem("p_v"); s_cntp = sem("p_cntp"); s_cnt = sem("p_cnt"); s_off = sem("p_off")
        s_rec = sem("p_rec"); s_frec = sem("p_frec")
        s_h1 = sem("p_hist_onehot"); s_h1u = sem("p_hist_used"); s_base0 = sem("p_hist_done")
        s_cs = sem("p_cnt_copied"); s_base = sem("p_base")
        s_oh = sem("p_onehots"); s_new = sem("p_new_counts"); s_C = sem("p_counts_set")
        s_selr = sem("p_sel_ready"); s_idx = sem("p_idx"); s_vl = sem("p_vl"); s_vh = sem("p_vh")
        s_row = [sem(f"p_row{h}") for h in range(RING)]
        s_rowu = sem("p_row_used"); s_ohu = sem("p_onehots_used"); s_selu = sem("p_sel_used")
        s_sc = [sem(f"p_scatter{h}") for h in range(RING)]
        s_scf = sem("p_scatter_free"); s_start = sem("p_start")

        block = banks.enter_context(nc.Block("prepare"))

        @block.sync
        def _(sp):
            sp.dma_start(srcI[:], a["edges_by_partition"]).then_inc(s_in, 16)
            sp.dma_start(dstI[:], a["dst_by_partition"]).then_inc(s_in, 16)
            sp.dma_start(c.x[:], a["x"].rearrange("(b p) d -> p b d", p=P)).then_inc(s_in, 16)
            sp.wait_ge(s_fill0, 2)
            sp.dma_start(c.recS_dram.rearrange("(p s) f -> p (s f)", p=P),
                         c.recS[:, 0:STEPS, :].rearrange("p s f -> p (s f)")).then_inc(s_fill, 16)
            rows = a["src_by_tile"]
            with sp.Fori(0, TITERS) as i:
                for h in range(RING):
                    sp.wait_ge(s_rowu, i * RING + h + 1)
                    sp.dma_start(row[h][:], rows[ds((i * RING + h) * W, W)].partition_broadcast(P)
                                 ).then_inc(s_row[h], 16)
            sp.wait_ge(s_rowu, TGROUPS + 1)
            sp.dma_start(row[0][:], rows[TGROUPS * W:TGROUPS * W + W].partition_broadcast(P)
                         ).then_inc(s_row[0], 16)
            sp.wait_ge(s_row[0], 16 * (TITERS + 1))

        @block.gpsimd
        def _(pool):
            g = Chain(pool, s_cchain)
            nc.gpsimd.iota(c.iota[:], pattern=[[1, P]], base=0, channel_multiplier=0,
                           allow_small_or_imprecise_dtypes=True).then_inc(s_const, 1)
            nc.gpsimd.iota(c.iota_p[:], pattern=[[0, 1]], base=0, channel_multiplier=1,
                           allow_small_or_imprecise_dtypes=True).then_inc(s_const, 1)
            nc.gpsimd.iota(steps[:], pattern=[[1, STEPS]], base=0, channel_multiplier=0,
                           allow_small_or_imprecise_dtypes=True).then_inc(s_const, 1)
            nc.gpsimd.memset(c.zeros[:], 0.0).then_inc(s_const, 1)
            g.link(nc.gpsimd.memset(c.ident[:], 0.0))
            g.link(nc.gpsimd.memset(prev[:], 0.0))
            g.link(nc.gpsimd.memset(nxt[:], 0.0))
            g.link(nc.gpsimd.memset(c.ones[:], 1.0))
            for t, base in ((c.ident, 0), (prev, 1), (nxt, -1)):
                nc.gpsimd.affine_select(out=t[:], in_=t[:], compare_op=ALU.not_equal, fill=1.0, base=base,
                                        pattern=[[-1, P]], channel_multiplier=1).then_inc(s_const, 1)
            nc.gpsimd.affine_select(out=before[:], in_=c.ones[:], compare_op=ALU.is_gt, fill=0.0, base=0,
                                    pattern=[[-1, P]], channel_multiplier=1).then_inc(s_const, 1)
            nc.gpsimd.affine_select(out=after[:], in_=c.ones[:], compare_op=ALU.is_gt, fill=0.0, base=0,
                                    pattern=[[1, P]], channel_multiplier=-1).then_inc(s_const, 1)
            pool.wait_ge(s_fill, 16)
            with pool.Fori(0, TITERS) as i:
                for h in range(RING):
                    pool.wait_ge(s_idx, i * RING + h + 1)
                    apart(pool, c.s_apart)
                    for k in range(U):
                        last = nc.gpsimd.indirect_dma_start(
                            out=c.recS_dram, out_offset=bass.IndirectOffsetOnAxis(ap=idx[h][:, k:k + 1], axis=0),
                            in_=rbuf[h][:, k, :], in_offset=None)
                        last.then_inc(s_sc[h], 16)
            for h in range(RING):
                pool.wait_ge(s_sc[h], TITERS * U * 16)

        CONSTS = 9

        @block.scalar
        def _(act):
            act.wait_ge(s_off, 1)
            with act.Fori(0, GROUPS) as g:
                e0 = four(nc, ACTIVATION, c.edge0, g * U, E)
                for k in range(U):
                    s = g * U + k
                    act.dma_start(recD[:, ds(s, 1), :].rearrange("p a f -> p (a f)"),
                                  a["edges"][ds(e0[k], P), :]).then_inc(s_rec, 16)
                    act.dma_start(frecD[:, ds(s, 1), :].rearrange("p a f -> p (a f)"),
                                  a["edge_values"][ds(e0[k], P), :]).then_inc(s_frec, 16)
            act.wait_ge(s_rec, 16 * STEPS)
            act.wait_ge(s_frec, 16 * STEPS)

        @block.vector
        def _(dve):
            v = Chain(dve, s_v)
            V = nc.vector
            v.link(V.memset(c.recS[:], 0))
            V.memset(c.recS[:, 0:STEPS, 0:1], NONE).then_inc(s_fill0, 2)
            v.link(V.memset(recD[:, STEPS:, :], 0))
            v.link(V.memset(c.locD[:], float(NONE)))
            v.link(V.memset(c.locS[:], float(NONE)))
            v.link(V.memset(cntp[:], 0.0))
            v.link(V.memset(first[:], 0.0))
            dve.wait_ge(s_in, 48)
            dve.wait_ge(s_const, CONSTS)
            src = srcI[:, :, 0]
            v.link(V.tensor_scalar(tmpI[:], src, 7, None, ALU.logical_shift_right))
            v.link(V.tensor_copy(srcB[:], tmpI[:]))
            v.link(V.tensor_scalar(tmpI[:], src, 127, None, ALU.bitwise_and))
            v.link(V.tensor_copy(srcL[:], tmpI[:]))
            v.link(V.tensor_scalar(tmpI[:, 0:TILES], dstI[:], 7, None, ALU.logical_shift_right))
            v.link(V.tensor_copy(dstB[:], tmpI[:, 0:TILES]))
            for o, t in ((0, dstB[:]), (1, srcB[:, 0:TILES])):
                for b in range(NB):
                    v.link(V.tensor_scalar(junk[:, 0:TILES], t, float(b), None, ALU.is_equal, ALU.add,
                                           accum_out=cntp[:, o, b:b + 1]))
            V.tensor_copy(junk[:, 0:1], cntp[:, 0, 0:1]).then_inc(s_cntp, 1)
            dve.wait_ge(s_cnt, 1)
            v.link(V.tensor_copy(cnt[:].rearrange("p o b -> p (o b)"), ps_cnt[:, 0:64]))
            v.link(V.tensor_scalar(tilesI[:], cnt[:], float(P - 1), None, ALU.add))
            v.link(V.tensor_scalar(tilesI[:], tilesI[:], 7, None, ALU.logical_shift_right))
            v.link(V.tensor_copy(tiles[:], tilesI[:]))
            for o in range(2):
                v.link(V.tensor_tensor_scan(first[:, o, 1:33], c.ones[:, 0:32], tiles[:, o, :], 0.0, ALU.mult, ALU.add))
            v.link(V.scalar_tensor_tensor(shift[:], tiles[:, 0, :], -float(P), cnt[:, 0, :], ALU.mult, ALU.add))
            v.link(V.memset(blk[:], 0.0))
            v.link(V.memset(seven[:], 0.0))
            v.link(V.tensor_scalar(off[:], steps[:], float(P), None, ALU.mult))
            for b in range(1, NB):
                for o in range(2):
                    v.link(V.scalar_tensor_tensor(blk[:, o, :], steps[:], first[:, o, b:b + 1], blk[:, o, :],
                                                  ALU.is_ge, ALU.add))
                v.link(V.tensor_scalar(junk2[:], steps[:], first[:, 0, b:b + 1], shift[:, b - 1:b],
                                       ALU.is_ge, ALU.mult))
                v.link(V.tensor_tensor(off[:], off[:], junk2[:], ALU.add))
            v.link(V.tensor_scalar(off[:], off[:], float(E), None, ALU.min))
            v.link(V.memset(c.edge0[:, STEPS:], E))
            V.tensor_copy(c.edge0[:, 0:STEPS], off[0:1, :]).then_inc(s_off, 1)
            for k in range(1, 4):
                v.link(V.scalar_tensor_tensor(seven[:], blk[:], 7.0 * k, seven[:], ALU.is_ge, ALU.add))
            v.link(V.tensor_scalar(seven[:], seven[:], float(BANK - 7 * AGG), None, ALU.mult))
            v.link(V.scalar_tensor_tensor(seven[:], blk[:], float(AGG), seven[:], ALU.mult, ALU.add))
            for o, t in ((0, c.blkD), (1, c.blkS)):
                v.link(V.memset(t[:], 0))
                v.link(V.tensor_copy(t[:, 0:GROUPS, 0, :], blk[0:1, o, :].rearrange("a (g u) -> a g u", u=U)))
                v.link(V.tensor_copy(t[:, 0:GROUPS, 1, :], seven[0:1, o, :].rearrange("a (g u) -> a g u", u=U)))
            v.link(V.memset(c.prevD[:, 0:1], 0))
            v.link(V.tensor_copy(c.prevD[:, 1:STEPS], blk[0:1, 0, 0:STEPS - 1]))
            dve.sem_inc(s_h1u, RING)
            with dve.Fori(0, TITERS) as i:
                for h in range(RING):
                    at = i * (RING * U) + h * U
                    dve.wait_ge(s_h1u, i * RING + h + 1)
                    V.tensor_tensor(Hb[h][:], bc(c.iota[:, None, 0:NB], [P, U, NB]),
                                    bc(srcB[:, ds(at, U)].unsqueeze(2), [P, U, NB]), ALU.is_equal).then_inc(s_h1, 1)
                    V.tensor_tensor(Hr[h][:], bc(c.iota[:, None, :], [P, U, P]),
                                    bc(srcL[:, ds(at, U)].unsqueeze(2), [P, U, P]), ALU.is_equal).then_inc(s_h1, 1)
            dve.wait_ge(s_base0, 1)
            v.link(V.tensor_copy(junk[:, 0:NB], ps_hist[:, 0:NB]))
            V.tensor_copy(Cc[:], junk[:, 0:NB]).then_inc(s_cs, 1)
            dve.wait_ge(s_base, 1)
            dve.wait_ge(s_cs, 1)
            v.link(V.scalar_tensor_tensor(Cc[:], first[:, 1, 0:NB], float(P), ps_base[:, 0:NB], ALU.mult, ALU.add))

            def front(g, h, row_n):
                at = g * U
                n = g * FRONT
                V.tensor_tensor(Hb[h][:], bc(c.iota[:, None, 0:NB], [P, U, NB]),
                                bc(srcB[:, ds(at, U)].unsqueeze(2), [P, U, NB]), ALU.is_equal).then_inc(s_oh, 1)
                V.tensor_tensor(Hr[h][:], bc(c.iota[:, None, :], [P, U, P]),
                                bc(srcL[:, ds(at, U)].unsqueeze(2), [P, U, P]), ALU.is_equal).then_inc(s_oh, 1)
                dve.wait_ge(s_row[h], row_n)
                V.tensor_scalar(low[:], row[h][:], 127, None, ALU.bitwise_and).then_inc(s_vh, 1)
                dve.wait_ge(s_vh, n + 1)
                V.tensor_scalar(HT[h][:], low[:], c.iota_p[:, 0:1], None, ALU.is_equal).then_inc(s_oh, 1)
                dve.wait_ge(s_oh, (g + 1) * 3)
                V.tensor_tensor(eq[:], row[h][:].rearrange("p (u e) -> p u e", u=U),
                                bc(srcI[:, ds(at, U), 0:1], [P, U, P]), ALU.is_equal).then_inc(s_rowu, 1)
                dve.wait_ge(s_rowu, g + RING + 1)
                V.tensor_tensor(eq[:], eq[:], bc(before[:, None, :], [P, U, P]), ALU.mult).then_inc(s_vh, 1)
                dve.wait_ge(s_vh, n + 2)
                V.tensor_reduce(rank[:, h, :], eq[:], AX.X, ALU.add).then_inc(s_vh, 1)
                dve.wait_ge(s_vh, n + 3)

            def back(g, h, i):
                at = g * U
                ch = Chain(dve, s_vl, g * BACK)
                ch.link(V.tensor_copy(C[:, h, 0, :], Cc[:]))
                dve.wait_ge(s_new, g + 1)
                for k in range(1, U):
                    ch.link(V.tensor_tensor(C[:, h, k, :], C[:, h, k - 1, :], ps_new[h][:, k - 1, :], ALU.add))
                V.tensor_tensor(Cc[:], C[:, h, U - 1, :], ps_new[h][:, U - 1, :], ALU.add).then_inc(s_C, 1)
                dve.wait_ge(s_C, g + 1)
                dve.wait_ge(s_selr, g + 1)
                ch.link(V.tensor_tensor(sel[:], ps_sel[:], Hb[h][:], ALU.mult))
                ch.link(V.tensor_reduce(pos[:], sel[:], AX.X, ALU.add))
                ch.link(V.tensor_tensor(posI[:], pos[:], rank[:, h, :], ALU.add))
                ch.link(V.tensor_scalar(posA[:], posI[:], 127, None, ALU.bitwise_and))
                if not isinstance(i, int):
                    dve.wait_ge(s_sc[h], i * (16 * U))
                ch.link(V.tensor_scalar(posB[:], posI[:], 7, None, ALU.logical_shift_right))
                ch.link(V.tensor_scalar(rbuf[h][:], srcI[:, ds(at, U), :], 1, None, ALU.mult))
                V.scalar_tensor_tensor(idx[h][:], posA[:], STEPS, posB[:], ALU.mult, ALU.add).then_inc(s_idx, 1)
                dve.wait_ge(s_idx, g + 1)
                assert ch.n == BACK

            FRONT, BACK = 3, 10
            dve.sem_inc(s_rowu, RING)
            front(0, 0, 16)

            def sort_groups(i):
                for h in range(RING):
                    front(i * RING + (h + 1), (h + 1) % RING, i * 16 + (16 if h + 1 < RING else 32))
                    back(i * RING + h, h, i)

            sort_groups(0)
            with dve.Fori(1, TITERS) as i:
                sort_groups(i)

        @block.tensor
        def _(pe):
            T = nc.tensor
            pe.wait_ge(s_const, CONSTS)
            pe.wait_ge(s_cchain, 4)
            pe.wait_ge(s_cntp, 1)
            T.matmul(ps_cnt[:, 0:64], c.ones[:], cntp[:].rearrange("p o b -> p (o b)"), start=True, stop=True
                     ).then_inc(s_cnt, 1)
            T.matmul(ps_hist[:], c.zeros[:, 0:P], c.zeros[:], start=True, stop=True)
            with pe.Fori(0, TITERS) as i:
                for h in range(RING):
                    pe.wait_ge(s_h1, (i * RING + h + 1) * 2)
                    for k in range(U):
                        last = T.matmul(ps_hist[:, 0:NB], Hr[h][:, k, :], Hb[h][:, k, :], start=False, stop=True,
                                        skip_group_check=True)
                    last.then_inc(s_h1u, 1)
            pe.wait_ge(s_h1u, TGROUPS + RING)
            pe.sem_inc(s_base0, 1)
            pe.wait_ge(s_cs, 1)
            T.matmul(ps_base[:, 0:NB], after[:], Cc[:], start=True, stop=True).then_inc(s_base, 1)
            with pe.Fori(0, TITERS) as i:
                for h in range(RING):
                    g = i * RING + h
                    pe.wait_ge(s_oh, (g + 1) * 3)
                    for k in range(U):
                        last = T.matmul(ps_new[h][:, k, :], Hr[h][:, k, :], Hb[h][:, k, :], start=True, stop=True)
                    last.then_inc(s_new, 1)
                    pe.wait_ge(s_C, g + 1)
                    for k in range(U):
                        last = T.matmul(ps_sel[:, k, :], HT[h][:, k * P:(k + 1) * P], C[:, h, k, :],
                                        start=True, stop=True)
                    last.then_inc(s_selr, 1)

        banks.close()
        slots(nc, c, blk, prev, nxt, recD, frecD)


def slots(nc, c, blk, prev, nxt, recD, frecD):
    st = ExitStack()
    sb, pb, sem = c.sb, c.pb, c.sem
    with st:
        node = sb("node", [P, 2, STEPS], F32, st)
        key = sb("key", [P, 2, STEPS], F32, st)
        ok = sb("ok", [P, 2, STEPS], F32, st)
        KT = sb("KT", [Q, 2, W + 1], F32, st)
        ps_key = [pb(f"ps_key{o}", [Q, BANK], st) for o in range(2)]
        ps_edge = pb("ps_edge", [Q, 4], st)
        srcs = sb("srcs", [P, STEPS + U], I32, st)
        LT = sb("LT", [Q, W], F32, st)
        ps_loc = pb("ps_loc", [Q, W], st)
        s_loc = sem("k_loc"); s_lt = sem("k_loc_turned"); s_ltc = sem("k_loc_copied")
        s_out = sem("k_out"); s_srcc = sem("k_srcs"); s_rs = sem("k_records"); s_v = sem("k_v"); s_key = sem("k_key"); s_t = sem("k_turned")
        s_c = sem("k_copied"); s_prev = sem("k_prev"); s_pen = sem("k_pen"); s_nxt = sem("k_next")
        block = st.enter_context(nc.Block("slots"))

        @block.sync
        def _(sp):
            sp.dma_start(c.recS[:, 0:STEPS, :].rearrange("p s f -> p (s f)"),
                         c.recS_dram.rearrange("(p s) f -> p (s f)", p=P)).then_inc(s_rs, 16)
            sp.dma_start(c.val_dram, frecD[:].rearrange("p s f -> p (s f)")).then_inc(s_out, 16)
            sp.wait_ge(s_srcc, 1)
            sp.dma_start(c.src_dram, srcs[:]).then_inc(s_out, 16)
            sp.dma_start(c.loc_dram[STEPS * P:].rearrange("(a f) -> a f", a=1), c.zeros[0:1, :]).then_inc(s_out, 16)
            sp.wait_ge(s_ltc, 1)
            sp.dma_start(c.loc_dram[0:STEPS * P].rearrange("(q f) -> q f", q=Q), LT[:]).then_inc(s_out, 16)
            sp.wait_ge(s_out, 64)

        @block.scalar
        def _(act):
            act.wait_ge(s_lt, 1)
            nc.scalar.copy(LT[:], ps_loc[:]).then_inc(s_ltc, 1)

        @block.vector
        def _(dve):
            V = nc.vector
            v = Chain(dve, s_v)
            V.tensor_copy(srcs[:], recD[:, :, 0]).then_inc(s_srcc, 1)
            v.link(V.tensor_copy(node[:, 0, :], recD[:, 0:STEPS, 1]))
            dve.wait_ge(s_rs, 16)
            v.link(V.tensor_copy(node[:, 1, :], c.recS[:, 0:STEPS, 0]))
            for o, loc in ((0, c.locD), (1, c.locS)):
                v.link(V.scalar_tensor_tensor(loc[:, 0:STEPS], blk[:, o, :], -float(P), node[:, o, :], ALU.mult, ALU.add))
                dve.sem_inc(s_loc, 1)
                v.link(V.tensor_scalar(ok[:, o, :], loc[:, 0:STEPS], 0.0, None, ALU.is_ge))
                v.link(V.scalar_tensor_tensor(ok[:, o, :], loc[:, 0:STEPS], float(P - 1), ok[:, o, :], ALU.is_le, ALU.mult))
                V.scalar_tensor_tensor(key[:, o, :], node[:, o, :], 1.0, ok[:, o, :], ALU.add, ALU.mult
                                       ).then_inc(s_key, 1)
            for o, pen in ((0, c.penD), (1, c.penS)):
                dve.wait_ge(s_t, o + 1)
                V.tensor_copy(KT[:, o, 1:W + 1], ps_key[o][:]).then_inc(s_c, 1)
                dve.wait_ge(s_prev, o + 1)
                v.link(V.tensor_copy(KT[:, o, 0:1], ps_edge[:, o:o + 1]))
                v.link(V.tensor_tensor(pen[:, 0:W], KT[:, o, 1:W + 1], KT[:, o, 0:W], ALU.not_equal))
                V.tensor_scalar(pen[:, 0:W], pen[:, 0:W], -BIG, None, ALU.mult).then_inc(s_pen, 1)
                dve.wait_ge(s_nxt, o + 1)
                v.link(V.tensor_copy(pen[:, W:W + 1], ps_edge[:, 2 + o:3 + o]))

        @block.tensor
        def _(pe):
            T = nc.tensor
            pe.wait_ge(s_loc, 1)
            for j in range(4):
                last = T.transpose(ps_loc[:, j * P:(j + 1) * P], c.locD[:, j:STEPS:4], c.ident[:])
            last.then_inc(s_lt, 1)
            for o, pen in ((0, c.penD), (1, c.penS)):
                pe.wait_ge(s_key, o + 1)
                for j in range(4):
                    last = T.transpose(ps_key[o][:, j * P:(j + 1) * P], key[:, o, j:STEPS:4], c.ident[:])
                last.then_inc(s_t, 1)
            for o, pen in ((0, c.penD), (1, c.penS)):
                pe.wait_ge(s_c, o + 1)
                T.matmul(ps_edge[:, o:o + 1], prev[0:Q, 0:Q], KT[:, o, W:W + 1], start=True, stop=True).then_inc(s_prev, 1)
                pe.wait_ge(s_pen, o + 1)
                T.matmul(ps_edge[:, 2 + o:3 + o], nxt[0:Q, 0:Q], pen[:, 0:1], start=True, stop=True).then_inc(s_nxt, 1)


def kernel(**inputs):
    import numpy as np
    import concourse.bacc as bacc
    from concourse.bass_utils import run_bass_kernel_spmd
    src, dst, typ = (np.asarray(inputs[k]) for k in ("src", "dst", "edge_type_64"))
    f = {k: np.asarray(v) for k, v in inputs.items()}
    full = TILES * P - E
    by_p = np.stack([np.pad(src, (0, full), constant_values=NP - 1), np.pad(dst, (0, full)),
                     np.pad(typ, (0, full)), np.zeros(E + full, src.dtype)], 1).reshape(P, TILES, 4)
    arrays = {
        "edges_by_partition": np.pad(by_p, ((0, 0), (0, U), (0, 0))),
        "dst_by_partition": np.pad(dst, (0, full), constant_values=NP - 1).reshape(P, TILES),
        "src_by_tile": np.pad(by_p[:, :, 0].T, ((0, U), (0, 0))).reshape(-1),
        "edges": np.stack([np.pad(v, (0, EPAD - E), constant_values=w)
                           for v, w in ((src, 0), (dst, NONE), (typ, 0), (src, 0))], 1),
        "edge_values": np.pad(np.concatenate([f["edge_weight"][:, None], f["edge_attr_8"]], 1),
                              ((0, EPAD - E), (0, 0))),
        "l0_WT": f["L0_gnn_W"].T,
        "l0_relT": f["L0_gnn_relation_emb"].T,
        "l1_edges": np.pad(f["edge_attr_64"], ((0, EPAD - E), (0, 0))).T,
        **{"l1_" + k: f["L1_gnn_" + k] for k in ("Wk1", "Wk2", "Wk3", "Wv1", "Wv2", "Wv3", "W_logit", "W_out")},
        **{"l2_" + k: f["L2_gnn_" + k] for k in ("W1", "b1", "gamma", "beta", "W2", "b2")},
        **{"l3_WT_" + k: f["L3_gnn_W_" + k].T for k in ("self", "neigh", "var")},
        **{"l3_b_" + k: f["L3_gnn_b_" + k] for k in ("self", "neigh", "var")},
        "x": np.pad(f["x"], ((0, NP - N), (0, 0))),
    }
    nc = bacc.Bacc("TRN2", target_bir_lowering=False, num_devices=1)
    arrays = {k: np.ascontiguousarray(v) for k, v in arrays.items()}
    aps = {k: nc.dram_tensor("in_" + k, v.shape, mybir.dt.from_np(v.dtype), kind="ExternalInput").ap()
           for k, v in arrays.items()}
    out = nc.dram_tensor("out", (NP, D), F32, kind="ExternalOutput").ap()
    program(nc, aps, out)
    r = run_bass_kernel_spmd(nc, [{"in_" + k: v for k, v in arrays.items()}], core_ids=[0])
    return r.results[0]["out"][:N]
```

```python
import concourse.bass as bass
from concourse import mybir
from contextlib import ExitStack

F32 = mybir.dt.float32
I32 = mybir.dt.int32
BF16 = mybir.dt.bfloat16
ALU = mybir.AluOpType
ACT = mybir.ActivationFunctionType
AX = mybir.AxisListType
ds = bass.ds
PE, DVE, ACTIVATION, SP = (mybir.EngineType.PE, mybir.EngineType.DVE, mybir.EngineType.Activation,
                           mybir.EngineType.SP)

N, E, D = 3125, 53125, 64
P = 128
BLOCKS = -(-N // P)
NP = BLOCKS * P
TILES = -(-E // P)
STEPS = TILES + BLOCKS - 1
U = 4
GROUPS = STEPS // U
RING = 2
ITERS = GROUPS // RING
DEEP = 5
TGROUPS = TILES // U
TITERS = TGROUPS // RING
TPAD = TILES + RING * U
Q = 110
W = 4 * P
EPAD = E + P + 123
NONE = 16384
BIG = 1.0e30
AGG = 72
BANK = 512
EPS = 1e-5
F1 = 9 * D
assert STEPS % (U * RING) == 0 and GROUPS % DEEP == 0 and TILES % (U * RING) == 0 and Q * 4 == STEPS


class Kernel:

    def __init__(self, sb, pb, sem, a, out, ctx):
        self.sb, self.pb, self.sem, self.a, self.out, self.ctx = sb, pb, sem, a, out, ctx


class Scratch:

    def __init__(self, s, w):
        self.s, self.w = s, w


class Chain:

    def __init__(self, eng, sem, base=0):
        self.eng, self.sem, self.base, self.n = eng, sem, base, 0

    def inc(self, ins):
        ins.then_inc(self.sem, 1)
        self.n += 1
        return self.base + self.n

    def link(self, ins):
        self.inc(ins)
        self.eng.wait_ge(self.sem, self.base + self.n)


def apart(eng, sem):
    eng.sem_inc(sem, 1)


def bc(ap, shape):
    return ap.broadcast_to(shape)


def some(nc, engine, row, at, n, max_val):
    return nc.values_load_multi_w_load_instructions(
        row[0:1, ds(at, n)], engines=[engine], min_val=0, max_val=max_val,
        skip_runtime_bounds_check_because="the tables are sums of 0 / 1 over the blocks, clamped to the edges")[1]


def blocks_at(nc, engine, blk, g, groups=1):
    return some(nc, engine, blk[:, 0, :], g * U, U * groups, BLOCKS - 1)


def split3(nc, c, name, x):
    parts = c.sb(name + "parts", [P, BLOCKS, 3, D], BF16, c.layer)
    s_v = c.sem(name + "v")
    with nc.sbuf_tensor(name + "rest", [P, BLOCKS, D], F32) as rest, nc.Block(name) as block:
        @block.vector
        def _(dve):
            V = nc.vector
            v = Chain(dve, s_v)
            v.link(V.tensor_copy(parts[:, :, 0, :], x[:]))
            v.link(V.tensor_tensor(rest[:], x[:], parts[:, :, 0, :], ALU.subtract))
            v.link(V.tensor_copy(parts[:, :, 1, :], rest[:]))
            v.link(V.tensor_tensor(parts[:, :, 2, :], rest[:], parts[:, :, 1, :], ALU.subtract))
    return parts


def rows_of_slots(T, out, onehot, parts, blk):
    for j in range(3):
        last = T.matmul(out, onehot, parts[:, ds(blk, 1), j, :].rearrange("p a d -> p (a d)"), start=(j == 0),
                        stop=(j == 2))
    return last


def columns_at(nc, engine, blk, g, groups=1):
    return some(nc, engine, blk[:, 1, :], g * U, U * groups, 4 * BANK - AGG)


def program(nc, a, out):
    with ExitStack() as ctx:
        def sb(name, shape, dt=F32, stack=ctx):
            return stack.enter_context(nc.sbuf_tensor(name, shape, dt))

        def pb(name, shape, stack):
            return stack.enter_context(nc.psum_tensor(name, shape, F32))

        used = []

        def sem(name):
            used.append(nc.alloc_semaphore(name))
            return used[-1]

        def renew():
            nc.all_engine_barrier()
            nc.clear_and_free_semaphores(used)
            nc.all_engine_barrier()
            used.clear()

        c = Kernel(sb=sb, pb=pb, sem=sem, a=a, out=out, ctx=ctx)
        c.s_apart = nc.alloc_semaphore("apart")
        c.iota = sb("iota", [P, P])
        c.iota_p = sb("iota_p", [P, 1])
        c.ident = sb("ident", [P, P])
        c.ones = sb("ones", [P, P])
        c.zeros = sb("zeros", [P, BANK])
        c.recS = sb("recS", [P, STEPS + U, 4], I32)
        c.locD = sb("locD", [P, STEPS + U])
        c.locS = sb("locS", [P, STEPS + U])
        c.penD = sb("penD", [Q, W + 1])
        c.penS = sb("penS", [Q, W + 1])
        c.edge0 = sb("edge0", [1, STEPS + U], I32)
        c.deg = sb("deg", [P, BLOCKS])
        c.tick = sb("tick", [P, 1])
        rows = nc.dram_tensor("rows", (NP, D), F32, kind="Internal").ap()
        c.rows_flat, c.rows = rows, rows.rearrange("(b p) d -> p b d", p=P)
        c.blkD = sb("blkD", [1, 2, STEPS + RING * U], I32)
        c.blkS = sb("blkS", [1, 2, STEPS + RING * U], I32)
        c.prevD = sb("prevD", [1, STEPS], I32)
        c.x = sb("x", [P, BLOCKS, D])
        c.src_dram = nc.dram_tensor("src_dram", (P, STEPS + U), I32, kind="Internal").ap()
        c.loc_dram = nc.dram_tensor("loc_dram", ((STEPS + U) * P,), F32, kind="Internal").ap()
        c.val_dram = nc.dram_tensor("val_dram", (P, STEPS * 9), F32, kind="Internal").ap()
        c.recS_dram = nc.dram_tensor("recS_dram", (P * STEPS, 4), I32, kind="Internal").ap()
        c.table = nc.dram_tensor("table", (NP, 2 * D), F32, kind="Internal").ap()
        prepare(nc, c)
        renew()
        for layer in (layer0, layer1, layer2, layer3):
            layer(nc, c)
            renew()
        finish(nc, c)


def layernorm_relu(v, V, act_root, x, h, t):
    full = [P, BLOCKS, D]
    v.link(V.tensor_reduce(t.s[:], x[:], AX.X, ALU.add))
    v.link(V.tensor_scalar(t.s[:], t.s[:], 1.0 / D, None, ALU.mult))
    v.link(V.tensor_tensor(h[:], x[:], bc(t.s[:].unsqueeze(2), full), ALU.subtract))
    v.link(V.tensor_tensor(t.w[:], h[:], h[:], ALU.mult))
    v.link(V.tensor_reduce(t.s[:], t.w[:], AX.X, ALU.add))
    act_root(V.tensor_scalar(t.s[:], t.s[:], 1.0 / D, EPS, ALU.mult, ALU.add))
    v.link(V.reciprocal(t.s[:], t.s[:]))
    v.link(V.tensor_tensor(h[:], h[:], bc(t.s[:].unsqueeze(2), full), ALU.mult))
    v.link(V.tensor_scalar(h[:], h[:], 0.0, None, ALU.max))


def blocks_of(ps, width):
    for j in range(4):
        n = min(7, BLOCKS - 7 * j)
        yield (slice(7 * j, 7 * j + n),
               ps[:, j * BANK:j * BANK + n * AGG].rearrange("p (b f) -> p b f", f=AGG)[:, :, 0:width])


def segment_exp(nc, c, name, L, pen, heads, rows=None):
    st = ExitStack()
    sb, pb, sem = c.sb, c.pb, c.sem
    with st:
        X = sb(name + "X", [Q, heads, W], F32, st)
        F = sb(name + "F", [Q, W], F32, st)
        B = sb(name + "B", [Q, W], F32, st)
        runs = sb(name + "runs", [Q, 2], F32, st)
        rrow = sb(name + "rrow", [1, 2, Q], F32, st)
        erow = sb(name + "erow", [1, 2, Q], F32, st)
        carry = sb(name + "carry", [1, 2, Q + 2], F32, st)
        ccol = sb(name + "ccol", [Q, 2], F32, st)
        ps_x = pb(name + "ps_x", [Q, W], st)
        ps_r = pb(name + "ps_r", [1, 2, Q], st)
        ps_e = pb(name + "ps_e", [1, 2, Q], st)
        ps_c = pb(name + "ps_c", [Q, 2], st)
        ps_b = pb(name + "ps_b", [P, 4, Q], st)
        s_v = sem(name + "v"); s_run = sem(name + "run"); s_rr = sem(name + "rr")
        s_x = sem(name + "x"); s_e = sem(name + "e"); s_er = sem(name + "er"); s_cr = sem(name + "cr")
        s_cc = sem(name + "cc"); s_m = sem(name + "m"); s_ex = sem(name + "ex"); s_b = sem(name + "b")
        s_done = sem(name + "done"); s_in = sem(name + "in")
        block = st.enter_context(nc.Block(name))

        if rows is not None:
            @block.sync
            def _(sp):
                sp.dma_start(X[:], rows).then_inc(s_in, 16)

        @block.vector
        def _(dve):
            V = nc.vector
            if rows is not None:
                dve.wait_ge(s_in, 16)
            v = Chain(dve, s_v)
            v.link(V.tensor_reduce(runs[:, 0:1], pen[:, 0:W], AX.X, ALU.min))
            v.link(V.tensor_reduce(runs[:, 1:2], pen[:, 1:W + 1], AX.X, ALU.min))
            v.link(V.memset(carry[:], -BIG))
            V.tensor_copy(ccol[:], runs[:]).then_inc(s_run, 1)
            dve.wait_ge(s_rr, 1)
            v.link(V.tensor_copy(rrow[:], ps_r[:]))
            for n in range(heads):
                x = X[:, n, :]
                if rows is None:
                    dve.wait_ge(s_x, n + 1)
                    v.link(V.tensor_copy(x, ps_x[:]))
                v.link(V.tensor_tensor_scan(F[:], pen[:, 0:W], x, -BIG, ALU.add, ALU.max))
                v.link(V.tensor_tensor_scan(B[:, ::-1], pen[:, 1:W + 1][:, ::-1], x[:, ::-1], -BIG, ALU.add, ALU.max))
                dve.sem_inc(s_e, 1)
                dve.wait_ge(s_er, n + 1)
                v.link(V.tensor_copy(erow[:], ps_e[:]))
                v.link(V.tensor_tensor_scan(carry[:, 0, 1:Q + 1], rrow[:, 0, :], erow[:, 0, :], -BIG, ALU.add, ALU.max))
                v.link(V.tensor_tensor_scan(carry[:, 1, 1:Q + 1][:, ::-1], rrow[:, 1, :][:, ::-1],
                                            erow[:, 1, :][:, ::-1], -BIG, ALU.add, ALU.max))
                dve.sem_inc(s_cr, 1)
                dve.wait_ge(s_cc, n + 1)
                v.link(V.tensor_copy(ccol[:], ps_c[:]))
                v.link(V.tensor_tensor_scan(F[:], pen[:, 0:W], x, ccol[:, 0:1], ALU.add, ALU.max))
                v.link(V.tensor_tensor_scan(B[:, ::-1], pen[:, 1:W + 1][:, ::-1], x[:, ::-1], ccol[:, 1:2],
                                            ALU.add, ALU.max))
                v.link(V.tensor_tensor(F[:], F[:], B[:], ALU.max))
                V.tensor_tensor(x, x, F[:], ALU.subtract).then_inc(s_m, 1)
                dve.wait_ge(s_b, n + 1)
                V.tensor_copy(L[:, 0:STEPS, n].rearrange("p (q j) -> p j q", j=4), ps_b[:]).then_inc(s_done, 1)
                dve.wait_ge(s_done, n + 1)

        @block.scalar
        def _(act):
            for n in range(heads):
                act.wait_ge(s_m, n + 1)
                nc.scalar.activation(X[:, n, :], X[:, n, :], ACT.Exp).then_inc(s_ex, 1)

        @block.tensor
        def _(pe):
            T = nc.tensor
            pe.wait_ge(s_run, 1)
            for o in range(2):
                last = T.transpose(ps_r[:, o, :], runs[:, o:o + 1], c.ident[0:Q, 0:Q])
            last.then_inc(s_rr, 1)
            for n in range(heads):
                if rows is None:
                    for j in range(4):
                        last = T.transpose(ps_x[:, j * P:(j + 1) * P], L[:, j:STEPS:4, n], c.ident[:])
                    last.then_inc(s_x, 1)
                pe.wait_ge(s_e, n + 1)
                T.transpose(ps_e[:, 0, :], F[:, W - 1:W], c.ident[0:Q, 0:Q])
                T.transpose(ps_e[:, 1, :], B[:, 0:1], c.ident[0:Q, 0:Q]).then_inc(s_er, 1)
                pe.wait_ge(s_cr, n + 1)
                T.transpose(ps_c[:, 0:1], carry[:, 0, 0:Q], c.ident[0:1, 0:1])
                T.transpose(ps_c[:, 1:2], carry[:, 1, 2:Q + 2], c.ident[0:1, 0:1]).then_inc(s_cc, 1)
                pe.wait_ge(s_ex, n + 1)
                for j in range(4):
                    last = T.transpose(ps_b[:, j, :], X[:, n, j * P:(j + 1) * P], c.ident[0:Q, 0:Q])
                last.then_inc(s_b, 1)


def weighted_sums(nc, c, name, order, G, EX, ps, squares=False):
    st = ExitStack()
    sb, sem = c.sb, c.sem
    loc, blk = (c.locD, c.blkD) if order == "dst" else (c.locS, c.blkS)
    F = D + 1 + D * squares
    with st:
        H = [sb(f"{name}H{h}", [P, U, P], BF16, st) for h in range(DEEP)]
        Y = [sb(f"{name}Y{h}", [P, U, F], F32, st) for h in range(DEEP)]
        part = [[sb(f"{name}part{j}{h}", [P, U, F], BF16, st) for h in range(DEEP)] for j in range(3)]
        s_h = sem(name + "h"); s_y = sem(name + "y"); s_e = sem(name + "e"); s_hi = sem(name + "hi")
        s_rest = sem(name + "rest"); s_mid = sem(name + "mid"); s_lo = sem(name + "lo"); s_used = sem(name + "used")
        block = st.enter_context(nc.Block(name))

        @block.vector
        def _(dve):
            V = nc.vector

            def low_part(g, h):
                dve.wait_ge(s_mid, g + 1)
                V.tensor_tensor(part[2][h][:], Y[h][:], part[1][h][:], ALU.subtract).then_inc(s_lo, 1)

            def groups(i):
                for h in range(DEEP):
                    g = i * DEEP + h
                    dve.wait_ge(s_used, g + 1)
                    V.tensor_tensor(H[h][:], bc(c.iota[:, None, :], [P, U, P]),
                                    bc(loc[:, ds(g * U, U)].unsqueeze(2), [P, U, P]), ALU.is_equal).then_inc(s_h, 1)
                    V.tensor_tensor(Y[h][:, :, 0:D], G[:, ds(g * U, U), :], bc(EX[:, ds(g * U, U), :], [P, U, D]),
                                    ALU.mult).then_inc(s_y, 1)
                    if not (isinstance(i, int) and h < 2):
                        low_part(g - 2, (h - 2) % DEEP)

            groups(0)
            with dve.Fori(1, GROUPS // DEEP) as i:
                groups(i)
            for g in range(GROUPS - 2, GROUPS):
                low_part(g, g % DEEP)

        @block.scalar
        def _(act):
            def mid_part(g, h):
                act.wait_ge(s_rest, g + 1)
                nc.scalar.copy(part[1][h][:], Y[h][:]).then_inc(s_mid, 1)

            def groups(i):
                for h in range(DEEP):
                    g = i * DEEP + h
                    act.wait_ge(s_used, g + 1)
                    apart(act, c.s_apart)
                    nc.scalar.copy(Y[h][:, :, D:D + 1], EX[:, ds(g * U, U), :]).then_inc(s_e, 1)
                    if squares:
                        nc.scalar.activation(Y[h][:, :, D + 1:], G[:, ds(g * U, U), :], ACT.Square).then_inc(s_e, 1)
                    act.wait_ge(s_y, g + 1)
                    act.wait_ge(s_e, (g + 1) * (1 + squares))
                    nc.scalar.copy(part[0][h][:], Y[h][:]).then_inc(s_hi, 1)
                    if not (isinstance(i, int) and h == 0):
                        mid_part(g - 1, (h - 1) % DEEP)

            groups(0)
            with act.Fori(1, GROUPS // DEEP) as i:
                groups(i)
            mid_part(GROUPS - 1, (GROUPS - 1) % DEEP)

        @block.gpsimd
        def _(pool):
            with pool.Fori(0, GROUPS // DEEP) as i:
                for h in range(DEEP):
                    pool.wait_ge(s_hi, i * DEEP + h + 1)
                    nc.gpsimd.tensor_tensor(Y[h][:], Y[h][:], part[0][h][:], ALU.subtract).then_inc(s_rest, 1)

        @block.tensor
        def _(pe):
            T = nc.tensor
            for j in range(8 if squares else 4):
                T.matmul(ps[:, j * BANK:(j + 1) * BANK], c.zeros[:, 0:P], c.zeros[:], start=True, stop=True)
            pe.sem_inc(s_used, DEEP)
            with pe.Fori(0, GROUPS // DEEP) as i:
                for h in range(DEEP):
                    g = i * DEEP + h
                    cols = columns_at(nc, PE, blk, g)
                    pe.wait_ge(s_h, g + 1)
                    pe.wait_ge(s_lo, g + 1)
                    for k in range(U):
                        for j in range(3):
                            if squares:
                                T.matmul(ps[:, ds(cols[k] + 4 * BANK, D)], H[h][:, k, :], part[j][h][:, k, D + 1:],
                                         start=False, stop=True, skip_group_check=True)
                            last = T.matmul(ps[:, ds(cols[k], D + 1)], H[h][:, k, :], part[j][h][:, k, 0:D + 1],
                                            start=False, stop=True, skip_group_check=True)
                    last.then_inc(s_used, 1)


def layer0(nc, c):
    sb, pb, sem, a = c.sb, c.pb, c.sem, c.a
    st = ExitStack()
    full = [P, BLOCKS, D]
    with st:
        G = sb("l0G", [P, STEPS, D], F32, st)
        L = sb("l0L", [P, STEPS, 1], F32, st)
        emb = sb("l0emb", full, F32, st)
        res = sb("l0res", full, F32, st)
        T1 = sb("l0T1", full, F32, st)
        RW = sb("l0RW", [D, 2 * D], F32, st)
        typ = sb("l0typ", [P, STEPS], F32, st)
        t = Scratch(s=sb("l0s", [P, BLOCKS], F32, st), w=sb("l0w", full, F32, st))
        WT = sb("l0WT", [D, 2 * D], F32, st)
        relT = sb("l0relT", [D, D], F32, st)

        s_w = sem("l0_weights"); s_v = sem("l0_v"); s_q = sem("l0_var"); s_r = sem("l0_root"); s_rw = sem("l0_rw")
        with nc.psum_tensor("l0ps_rw", [D, 2 * D], F32) as ps_rw, nc.Block("l0_start") as block:
            @block.sync
            def _(sp):
                sp.dma_start(WT[:], a["l0_WT"]).then_inc(s_w, 16)
                sp.dma_start(relT[:], a["l0_relT"]).then_inc(s_w, 16)

            @block.vector
            def _(dve):
                V = nc.vector
                v = Chain(dve, s_v)

                def root(ins):
                    ins.then_inc(s_q, 1)
                    dve.wait_ge(s_r, 1)
                v.link(V.tensor_copy(typ[:], c.recS[:, 0:STEPS, 2]))
                layernorm_relu(v, V, root, c.x, emb, t)
                v.link(V.tensor_copy(res[:], emb[:]))
                dve.wait_ge(s_rw, 1)
                v.link(V.tensor_copy(RW[:], ps_rw[:]))

            @block.scalar
            def _(act):
                act.wait_ge(s_q, 1)
                nc.scalar.activation(t.s[:], t.s[:], ACT.Sqrt).then_inc(s_r, 1)

            @block.tensor
            def _(pe):
                pe.wait_ge(s_w, 32)
                nc.tensor.matmul(ps_rw[:, 0:D], WT[:, 0:D], relT[:], start=True, stop=True)
                nc.tensor.matmul(ps_rw[:, D:2 * D], WT[:, D:2 * D], relT[:], start=True, stop=True).then_inc(s_rw, 1)

        for hop in range(2):
            layer0_tables(nc, c, f"l0t{hop}", emb, T1, RW)
            layer0_logits(nc, c, f"l0a{hop}", G, L, T1, typ)
            segment_exp(nc, c, f"l0e{hop}", L, c.penS, 1)
            with nc.psum_tensor(f"l0ps{hop}", [P, 4 * BANK], F32) as ps:
                weighted_sums(nc, c, f"l0s{hop}", "src", G, L, ps)
                s_v = sem(f"l0u{hop}"); s_q = sem(f"l0q{hop}"); s_r = sem(f"l0r{hop}")
                with nc.sbuf_tensor(f"l0agg{hop}", [P, BLOCKS, D + 1], F32) as agg, nc.Block(f"l0_update{hop}") as block:
                    @block.vector
                    def _(dve):
                        V = nc.vector
                        v = Chain(dve, s_v)
                        for b, view in blocks_of(ps, D + 1):
                            v.link(V.tensor_copy(agg[:, b, :], view))
                        den = agg[:, :, D:D + 1]
                        v.link(V.tensor_scalar(t.s[:].unsqueeze(2), den, 0.0, None, ALU.is_equal))
                        v.link(V.tensor_tensor(t.s[:].unsqueeze(2), den, t.s[:].unsqueeze(2), ALU.add))
                        v.link(V.reciprocal(t.s[:], t.s[:]))
                        v.link(V.tensor_tensor(agg[:, :, 0:D], agg[:, :, 0:D], bc(t.s[:].unsqueeze(2), full), ALU.mult))
                        v.link(V.tensor_tensor(emb[:], emb[:], agg[:, :, 0:D], ALU.add))
                        v.link(V.tensor_tensor(t.w[:], emb[:], emb[:], ALU.mult))
                        v.link(V.tensor_reduce(t.s[:], t.w[:], AX.X, ALU.add))
                        V.tensor_scalar(t.s[:], t.s[:], 1e-30, None, ALU.max).then_inc(s_q, 1)
                        dve.wait_ge(s_r, 1)
                        v.link(V.tensor_scalar(t.s[:], t.s[:], 1e-12, None, ALU.max))
                        v.link(V.reciprocal(t.s[:], t.s[:]))
                        v.link(V.tensor_tensor(emb[:], emb[:], bc(t.s[:].unsqueeze(2), full), ALU.mult))
                        v.link(V.scalar_tensor_tensor(res[:], res[:], 0.5, emb[:], ALU.mult, ALU.add))
                        if hop == 1:
                            v.link(V.tensor_tensor(c.x[:], c.x[:], res[:], ALU.add))

                    @block.scalar
                    def _(act):
                        act.wait_ge(s_q, 1)
                        nc.scalar.activation(t.s[:], t.s[:], ACT.Sqrt).then_inc(s_r, 1)


def layer0_tables(nc, c, name, emb, T1, RW):
    sb, pb, sem = c.sb, c.pb, c.sem
    with ExitStack() as st:
        rows = sb(name + "rows", [P, BLOCKS, 2 * D], F32, st)
        eT = [sb(f"{name}eT{j}", [D, W], F32, st) for j in range(2)]
        ps_t = [pb(f"{name}ps_t{j}", [D, W], st) for j in range(2)]
        ps_m = [pb(f"{name}ps_m{j}", [P, W], st) for j in range(2)]
        s_t = sem(name + "t"); s_c = sem(name + "c"); s_m = sem(name + "m"); s_v = sem(name + "v"); s_o = sem(name + "o")
        groups = [(b, min(4, BLOCKS - b)) for b in range(0, BLOCKS, 4)]
        block = st.enter_context(nc.Block(name))

        @block.tensor
        def _(pe):
            for j, (b, n) in enumerate(groups):
                if j >= 2:
                    pe.wait_ge(s_c, j - 1)
                for k in range(n):
                    last = nc.tensor.transpose(ps_t[j % 2][:, k * P:(k + 1) * P], emb[:, b + k, :], c.ident[:])
                last.then_inc(s_t, 1)
                pe.wait_ge(s_c, j + 1)
                if j >= 2:
                    pe.wait_ge(s_v, 1 + 2 * (j - 1))
                for k in range(n):
                    last = nc.tensor.matmul(ps_m[j % 2][:, k * P:(k + 1) * P], eT[j % 2][:, k * P:(k + 1) * P], RW[:],
                                            start=True, stop=True)
                last.then_inc(s_m, 1)

        @block.scalar
        def _(act):
            for j, (b, n) in enumerate(groups):
                act.wait_ge(s_t, j + 1)
                if j >= 2:
                    act.wait_ge(s_m, j - 1)
                nc.scalar.copy(eT[j % 2][:, 0:n * P], ps_t[j % 2][:, 0:n * P]).then_inc(s_c, 1)

        @block.vector
        def _(dve):
            V = nc.vector
            v = Chain(dve, s_v)
            v.link(V.tensor_copy(rows[:, :, 0:D], emb[:]))
            for j, (b, n) in enumerate(groups):
                dve.wait_ge(s_m, j + 1)
                m = ps_m[j % 2][:, 0:n * P].rearrange("p (b f) -> p b f", f=P)
                v.link(V.tensor_copy(T1[:, b:b + n, :], m[:, :, 0:D]))
                v.link(V.tensor_copy(rows[:, b:b + n, D:], m[:, :, D:]))

        @block.sync
        def _(sp):
            sp.wait_ge(s_v, 1 + 2 * len(groups))
            sp.dma_start(c.table.rearrange("(b p) f -> p b f", p=P), rows[:]).then_inc(s_o, 16)
            sp.wait_ge(s_o, 16)


def layer0_logits(nc, c, name, G, L, T1, typ):
    sb, pb, sem = c.sb, c.pb, c.sem
    with ExitStack() as st:
        R = [sb(f"{name}R{h}", [P, U, 2 * D], F32, st) for h in range(RING)]
        H = [sb(f"{name}H{h}", [P, U, P], F32, st) for h in range(RING)]
        HT = [sb(f"{name}HT{h}", [P, W], F32, st) for h in range(RING)]
        idx = [sb(f"{name}idx{h}", [P, U], I32, st) for h in range(RING)]
        S = sb(name + "S", [P, U, D], F32, st)
        one = sb(name + "one", [P, U, D], F32, st)
        e = sb(name + "e", [P, U], F32, st)
        ps_h = [pb(f"{name}ps_h{h}", [P, W], st) for h in range(RING)]
        ps_s = [pb(f"{name}ps_s{h}", [P, BANK], st)[:, 0:U * D].rearrange("p (u d) -> p u d", u=U) for h in range(RING)]
        s_idx = sem(name + "idx"); s_g = [sem(f"{name}g{h}") for h in range(RING)]
        s_h = sem(name + "h"); s_t = sem(name + "t"); s_tc = sem(name + "tc"); s_s = sem(name + "s")
        s_used = sem(name + "used"); s_keep = sem(name + "keep"); s_v = sem(name + "v")
        block = st.enter_context(nc.Block(name))

        @block.gpsimd
        def _(pool):
            with pool.Fori(0, ITERS) as i:
                for h in range(RING):
                    pool.wait_ge(s_idx, i * RING + h + 1)
                    apart(pool, c.s_apart)
                    for k in range(U):
                        nc.gpsimd.indirect_dma_start(
                            out=R[h][:, k, :], out_offset=None, in_=c.table,
                            in_offset=bass.IndirectOffsetOnAxis(ap=idx[h][:, k:k + 1], axis=0)).then_inc(s_g[h], 16)

        @block.scalar
        def _(act):
            A = nc.scalar

            def indices(g, h):
                act.wait_ge(s_used, g + 1)
                act.wait_ge(s_keep, g + 1)
                apart(act, c.s_apart)
                A.copy(idx[h][:], c.recS[:, ds(g * U, U), 1]).then_inc(s_idx, 1)

            act.sem_inc(s_keep, RING)
            indices(0, 0)
            with act.Fori(0, ITERS) as i:
                for h in range(RING):
                    g = i * RING + h
                    indices(g + 1, (h + 1) % RING)
                    act.wait_ge(s_t, g + 1)
                    A.copy(HT[h][:], ps_h[h][:]).then_inc(s_tc, 1)
                    act.wait_ge(s_g[h], (i + 1) * (16 * U))
                    apart(act, c.s_apart)
                    A.copy(G[:, ds(g * U, U), :], R[h][:, :, 0:D]).then_inc(s_keep, 1)

        @block.vector
        def _(dve):
            V = nc.vector

            def onehot(g, h):
                V.tensor_tensor(H[h][:], bc(c.iota[:, None, :], [P, U, P]),
                                bc(c.locS[:, ds(g * U, U)].unsqueeze(2), [P, U, P]), ALU.is_equal).then_inc(s_h, 1)

            dve.sem_inc(s_used, RING)
            onehot(0, 0)
            with dve.Fori(0, ITERS) as i:
                for h in range(RING):
                    g = i * RING + h
                    onehot(g + 1, (h + 1) % RING)
                    v = Chain(dve, s_v, g * 4)
                    v.link(V.tensor_tensor(one[:], bc(c.iota[:, None, 0:D], [P, U, D]),
                                           bc(typ[:, ds(g * U, U)].unsqueeze(2), [P, U, D]), ALU.is_equal))
                    dve.wait_ge(s_s, g + 1)
                    dve.wait_ge(s_g[h], (i + 1) * (16 * U))
                    V.tensor_tensor(S[:], ps_s[h], R[h][:, :, D:], ALU.add).then_inc(s_used, 1)
                    dve.wait_ge(s_used, g + RING + 1)
                    v.link(V.tensor_tensor(S[:], S[:], one[:], ALU.mult))
                    v.link(V.tensor_reduce(e[:], S[:], AX.X, ALU.add))
                    v.link(V.scalar_tensor_tensor(L[:, ds(g * U, U), 0], e[:], 0.2, e[:], ALU.mult, ALU.max))

        @block.tensor
        def _(pe):
            T = nc.tensor
            with pe.Fori(0, ITERS) as i:
                for h in range(RING):
                    g = i * RING + h
                    pe.wait_ge(s_h, g + 1)
                    for k in range(U):
                        last = T.transpose(ps_h[h][:, k * P:(k + 1) * P], H[h][:, k, :], c.ident[:])
                    last.then_inc(s_t, 1)
                    blk = blocks_at(nc, PE, c.blkS, g)
                    pe.wait_ge(s_tc, g + 1)
                    pe.wait_ge(s_used, g + 1)
                    for k in range(U):
                        last = T.matmul(ps_s[h][:, k, :], HT[h][:, k * P:(k + 1) * P], T1[:, ds(blk[k], 1), :]
                                        .rearrange("p a d -> p (a d)"), start=True, stop=True)
                    last.then_inc(s_s, 1)


def node_linear(nc, c, name, terms, dest, bias, add):
    sb, pb, sem = c.sb, c.pb, c.sem
    n_t = len(terms)
    with ExitStack() as st:
        eT = [sb(f"{name}eT{j}", [D, n_t, W], F32, st) for j in range(2)]
        ps_t = [pb(f"{name}ps_t{j}", [D, W], st) for j in range(2)]
        ps_m = [pb(f"{name}ps_m{j}", [P, BANK], st) for j in range(2)]
        s_t = sem(name + "t"); s_c = sem(name + "c"); s_m = sem(name + "m"); s_v = sem(name + "v")
        groups = [(b, min(4, BLOCKS - b)) for b in range(0, BLOCKS, 4)]
        block = st.enter_context(nc.Block(name))

        @block.tensor
        def _(pe):
            q = 0
            for j, (b, n) in enumerate(groups):
                for X, _ in terms:
                    if q >= 2:
                        pe.wait_ge(s_c, q - 1)
                    for k in range(n):
                        last = nc.tensor.transpose(ps_t[q % 2][:, k * P:(k + 1) * P], X[:, b + k, 0:D], c.ident[:])
                    last.then_inc(s_t, 1)
                    q += 1
                pe.wait_ge(s_c, n_t * (j + 1))
                if j >= 2:
                    pe.wait_ge(s_v, 2 * (j - 1))
                for k in range(n):
                    for i, (_, w) in enumerate(terms):
                        last = nc.tensor.matmul(ps_m[j % 2][:, k * D:(k + 1) * D], eT[j % 2][:, i, k * P:(k + 1) * P],
                                                w[:], start=(i == 0), stop=(i == n_t - 1))
                last.then_inc(s_m, 1)

        @block.scalar
        def _(act):
            q = 0
            for j, (b, n) in enumerate(groups):
                if j >= 2:
                    act.wait_ge(s_m, j - 1)
                for i in range(n_t):
                    act.wait_ge(s_t, q + 1)
                    nc.scalar.copy(eT[j % 2][:, i, 0:n * P], ps_t[q % 2][:, 0:n * P]).then_inc(s_c, 1)
                    q += 1

        @block.vector
        def _(dve):
            V = nc.vector
            v = Chain(dve, s_v)
            for j, (b, n) in enumerate(groups):
                dve.wait_ge(s_m, j + 1)
                m = ps_m[j % 2][:, 0:n * D].rearrange("p (b f) -> p b f", f=D)
                part = dest[:, b:b + n, :]
                if add:
                    v.link(V.tensor_tensor(part, part, m, ALU.add))
                    v.link(V.tensor_tensor(part, part, bc(bias[:, None, :], [P, n, D]), ALU.add))
                else:
                    v.link(V.tensor_tensor(part, m, bc(bias[:, None, :], [P, n, D]), ALU.add))
                    v.link(V.tensor_copy(c.tick[:], c.ones[:, 0:1]))


def norm_and_table(nc, c, name, h, t, scale=None, width=D):
    sem = c.sem
    s_v = sem(name + "v"); s_q = sem(name + "q"); s_r = sem(name + "r"); s_h = sem(name + "h"); s_o = sem(name + "o")
    with nc.Block(name) as block:
        @block.vector
        def _(dve):
            V = nc.vector
            v = Chain(dve, s_v)

            def root(ins):
                ins.then_inc(s_q, 1)
                dve.wait_ge(s_r, 1)
            layernorm_relu(v, V, root, c.x, h, t)
            if scale is not None:
                v.link(V.tensor_tensor(h[:], h[:], bc(scale[:].unsqueeze(2), [P, BLOCKS, D]), ALU.mult))
            V.tensor_copy(c.tick[:], c.ones[:, 0:1]).then_inc(s_h, 1)

        @block.scalar
        def _(act):
            act.wait_ge(s_q, 1)
            nc.scalar.activation(t.s[:], t.s[:], ACT.Sqrt).then_inc(s_r, 1)

        @block.sync
        def _(sp):
            sp.wait_ge(s_h, 1)
            sp.dma_start(c.rows, h[:]).then_inc(s_o, 16)
            sp.wait_ge(s_o, 16)


def layer2(nc, c):
    sb, sem, a = c.sb, c.sem, c.a
    full = [P, BLOCKS, D]
    st = ExitStack()
    with st:
        src = sb("l2src", [P, STEPS + U], I32, st)
        val = sb("l2val", [P, STEPS, 9], F32, st)
        h = sb("l2h", full, F32, st)
        y = sb("l2y", full, F32, st)
        dinv = sb("l2dinv", [P, BLOCKS], F32, st)
        t = Scratch(s=sb("l2s", [P, BLOCKS], F32, st), w=sb("l2w", full, F32, st))
        real = sb("l2real", [P, 1], F32, st)
        Wt = [sb(f"l2W{i}", [D, D], F32, st) for i in range(2)]
        row = sb("l2row", [P, 4, D], F32, st)
        sums = sb("l2sums", [P, D], F32, st)
        mean = sb("l2mean", [P, D], F32, st)
        s_in = sem("l2_in"); s_v = sem("l2_v"); s_q = sem("l2_q"); s_r = sem("l2_r")
        with nc.Block("l2_start") as block:
            @block.sync
            def _(sp):
                sp.dma_start(src[:], c.src_dram).then_inc(s_in, 16)
                sp.dma_start(val[:].rearrange("p s f -> p (s f)"), c.val_dram).then_inc(s_in, 16)
                for i in range(2):
                    sp.dma_start(Wt[i][:], a[f"l2_W{i + 1}"]).then_inc(s_in, 16)
                for i, k in enumerate(("l2_b1", "l2_gamma", "l2_beta", "l2_b2")):
                    sp.dma_start(row[:, i, :], a[k].partition_broadcast(P)).then_inc(s_in, 16)
                sp.wait_ge(s_in, 16 * 8)

            @block.vector
            def _(dve):
                V = nc.vector
                v = Chain(dve, s_v)
                v.link(V.tensor_scalar(t.s[:], c.deg[:], 1.0, None, ALU.add))
                v.link(V.tensor_scalar(dinv[:], t.s[:], 0.0, None, ALU.is_gt))
                V.tensor_scalar(t.s[:], t.s[:], 1e-30, None, ALU.max).then_inc(s_q, 1)
                dve.wait_ge(s_r, 1)
                v.link(V.reciprocal(t.s[:], t.s[:]))
                v.link(V.tensor_tensor(dinv[:], dinv[:], t.s[:], ALU.mult))
                v.link(V.tensor_scalar(real[:], c.iota_p[:], float(N - (BLOCKS - 1) * P), None, ALU.is_lt))

            @block.scalar
            def _(act):
                act.wait_ge(s_q, 1)
                nc.scalar.activation(t.s[:], t.s[:], ACT.Sqrt).then_inc(s_r, 1)

        norm_and_table(nc, c, "l2n", h, t, scale=dinv)
        for conv in range(2):
            n = f"l2c{conv}"
            with nc.psum_tensor(n + "ps", [P, 4 * BANK], F32) as ps:
                gathered_sums(nc, c, n, src, val, ps)
                s_v = sem(n + "v")
                with nc.Block(n + "_node") as block:
                    @block.vector
                    def _(dve):
                        V = nc.vector
                        v = Chain(dve, s_v)
                        for b, view in blocks_of(ps, D):
                            v.link(V.tensor_tensor(y[:, b, :], view, h[:, b, :], ALU.add))
                        v.link(V.tensor_tensor(y[:], y[:], bc(dinv[:].unsqueeze(2), full), ALU.mult))
            if conv == 1:
                node_linear(nc, c, n + "w", [(y, Wt[1])], c.x, row[:, 3, :], True)
                break
            node_linear(nc, c, n + "w", [(y, Wt[0])], h, row[:, 0, :], False)
            s_v = sem("l2b_v"); s_s = sem("l2b_s"); s_m = sem("l2b_m"); s_q = sem("l2b_q"); s_r = sem("l2b_r")
            s_h = sem("l2b_h"); s_o = sem("l2b_o")
            with nc.psum_tensor("l2b_ps", [P, 2, D], F32) as ps, nc.Block("l2_batch_norm") as block:
                @block.vector
                def _(dve):
                    V = nc.vector
                    v = Chain(dve, s_v)
                    edge = h[:, BLOCKS - 1, :]
                    v.link(V.tensor_scalar(edge, edge, real[:, 0:1], None, ALU.mult))
                    V.tensor_reduce(sums[:], h[:].rearrange("p b d -> p d b"), AX.X, ALU.add).then_inc(s_s, 1)
                    dve.wait_ge(s_m, 1)
                    v.link(V.tensor_scalar(mean[:], ps[:, 0, :], 1.0 / N, None, ALU.mult))
                    v.link(V.tensor_tensor(h[:], h[:], bc(mean[:, None, :], full), ALU.subtract))
                    v.link(V.tensor_scalar(edge, edge, real[:, 0:1], None, ALU.mult))
                    v.link(V.tensor_tensor(t.w[:], h[:], h[:], ALU.mult))
                    V.tensor_reduce(sums[:], t.w[:].rearrange("p b d -> p d b"), AX.X, ALU.add).then_inc(s_s, 1)
                    dve.wait_ge(s_m, 2)
                    V.tensor_scalar(mean[:], ps[:, 1, :], 1.0 / N, EPS, ALU.mult, ALU.add).then_inc(s_q, 1)
                    dve.wait_ge(s_r, 1)
                    v.link(V.reciprocal(mean[:], mean[:]))
                    v.link(V.tensor_tensor(mean[:], mean[:], row[:, 1, :], ALU.mult))
                    v.link(V.tensor_tensor(h[:], h[:], bc(mean[:, None, :], full), ALU.mult))
                    v.link(V.tensor_tensor(h[:], h[:], bc(row[:, 2:3, :], full), ALU.add))
                    v.link(V.tensor_scalar(h[:], h[:], 0.0, None, ALU.max))
                    V.tensor_tensor(h[:], h[:], bc(dinv[:].unsqueeze(2), full), ALU.mult).then_inc(s_h, 1)

                @block.scalar
                def _(act):
                    act.wait_ge(s_q, 1)
                    nc.scalar.activation(mean[:], mean[:], ACT.Sqrt).then_inc(s_r, 1)

                @block.tensor
                def _(pe):
                    for j in range(2):
                        pe.wait_ge(s_s, j + 1)
                        nc.tensor.matmul(ps[:, j, :], c.ones[:], sums[:], start=True, stop=True).then_inc(s_m, 1)

                @block.sync
                def _(sp):
                    sp.wait_ge(s_h, 1)
                    sp.dma_start(c.rows, h[:]).then_inc(s_o, 16)
                    sp.wait_ge(s_o, 16)


def gathered_sums(nc, c, name, src, val, ps):
    sb, sem = c.sb, c.sem
    with ExitStack() as st:
        R = [sb(f"{name}R{h}", [P, U, D], F32, st) for h in range(RING)]
        H = [sb(f"{name}H{h}", [P, U, P], F32, st) for h in range(RING)]
        Y = [sb(f"{name}Y{h}", [P, U, D], F32, st) for h in range(RING)]
        idx = [sb(f"{name}idx{h}", [P, U], I32, st) for h in range(RING)]
        s_idx = sem(name + "idx"); s_g = [sem(f"{name}g{h}") for h in range(RING)]
        s_y = sem(name + "y"); s_taken = sem(name + "taken"); s_used = sem(name + "used")
        block = st.enter_context(nc.Block(name))

        @block.gpsimd
        def _(pool):
            gather(nc, c, pool, c.rows_flat, R, idx, s_idx, s_g)

        @block.scalar
        def _(act):
            with act.Fori(0, ITERS) as i:
                for h in range(RING):
                    g = i * RING + h
                    act.wait_ge(s_taken, g + 1)
                    apart(act, c.s_apart)
                    nc.scalar.copy(idx[h][:], src[:, ds(g * U, U)]).then_inc(s_idx, 1)

        @block.vector
        def _(dve):
            V = nc.vector
            dve.sem_inc(s_taken, RING)
            with dve.Fori(0, ITERS) as i:
                for h in range(RING):
                    g = i * RING + h
                    dve.wait_ge(s_used, g + 1)
                    V.tensor_tensor(H[h][:], bc(c.iota[:, None, :], [P, U, P]),
                                    bc(c.locD[:, ds(g * U, U)].unsqueeze(2), [P, U, P]), ALU.is_equal).then_inc(s_y, 1)
                    dve.wait_ge(s_g[h], (i + 1) * (16 * U))
                    V.tensor_tensor(Y[h][:], R[h][:], bc(val[:, ds(g * U, U), 0:1], [P, U, D]),
                                    ALU.mult).then_inc(s_taken, 1)

        @block.tensor
        def _(pe):
            T = nc.tensor
            for j in range(4):
                T.matmul(ps[:, j * BANK:(j + 1) * BANK], c.zeros[:, 0:P], c.zeros[:], start=True, stop=True)
            pe.sem_inc(s_used, RING)
            with pe.Fori(0, ITERS) as i:
                both = columns_at(nc, PE, c.blkD, i * RING, RING)
                for h in range(RING):
                    g = i * RING + h
                    cols = both[h * U:(h + 1) * U]
                    pe.wait_ge(s_y, g + 1)
                    pe.wait_ge(s_taken, g + RING + 1)
                    for k in range(U):
                        last = T.matmul(ps[:, ds(cols[k], D)], H[h][:, k, :], Y[h][:, k, :], start=False, stop=True,
                                        skip_group_check=True)
                    last.then_inc(s_used, 1)


def gather(nc, c, pool, table, R, idx, s_idx, s_g):
    with pool.Fori(0, ITERS) as i:
        for h in range(RING):
            pool.wait_ge(s_idx, i * RING + h + 1)
            apart(pool, c.s_apart)
            for k in range(U):
                nc.gpsimd.indirect_dma_start(
                    out=R[h][:, k, 0:D], out_offset=None, in_=table,
                    in_offset=bass.IndirectOffsetOnAxis(ap=idx[h][:, k:k + 1], axis=0)).then_inc(s_g[h], 16)


def layer3(nc, c):
    sb, sem, a = c.sb, c.sem, c.a
    full = [P, BLOCKS, D]
    st = ExitStack()
    with st:
        src = sb("l3src", [P, STEPS + U], I32, st)
        h = sb("l3h", full, F32, st)
        G = sb("l3G", [P, STEPS, D], F32, st)
        L = sb("l3L", [P, STEPS, 1], F32, st)
        Wt = [sb(f"l3W{i}", [D, D], F32, st) for i in range(3)]
        row = sb("l3row", [P, 3, D], F32, st)
        t = Scratch(s=sb("l3s", [P, BLOCKS], F32, st), w=sb("l3w", full, F32, st))
        mean = sb("l3mean", [P, BLOCKS, D + 1], F32, st)
        agg = sb("l3agg", [P, BLOCKS, D + 1], F32, st)
        s_in = sem("l3_in"); s_v = sem("l3_v")
        with nc.Block("l3_start") as block:
            @block.sync
            def _(sp):
                sp.dma_start(src[:], c.src_dram).then_inc(s_in, 16)
                for i, k in enumerate(("self", "neigh", "var")):
                    sp.dma_start(Wt[i][:], a[f"l3_WT_{k}"]).then_inc(s_in, 16)
                    sp.dma_start(row[:, i, :], a[f"l3_b_{k}"].partition_broadcast(P)).then_inc(s_in, 16)
                sp.wait_ge(s_in, 16 * 7)

            @block.vector
            def _(dve):
                v = Chain(dve, s_v)
                dve.wait_ge(s_in, 16 * 7)
                for i in (1, 2):
                    v.link(nc.vector.tensor_tensor(row[:, 0, :], row[:, 0, :], row[:, i, :], ALU.add))
        norm_and_table(nc, c, "l3n", h, t)
        with ExitStack() as c.layer, nc.psum_tensor("l3ps1", [P, 4 * BANK], F32) as ps:
            parts = split3(nc, c, "l3p", h)
            layer3_logits(nc, c, src, parts, G, L, ps)
            s_v = sem("l3m_v")
            with nc.Block("l3_counts") as block:
                @block.vector
                def _(dve):
                    v = Chain(dve, s_v)
                    for b, view in blocks_of(ps, D + 1):
                        v.link(nc.vector.tensor_copy(mean[:, b, :], view))
        segment_exp(nc, c, "l3e", L, c.penD, 1)
        with nc.psum_tensor("l3ps2", [P, 8 * BANK], F32) as ps:
            weighted_sums(nc, c, "l3s", "dst", G, L, ps, squares=True)
            s_v = sem("l3f_v")
            with nc.Block("l3_node") as block:
                @block.vector
                def _(dve):
                    V = nc.vector
                    v = Chain(dve, s_v)
                    v.link(V.tensor_scalar(t.s[:].unsqueeze(2), mean[:, :, D:D + 1], 1.0, None, ALU.max))
                    v.link(V.reciprocal(t.s[:], t.s[:]))
                    v.link(V.tensor_tensor(mean[:, :, 0:D], mean[:, :, 0:D], bc(t.s[:].unsqueeze(2), full), ALU.mult))
                    for b, view in blocks_of(ps[:, 4 * BANK:], D):
                        v.link(V.tensor_copy(agg[:, b, 0:D], view))
                    v.link(V.tensor_tensor(agg[:, :, 0:D], agg[:, :, 0:D], bc(t.s[:].unsqueeze(2), full), ALU.mult))
                    v.link(V.tensor_tensor(t.w[:], mean[:, :, 0:D], mean[:, :, 0:D], ALU.mult))
                    v.link(V.tensor_tensor(t.w[:], agg[:, :, 0:D], t.w[:], ALU.subtract))
                    for b, view in blocks_of(ps, D + 1):
                        v.link(V.tensor_copy(agg[:, b, :], view))
                    den = agg[:, :, D:D + 1]
                    v.link(V.tensor_scalar(t.s[:].unsqueeze(2), den, 0.0, None, ALU.is_equal))
                    v.link(V.tensor_tensor(t.s[:].unsqueeze(2), den, t.s[:].unsqueeze(2), ALU.add))
                    v.link(V.reciprocal(t.s[:], t.s[:]))
                    v.link(V.tensor_tensor(agg[:, :, 0:D], agg[:, :, 0:D], bc(t.s[:].unsqueeze(2), full), ALU.mult))
        node_linear(nc, c, "l3w", [(h, Wt[0]), (agg, Wt[1]), (t.w, Wt[2])], c.x, row[:, 0, :], True)


def layer3_logits(nc, c, src, x, G, L, ps):
    sb, pb, sem = c.sb, c.pb, c.sem
    name = "l3a"
    with ExitStack() as st:
        R = [sb(f"{name}R{h}", [P, U, D + 1], F32, st) for h in range(RING)]
        H = [sb(f"{name}H{h}", [P, U, P], F32, st) for h in range(RING)]
        HT = [sb(f"{name}HT{h}", [P, W], BF16, st) for h in range(RING)]
        loc = [sb(f"{name}loc{h}", [P, W], F32, st) for h in range(RING)]
        idx = [sb(f"{name}idx{h}", [P, U], I32, st) for h in range(RING)]
        S = sb(name + "S", [P, U, D], F32, st)
        e = sb(name + "e", [P, U], F32, st)
        ps_q = [pb(f"{name}ps_q{h}", [P, BANK], st)[:, 0:U * D].rearrange("p (u d) -> p u d", u=U) for h in range(RING)]
        s_idx = sem(name + "idx"); s_g = [sem(f"{name}g{h}") for h in range(RING)]
        s_loc = [sem(f"{name}loc{h}") for h in range(RING)]
        s_h = sem(name + "h"); s_ht = sem(name + "ht"); s_q = sem(name + "q")
        s_used = sem(name + "used"); s_keep = sem(name + "keep"); s_v = sem(name + "v"); s_sum = sem(name + "sum")
        s_one = sem(name + "one")
        block = st.enter_context(nc.Block(name))

        @block.gpsimd
        def _(pool):
            gather(nc, c, pool, c.rows_flat, R, idx, s_idx, s_g)

        @block.sync
        def _(sp):
            def node_rows(g, h):
                sp.wait_ge(s_ht, g + 1)
                sp.dma_start(loc[h][:], c.loc_dram[ds(g * W, W)].partition_broadcast(P)).then_inc(s_loc[h], 16)

            node_rows(0, 0)
            with sp.Fori(0, ITERS) as i:
                for h in range(RING):
                    node_rows(i * RING + (h + 1), (h + 1) % RING)
            sp.wait_ge(s_loc[0], 16 * (ITERS + 1))

        @block.scalar
        def _(act):
            A = nc.scalar

            def indices(g, h):
                act.wait_ge(s_used, g + 1)
                act.wait_ge(s_keep, g + 1)
                act.wait_ge(s_sum, g + 1)
                apart(act, c.s_apart)
                A.copy(idx[h][:], src[:, ds(g * U, U)]).then_inc(s_idx, 1)

            act.sem_inc(s_keep, RING)
            indices(0, 0)
            with act.Fori(0, ITERS) as i:
                for h in range(RING):
                    g = i * RING + h
                    indices(g + 1, (h + 1) % RING)
                    act.wait_ge(s_g[h], (i + 1) * (16 * U))
                    apart(act, c.s_apart)
                    A.copy(G[:, ds(g * U, U), :], R[h][:, :, 0:D]).then_inc(s_keep, 1)

        @block.vector
        def _(dve):
            V = nc.vector

            def onehot(g, h):
                V.tensor_tensor(H[h][:], bc(c.iota[:, None, :], [P, U, P]),
                                bc(c.locD[:, ds(g * U, U)].unsqueeze(2), [P, U, P]), ALU.is_equal).then_inc(s_h, 1)

            def turned_onehot(h, loads):
                dve.wait_ge(s_loc[h], loads * 16)
                V.tensor_scalar(HT[h][:], loc[h][:], c.iota_p[:, 0:1], None, ALU.is_equal).then_inc(s_ht, 1)

            for h in range(RING):
                V.memset(R[h][:, :, D:D + 1], 1.0).then_inc(s_one, 1)
            dve.sem_inc(s_used, RING)
            dve.sem_inc(s_ht, RING)
            turned_onehot(0, 1)
            onehot(0, 0)
            def groups(i):
                for h in range(RING):
                    g = i * RING + h
                    if not (isinstance(i, int) and h == 0):
                        dve.wait_ge(s_q, g)
                    turned_onehot((h + 1) % RING, i + 1 + (h + 1) // RING)
                    v = Chain(dve, s_v, g * 2)
                    dve.wait_ge(s_q, g + 1)
                    dve.wait_ge(s_g[h], (i + 1) * (16 * U))
                    V.tensor_tensor(S[:], ps_q[h], R[h][:, :, 0:D], ALU.mult).then_inc(s_used, 1)
                    dve.wait_ge(s_used, g + RING + 1)
                    v.link(V.tensor_reduce(e[:], S[:], AX.X, ALU.add))
                    v.link(V.tensor_scalar(L[:, ds(g * U, U), 0], e[:], D ** -0.5, None, ALU.mult))
                    dve.wait_ge(s_sum, g + RING)
                    onehot(g + 1, (h + 1) % RING)

            groups(0)
            with dve.Fori(1, ITERS) as i:
                groups(i)

        @block.tensor
        def _(pe):
            T = nc.tensor
            for j in range(4):
                T.matmul(ps[:, j * BANK:(j + 1) * BANK], c.zeros[:, 0:P], c.zeros[:], start=True, stop=True)
            pe.wait_ge(s_one, RING)
            pe.sem_inc(s_sum, RING)

            def dst_rows(g, h, blk):
                pe.wait_ge(s_ht, g + RING + 1)
                pe.wait_ge(s_used, g + 1)
                for k in range(U):
                    last = rows_of_slots(T, ps_q[h][:, k, :], HT[h][:, k * P:(k + 1) * P], x, blk[k])
                last.then_inc(s_q, 1)

            dst_rows(0, 0, blocks_at(nc, PE, c.blkD, 0))
            with pe.Fori(0, ITERS) as i:
                for h in range(RING):
                    g = i * RING + h
                    dst_rows(g + 1, (h + 1) % RING, blocks_at(nc, PE, c.blkD, g + 1))
                    cols = columns_at(nc, PE, c.blkD, g)
                    pe.wait_ge(s_h, g + 1)
                    pe.wait_ge(s_g[h], (i + 1) * (16 * U))
                    for k in range(U):
                        last = T.matmul(ps[:, ds(cols[k], D + 1)], H[h][:, k, :], R[h][:, k, :], start=False, stop=True,
                                        skip_group_check=True)
                    last.then_inc(s_sum, 1)


HEADS = 4
HEAD_D = [(max(0, (F1 // HEADS * n - D) // 8), (F1 // HEADS * (n + 1) - D) // 8) for n in range(HEADS)]
OUTER = 8 * D


def layer1(nc, c):
    sb, sem, a = c.sb, c.sem, c.a
    full = [P, BLOCKS, D]
    G = nc.dram_tensor("l1_G", (P, STEPS * D), F32, kind="Internal").ap()
    logits = nc.dram_tensor("l1_logits", (HEADS, Q * W), F32, kind="Internal").ap()
    hidden = nc.dram_tensor("l1_hidden", (D, STEPS * P), F32, kind="Internal").ap()
    st = ExitStack()
    with st:
        src = sb("l1src", [P, STEPS + U], I32, st)
        val = sb("l1val", [P, STEPS, 9], F32, st)
        L = sb("l1L", [P, STEPS, HEADS], F32, st)
        WE = sb("l1WE", [P, STEPS, HEADS + 1], F32, st)
        W1 = sb("l1W1", [D, P], F32, st)
        W2 = sb("l1W2", [P, P], F32, st)
        K3, V3 = (sb(f"l1{k}", [D, F1], F32, st) for k in ("K3", "V3"))
        Wl = sb("l1Wl", [P, HEADS], F32, st)
        s_in = sem("l1_in"); s_w2 = sem("l1_w2")
        with nc.Block("l1_start") as block:
            @block.sync
            def _(sp):
                sp.dma_start(src[:], c.src_dram).then_inc(s_in, 16)
                sp.dma_start(val[:].rearrange("p s f -> p (s f)"), c.val_dram).then_inc(s_in, 16)
                sp.wait_ge(s_w2, 1)
                for t_, k in ((W1[:, 0:D], "Wk1"), (W2[0:D, 0:D], "Wk2"), (K3[:], "Wk3"), (W1[:, D:P], "Wv1"),
                              (W2[D:P, D:P], "Wv2"), (V3[:], "Wv3"), (Wl[:], "W_logit")):
                    sp.dma_start(t_, a["l1_" + k]).then_inc(s_in, 16)
                sp.wait_ge(s_in, 16 * 9)

            @block.vector
            def _(dve):
                nc.vector.memset(W2[:], 0.0).then_inc(s_w2, 1)

        with ExitStack() as keys:
            h = sb("l1h", full, F32, keys)
            sh2 = sb("l1sh2", [P, STEPS, 8], F32, keys)
            t = Scratch(s=sb("l1s", [P, BLOCKS], F32, keys), w=sb("l1w", full, F32, keys))
            norm_and_table(nc, c, "l1n", h, t)
            with nc.Block("l1_squares") as block:
                @block.vector
                def _(dve):
                    nc.vector.tensor_tensor(sh2[:], val[:, :, 1:9], val[:, :, 1:9], ALU.mult)
            c.layer = keys
            parts = split3(nc, c, "l1p", h)
            layer1_logits(nc, c, src, parts, sh2, logits, G, hidden, W1, W2, K3, Wl)
        segment_exp(nc, c, "l1e", L, c.penD, HEADS, logits.rearrange("n (q f) -> q n f", q=Q))
        s_v = sem("l1w_v"); s_q = sem("l1w_q"); s_r = sem("l1w_r")
        with nc.sbuf_tensor("l1pos", [P, STEPS, HEADS], F32) as pos, nc.Block("l1_weights") as block:
            @block.vector
            def _(dve):
                V = nc.vector
                v = Chain(dve, s_v)
                v.link(V.tensor_tensor(WE[:, :, 0:HEADS], L[:], bc(val[:, :, 0:1], [P, STEPS, HEADS]), ALU.mult))
                v.link(V.tensor_copy(WE[:, :, HEADS:HEADS + 1], val[:, :, 0:1]))
                v.link(V.tensor_scalar(pos[:], WE[:, :, 0:HEADS], 0.0, None, ALU.is_gt))
                V.tensor_scalar(L[:], WE[:, :, 0:HEADS], 1e-34, None, ALU.max).then_inc(s_q, 1)
                dve.wait_ge(s_r, 1)
                v.link(V.tensor_tensor(L[:], L[:], pos[:], ALU.mult))

            @block.scalar
            def _(act):
                act.wait_ge(s_q, 1)
                nc.scalar.activation(L[:], L[:], ACT.Sqrt).then_inc(s_r, 1)

        acc = sb("l1acc", [P, BLOCKS, F1 + HEADS + 1], F32, st)
        layer1_values(nc, c, val, L, WE, G, hidden, V3, acc)
        layer1_output(nc, c, acc)


def layer1_logits(nc, c, src, x, sh2, logits, G, hidden, W1, W2, K3, Wl):
    sb, pb, sem, a = c.sb, c.pb, c.sem, c.a
    name = "l1a"
    with ExitStack() as st:
        R = [sb(f"{name}R{h}", [P, U, D], F32, st) for h in range(RING)]
        loc = [sb(f"{name}loc{h}", [P, W], F32, st) for h in range(RING)]
        HT = [sb(f"{name}HT{h}", [P, W], BF16, st) for h in range(RING)]
        idx = [sb(f"{name}idx{h}", [P, U], I32, st) for h in range(RING)]
        ea = [sb(f"{name}ea{h}", [D, W], F32, st) for h in range(RING)]
        g1 = sb(name + "g1", [P, W], F32, st)
        g2 = [sb(f"{name}g2{h}", [P, W], F32, st) for h in range(RING)]
        z = [sb(f"{name}z{h}", [P, U, D], F32, st) for h in range(RING)]
        m = [sb(f"{name}m{j}", [P, D, 8], F32, st) for j in range(2)]
        scal = [sb(f"{name}scal{h}", [P, U, P], F32, st) for h in range(RING)]
        k1 = [sb(f"{name}k1{h}", [P, U, D], F32, st) for h in range(RING)]
        scT = sb(name + "scT", [P, W], F32, st)
        lrow = [sb(f"{name}lrow{h}", [HEADS, W], F32, st) for h in range(RING)]
        ps_m = pb(name + "ps_m", [P, W], st)
        ps_q = pb(name + "ps_q", [P, BANK], st)[:, 0:U * D].rearrange("p (u d) -> p u d", u=U)
        ps_d = [pb(f"{name}ps_d{j}", [P, OUTER], st) for j in range(2)]
        ps_0 = pb(name + "ps_0", [P, BANK], st)[:, 0:U * D].rearrange("p (u d) -> p u d", u=U)
        ps_s = pb(name + "ps_s", [P, W], st)
        ps_l = pb(name + "ps_l", [HEADS, W], st)
        s_idx = sem(name + "idx"); s_g = [sem(f"{name}g{h}") for h in range(RING)]
        s_G = [sem(f"{name}G{h}") for h in range(RING)]; s_ea = [sem(f"{name}ea{h}") for h in range(RING)]
        s_loc = [sem(f"{name}loc{h}") for h in range(RING)]
        s_h = sem(name + "h"); s_q = sem(name + "q")
        s_z = sem(name + "z"); s_m1 = sem(name + "m1"); s_m2 = sem(name + "m2"); s_a1 = sem(name + "a1")
        s_a2 = sem(name + "a2"); s_k = sem(name + "k"); s_0 = sem(name + "0"); s_d = sem(name + "d"); s_v = sem(name + "v")
        s_scal0 = sem(name + "scal0"); s_scal = sem(name + "scal"); s_st = sem(name + "st")
        s_stc = sem(name + "stc"); s_l = sem(name + "l")
        s_L = sem(name + "L"); s_Ld = [sem(f"{name}Ld{h}") for h in range(RING)]; s_hid = [sem(f"{name}hid{h}") for h in range(RING)]
        block = st.enter_context(nc.Block(name))

        @block.gpsimd
        def _(pool):
            Gp = nc.gpsimd

            def onehot(g, h, loads):
                pool.wait_ge(s_loc[h], loads * 16)
                apart(pool, c.s_apart)
                Gp.tensor_scalar(HT[h][:], loc[h][:], c.iota_p[:, 0:1], None, ALU.is_equal).then_inc(s_h, 1)

            def rows(g, h):
                pool.wait_ge(s_idx, g + 1)
                apart(pool, c.s_apart)
                for k in range(U):
                    Gp.indirect_dma_start(
                        out=R[h][:, k, :], out_offset=None, in_=c.rows_flat,
                        in_offset=bass.IndirectOffsetOnAxis(ap=idx[h][:, k:k + 1], axis=0)).then_inc(s_g[h], 16)

            def groups(i):
                for h in range(RING):
                    g = i * RING + h
                    if not (isinstance(i, int) and h == 0):
                        pool.wait_ge(s_q, g)
                    onehot(g + 1, (h + 1) % RING, i + 1 + (h + 1) // RING)
                    rows(g + 1, (h + 1) % RING)
                    if not isinstance(i, int):
                        pool.wait_ge(s_st, g - 1)
                    pool.wait_ge(s_scal0, g + 1)
                    pool.wait_ge(s_v, (g + 1) * U)
                    Gp.tensor_tensor(scal[h][:, :, D:P], z[h][:], k1[h][:], ALU.mult).then_inc(s_scal, 1)

            onehot(0, 0, 1)
            rows(0, 0)
            groups(0)
            with pool.Fori(1, ITERS) as i:
                groups(i)
            pool.wait_ge(s_g[0], (ITERS + 1) * (16 * U))

        @block.sync
        def _(sp):
            def edges(g, h):
                sp.wait_ge(s_m1, g + 1)
                e0 = some(nc, SP, c.edge0, g * U, U, E)
                for k in range(U):
                    sp.dma_start(ea[h][:, k * P:(k + 1) * P], a["l1_edges"][:, ds(e0[k], P)]).then_inc(s_ea[h], 16)
                sp.wait_ge(s_h, g + 1)
                sp.dma_start(loc[h][:], c.loc_dram[ds(g * W, W)].partition_broadcast(P)).then_inc(s_loc[h], 16)

            def store_logits(g, h):
                sp.wait_ge(s_L, g + 1)
                sp.dma_start(logits[:, ds(g * W, W)], lrow[h][:]).then_inc(s_Ld[h], 16)

            def groups(i):
                for h in range(RING):
                    g = i * RING + h
                    edges(g + 1, (h + 1) % RING)
                    if not isinstance(i, int):
                        store_logits(g - RING, h)
                    sp.wait_ge(s_g[h], (i + 1) * (16 * U))
                    sp.dma_start(G[:, ds(g * (U * D), U * D)], R[h][:].rearrange("p u d -> p (u d)")
                                 ).then_inc(s_G[h], 16)
                    sp.wait_ge(s_a2, g + 1)
                    sp.dma_start(hidden[:, ds(g * W, W)], g2[h][D:P, :]).then_inc(s_hid[h], 16)

            edges(0, 0)
            groups(0)
            with sp.Fori(1, ITERS) as i:
                groups(i)
            for h in range(RING):
                store_logits(GROUPS - RING + h, h)
            for h in range(RING):
                sp.wait_ge(s_Ld[h], 16 * ITERS)
                sp.wait_ge(s_G[h], 16 * ITERS)
                sp.wait_ge(s_hid[h], 16 * ITERS)
            sp.wait_ge(s_ea[0], 16 * U * (ITERS + 1))
            sp.wait_ge(s_loc[0], 16 * (ITERS + 1))

        @block.scalar
        def _(act):
            A = nc.scalar

            def groups(i):
                for h in range(RING):
                    g = i * RING + h
                    start = isinstance(i, int) and g == 0
                    act.wait_ge(s_z, g + RING)
                    if not start:
                        act.wait_ge(s_G[(h + 1) % RING], (i + h) * 16)
                    apart(act, c.s_apart)
                    A.copy(idx[(h + 1) % RING][:], src[:, ds((g + 1) * U, U)]).then_inc(s_idx, 1)
                    act.wait_ge(s_m1, g + RING + 2)
                    A.activation(g1[:], ps_m[:], ACT.Gelu_apprx_tanh).then_inc(s_a1, 1)
                    if not start:
                        act.wait_ge(s_st, g)
                        A.copy(scT[:], ps_s[:]).then_inc(s_stc, 1)
                        act.wait_ge(s_hid[(h + 1) % RING], (i + h) * 16)
                        apart(act, c.s_apart)
                    act.wait_ge(s_m2, g + 2)
                    A.activation(g2[(h + 1) % RING][:], ps_m[:], ACT.Gelu_apprx_tanh).then_inc(s_a2, 1)
                    if not start:
                        keep_logits(g - 1, (h + 1) % RING, i + h - 1)

            def keep_logits(g, h, stored):
                if not isinstance(stored, int) or stored > 0:
                    act.wait_ge(s_Ld[h], stored * 16)
                    apart(act, c.s_apart)
                act.wait_ge(s_l, g + 1)
                A.copy(lrow[h][:], ps_l[:]).then_inc(s_L, 1)

            A.copy(idx[0][:], src[:, 0:U]).then_inc(s_idx, 1)
            act.wait_ge(s_m1, RING + 1)
            A.activation(g1[:], ps_m[:], ACT.Gelu_apprx_tanh).then_inc(s_a1, 1)
            act.wait_ge(s_m2, 1)
            A.activation(g2[0][:], ps_m[:], ACT.Gelu_apprx_tanh).then_inc(s_a2, 1)
            groups(0)
            groups(1)
            with act.Fori(2, ITERS) as i:
                groups(i)
            act.wait_ge(s_st, GROUPS)
            A.copy(scT[:], ps_s[:]).then_inc(s_stc, 1)
            keep_logits(GROUPS - 1, 1, ITERS - 1)

        @block.vector
        def _(dve):
            V = nc.vector

            def groups(i):
                for h in range(RING):
                    g = i * RING + h
                    dve.wait_ge(s_q, g + 1)
                    dve.wait_ge(s_g[h], (i + 1) * (16 * U))
                    if not isinstance(i, int):
                        dve.wait_ge(s_scal, g - 1)
                        dve.wait_ge(s_st, g - 1)
                    V.tensor_tensor(z[h][:], ps_q, R[h][:], ALU.mult).then_inc(s_z, 1)
                    dve.wait_ge(s_z, g + RING + 1)
                    dve.wait_ge(s_0, g + 1)
                    V.tensor_tensor(scal[h][:, :, 0:D], z[h][:], ps_0, ALU.mult).then_inc(s_scal0, 1)
                    for k in range(U + 1):
                        s = g * U + k
                        if k < U:
                            dve.wait_ge(s_k, s + 1)
                            if not (isinstance(i, int) and h == 0 and k < 2):
                                dve.wait_ge(s_v, s - 1)
                            V.tensor_tensor(m[k % 2][:], ps_d[k % 2][:].rearrange("p (d s) -> p d s", s=8),
                                            bc(sh2[:, ds(s, 1), :], [P, D, 8]), ALU.mult).then_inc(s_d, 1)
                        if k:
                            dve.wait_ge(s_d, s + 2)
                            V.tensor_reduce(k1[h][:, k - 1, :], m[(k - 1) % 2][:], AX.X, ALU.add).then_inc(s_v, 1)

            dve.sem_inc(s_z, RING)
            dve.sem_inc(s_d, 2)
            groups(0)
            with dve.Fori(1, ITERS) as i:
                groups(i)

        @block.tensor
        def _(pe):
            T = nc.tensor

            def first_layer(h, loads):
                pe.wait_ge(s_ea[h], loads * (16 * U))
                T.matmul(ps_m[:], W1[:], ea[h][:], start=True, stop=True).then_inc(s_m1, 1)

            def second_layer(g):
                pe.wait_ge(s_a1, g + 1)
                T.matmul(ps_m[:], W2[:], g1[:], start=True, stop=True).then_inc(s_m2, 1)

            def dst_rows(g, h, blk):
                pe.wait_ge(s_h, g + RING + 1)
                pe.wait_ge(s_z, g + RING)
                for k in range(U):
                    last = rows_of_slots(T, ps_q[:, k, :], HT[h][:, k * P:(k + 1) * P], x, blk[k])
                last.then_inc(s_q, 1)

            def plain_channels(g, h, read):
                pe.wait_ge(s_a2, g + 1)
                if read:
                    pe.wait_ge(s_scal0, g)
                for k in range(U):
                    last = T.matmul(ps_0[:, k, :], g2[h][0:D, k * P:(k + 1) * P], K3[:, 0:D], start=True, stop=True)
                last.then_inc(s_0, 1)

            def channels(s, k, h):
                pe.wait_ge(s_d, s + 1)
                T.matmul(ps_d[k % 2][:], g2[h][0:D, k * P:(k + 1) * P], K3[:, D:F1], start=True, stop=True
                         ).then_inc(s_k, 1)

            def turn(g, h):
                pe.wait_ge(s_scal, g + 1)
                for k in range(U):
                    last = T.transpose(ps_s[:, k * P:(k + 1) * P], scal[h][:, k, :], c.ident[:])
                last.then_inc(s_st, 1)

            def project(g, read):
                pe.wait_ge(s_stc, g + 1)
                if read:
                    pe.wait_ge(s_L, g)
                T.matmul(ps_l[:], Wl[:], scT[:], start=True, stop=True).then_inc(s_l, 1)

            def groups(i):
                for h in range(RING):
                    g = i * RING + h
                    after_first = not (isinstance(i, int) and h == 0)
                    hn = (h + 1) % RING
                    channels(g * U, 0, h)
                    if h == 0:
                        blk = blocks_at(nc, PE, c.blkD, g + 1, RING)
                    first_layer(hn, i + 1 + (h + 1) // RING)
                    channels(g * U + 1, 1, h)
                    if after_first:
                        turn(g - 1, hn)
                    second_layer(g + 1)
                    channels(g * U + 2, 2, h)
                    dst_rows(g + 1, hn, blk[h * U:(h + 1) * U])
                    channels(g * U + 3, 3, h)
                    if after_first:
                        project(g - 1, not (isinstance(i, int) and h == 1))
                    plain_channels(g + 1, hn, True)

            pe.sem_inc(s_m1, RING)
            pe.sem_inc(s_h, RING)
            first_layer(0, 1)
            second_layer(0)
            dst_rows(0, 0, blocks_at(nc, PE, c.blkD, 0))
            plain_channels(0, 0, False)
            groups(0)
            with pe.Fori(1, ITERS) as i:
                groups(i)
            turn(GROUPS - 1, 1)
            project(GROUPS - 1, True)


def layer1_values(nc, c, val, A, WE, G, hidden, V3, acc):
    sb, pb, sem, a = c.sb, c.pb, c.sem, c.a
    name = "l1v"
    M = D + HEADS + 1
    with ExitStack() as st:
        R = [sb(f"{name}R{h}", [P, U, D], F32, st) for h in range(RING)]
        H = [sb(f"{name}H{h}", [P, U, P], F32, st) for h in range(RING)]
        g2 = [sb(f"{name}g2{h}", [D, W], F32, st) for h in range(RING)]
        xa = [sb(f"{name}xa{h}", [P, U, D], F32, st) for h in range(RING)]
        xs = [sb(f"{name}xs{k}", [P, D, 8], F32, st) for k in range(U)]
        x0 = [sb(f"{name}x0{h}", [P, U, D], F32, st) for h in range(RING)]
        Yd = [sb(f"{name}Yd{k}", [P, D, 8], F32, st) for k in range(U)]
        Y0 = [sb(f"{name}Y0{h}", [P, U, M], F32, st) for h in range(RING)]
        ps_d = [pb(f"{name}ps_d{j}", [P, OUTER], st) for j in range(2)]
        ps_0 = pb(name + "ps_0", [P, BANK], st)[:, 0:U * D].rearrange("p (u d) -> p u d", u=U)
        ps_sd = [pb(f"{name}ps_sd{j}", [P, OUTER], st) for j in range(2)]
        ps_s0 = [pb(f"{name}ps_s0{j}", [P, BANK], st)[:, 0:M] for j in range(2)]
        s_R = [sem(f"{name}R{h}") for h in range(RING)]; s_g2 = [sem(f"{name}g2{h}") for h in range(RING)]
        s_h = sem(name + "h"); s_k = sem(name + "k"); s_0 = sem(name + "0"); s_v = sem(name + "v")
        s_y0 = sem(name + "y0"); s_d = sem(name + "d"); s_seg = sem(name + "seg")
        s_acc = sem(name + "acc"); s_x = sem(name + "x"); s_z = sem(name + "z"); s_xs = sem(name + "xs")
        block = st.enter_context(nc.Block(name))

        @block.gpsimd
        def _(pool):
            pool.sem_inc(s_x, RING)
            with pool.Fori(0, ITERS) as i:
                for h in range(RING):
                    g = i * RING + h
                    at = g * U
                    pool.wait_ge(s_R[h], (i + 1) * 16)
                    pool.wait_ge(s_y0, g * 2 + 2)
                    for n, (d0, d1) in enumerate(HEAD_D):
                        nc.gpsimd.tensor_tensor(xa[h][:, :, d0:d1], R[h][:, :, d0:d1],
                                                bc(A[:, ds(at, U), n:n + 1], [P, U, d1 - d0]), ALU.mult).then_inc(s_v, 1)
                    nc.gpsimd.tensor_tensor(x0[h][:], R[h][:], bc(A[:, ds(at, U), 0:1], [P, U, D]),
                                            ALU.mult).then_inc(s_x, 1)
                    pool.wait_ge(s_v, (g + 1) * HEADS)
                    for k in range(U):
                        s = at + k
                        pool.wait_ge(s_d, s + 1)
                        nc.gpsimd.tensor_tensor(xs[k][:], bc(xa[h][:, k, :].unsqueeze(2), [P, D, 8]),
                                                bc(val[:, ds(s, 1), 1:9], [P, D, 8]), ALU.mult).then_inc(s_xs, 1)
                    pool.wait_ge(s_xs, (g + 1) * U)

        @block.sync
        def _(sp):
            def groups(i):
                for h in range(RING):
                    g = i * RING + h
                    sp.wait_ge(s_x, g + 1)
                    sp.dma_start(R[h][:].rearrange("p u d -> p (u d)"), G[:, ds(g * (U * D), U * D)]
                                 ).then_inc(s_R[h], 16)
                    if not isinstance(i, int):
                        sp.wait_ge(s_k, g * U - U)
                    sp.dma_start(g2[h][:], hidden[:, ds(g * W, W)]).then_inc(s_g2[h], 16)

            groups(0)
            with sp.Fori(1, ITERS) as i:
                groups(i)

        @block.vector
        def _(dve):
            V = nc.vector

            def add(s, j, blk):
                dve.wait_ge(s_seg, s + 1)
                d = acc[:, ds(blk, 1), 0:OUTER].rearrange("p a f -> p (a f)")
                V.tensor_tensor(d, d, ps_sd[j][:], ALU.add).then_inc(s_acc, 1)
                d = acc[:, ds(blk, 1), OUTER:].rearrange("p a f -> p (a f)")
                V.tensor_tensor(d, d, ps_s0[j], ALU.add).then_inc(s_acc, 1)
                dve.wait_ge(s_acc, 2 * s + 2 + 4)

            def groups(i):
                for h in range(RING):
                    g = i * RING + h
                    at = g * U
                    V.tensor_tensor(H[h][:], bc(c.iota[:, None, :], [P, U, P]),
                                    bc(c.locD[:, ds(at, U)].unsqueeze(2), [P, U, P]), ALU.is_equal).then_inc(s_h, 1)
                    before = some(nc, DVE, c.prevD, at, U, BLOCKS - 1)
                    V.tensor_scalar(Y0[h][:, :, D:M], WE[:, ds(at, U), :], 1.0, None, ALU.mult).then_inc(s_y0, 1)
                    dve.wait_ge(s_x, g + RING + 1)
                    dve.wait_ge(s_0, g + 1)
                    V.tensor_tensor(Y0[h][:, :, 0:D], ps_0, x0[h][:], ALU.mult).then_inc(s_y0, 1)
                    for k in range(U):
                        s = at + k
                        first = isinstance(i, int) and h == 0 and k == 0
                        dve.wait_ge(s_k, s + 1)
                        dve.wait_ge(s_xs, s + 1)
                        V.tensor_tensor(Yd[k][:], ps_d[k % 2][:].rearrange("p (d s) -> p d s", s=8),
                                        xs[k][:], ALU.mult).then_inc(s_d, 1)
                        if not first:
                            add(s - 1, (k + 1) % 2, before[k])

            dve.sem_inc(s_y0, 2 * RING)
            dve.sem_inc(s_d, U)
            V.memset(acc[:], 0.0).then_inc(s_z, 1)
            dve.wait_ge(s_z, 1)
            dve.sem_inc(s_acc, 4)
            groups(0)
            with dve.Fori(1, ITERS) as i:
                groups(i)
            blk = dve.value_load(c.blkD[0:1, 0, STEPS - 1:STEPS], min_val=0, max_val=BLOCKS - 1)
            add(STEPS - 1, 1, blk)

        @block.tensor
        def _(pe):
            T = nc.tensor

            def segment(s, k, h):
                pe.wait_ge(s_d, s + 1 + U)
                pe.wait_ge(s_acc, 2 * s + 2)
                T.matmul(ps_sd[k % 2][:], H[h][:, k, :], Yd[k][:].rearrange("p d s -> p (d s)"), start=True, stop=True)
                T.matmul(ps_s0[k % 2], H[h][:, k, :], Y0[h][:, k, :], start=True, stop=True).then_inc(s_seg, 1)

            def groups(i):
                for h in range(RING):
                    g = i * RING + h
                    pe.wait_ge(s_g2[h], (i + 1) * 16)
                    if not (isinstance(i, int) and h == 0):
                        pe.wait_ge(s_y0, 2 * g + 2 * RING)
                    for k in range(U):
                        last = T.matmul(ps_0[:, k, :], g2[h][:, k * P:(k + 1) * P], V3[:, 0:D], start=True, stop=True)
                    last.then_inc(s_0, 1)
                    for k in range(U):
                        s = g * U + k
                        pe.wait_ge(s_d, s + U - 1)
                        last = T.matmul(ps_d[k % 2][:], g2[h][:, k * P:(k + 1) * P], V3[:, D:F1], start=True, stop=True)
                        last.then_inc(s_k, 1)
                        if k == 1:
                            pe.wait_ge(s_h, g + 1)
                            pe.wait_ge(s_y0, 2 * g + 2 + 2 * RING)
                        if k or not isinstance(i, int) or h:
                            segment(s - 1, (k - 1) % U, h if k else (h + 1) % RING)

            groups(0)
            with pe.Fori(1, ITERS) as i:
                groups(i)
            segment(STEPS - 1, U - 1, 1)


def layer1_output(nc, c, acc):
    sb, pb, sem, a = c.sb, c.pb, c.sem, c.a
    name = "l1o"
    Z = OUTER + D
    with ExitStack() as st:
        z = sb(name + "z", [P, BLOCKS, HEADS], F32, st)
        zero = sb(name + "zero", [P, BLOCKS, HEADS], F32, st)
        Wo = sb(name + "Wo", [P, 5, D], F32, st)
        aT = [sb(f"{name}aT{j}", [P, 5, P], F32, st) for j in range(2)]
        ps_t = [pb(f"{name}ps_t{j}", [P, 4, P], st) for j in range(2)]
        ps_u = [pb(f"{name}ps_u{j}", [D, BANK], st)[:, 0:P] for j in range(2)]
        ps_o = [pb(f"{name}ps_o{j}", [P, BANK], st)[:, 0:D] for j in range(2)]
        s_in = sem(name + "in"); s_v = sem(name + "v"); s_q = sem(name + "q"); s_r = sem(name + "r")
        s_s = sem(name + "s"); s_t = sem(name + "t"); s_c = sem(name + "c"); s_o = sem(name + "o")
        s_x = sem(name + "x")
        block = st.enter_context(nc.Block(name))

        @block.sync
        def _(sp):
            sp.dma_start(Wo[:, 0:4, :], a["l1_W_out"][D:F1, :].rearrange("(c p) o -> p c o", p=P)).then_inc(s_in, 16)
            sp.dma_start(Wo[0:D, 4, :], a["l1_W_out"][0:D, :]).then_inc(s_in, 16)

        @block.vector
        def _(dve):
            V = nc.vector
            v = Chain(dve, s_v)
            v.link(V.tensor_scalar(zero[:], acc[:, :, Z:Z + HEADS], 0.0, None, ALU.is_equal))
            v.link(V.tensor_tensor(z[:], acc[:, :, Z:Z + HEADS], zero[:], ALU.add))
            v.link(V.tensor_copy(c.deg[:].unsqueeze(2), acc[:, :, Z + HEADS:Z + HEADS + 1]))
            V.reciprocal(z[:], z[:]).then_inc(s_q, 1)
            dve.wait_ge(s_r, 1)
            for n, (d0, d1) in enumerate(HEAD_D):
                part = acc[:, :, 8 * d0:8 * d1]
                v.link(V.tensor_tensor(part, part, bc(z[:, :, n:n + 1], [P, BLOCKS, 8 * (d1 - d0)]), ALU.mult))
            part = acc[:, :, OUTER:Z]
            V.tensor_tensor(part, part, bc(z[:, :, 0:1], [P, BLOCKS, D]), ALU.mult).then_inc(s_s, 1)
            for b in range(BLOCKS):
                dve.wait_ge(s_o, b + 1)
                V.tensor_tensor(c.x[:, b, :], c.x[:, b, :], ps_o[b % 2], ALU.add).then_inc(s_x, 1)

        @block.scalar
        def _(act):
            act.wait_ge(s_q, 1)
            nc.scalar.activation(z[:], z[:], ACT.Sqrt).then_inc(s_r, 1)
            for b in range(BLOCKS):
                act.wait_ge(s_t, b + 1)
                if b >= 2:
                    act.wait_ge(s_o, b - 1)
                nc.scalar.copy(aT[b % 2][:, 0:4, :], ps_t[b % 2][:]).then_inc(s_c, 1)
                nc.scalar.copy(aT[b % 2][0:D, 4, :], ps_u[b % 2]).then_inc(s_c, 1)

        @block.tensor
        def _(pe):
            T = nc.tensor
            pe.wait_ge(s_s, 1)
            pe.wait_ge(s_in, 32)

            def turn(b):
                if b >= 2:
                    pe.wait_ge(s_c, 2 * (b - 1))
                for j in range(4):
                    T.transpose(ps_t[b % 2][:, j, :], acc[:, b, j * P:(j + 1) * P], c.ident[:])
                T.transpose(ps_u[b % 2], acc[:, b, OUTER:Z], c.ident[:]).then_inc(s_t, 1)

            turn(0)
            for b in range(BLOCKS):
                if b + 1 < BLOCKS:
                    turn(b + 1)
                pe.wait_ge(s_c, 2 * (b + 1))
                if b >= 2:
                    pe.wait_ge(s_x, b - 1)
                for j in range(4):
                    T.matmul(ps_o[b % 2], aT[b % 2][:, j, :], Wo[:, j, :], start=(j == 0), stop=False)
                T.matmul(ps_o[b % 2], aT[b % 2][0:D, 4, :], Wo[0:D, 4, :], start=False, stop=True).then_inc(s_o, 1)


def finish(nc, c):
    s_out = c.sem("out")
    with nc.Block("finish") as block:
        @block.sync
        def _(sp):
            sp.dma_start(c.out.rearrange("(b p) d -> p b d", p=P), c.x[:]).then_inc(s_out, 16)
            sp.wait_ge(s_out, 16)


def prepare(nc, c):
    st, banks = ExitStack(), ExitStack()
    sb, pb, sem, a = c.sb, c.pb, c.sem, c.a
    NB = BLOCKS
    with st:
        recD = sb("recD", [P, STEPS + U, 4], I32, st)
        frecD = sb("frecD", [P, STEPS, 9], F32, st)
        srcI = sb("srcI", [P, TPAD, 4], I32, st)
        dstI = sb("dstI", [P, TILES], I32, st)
        srcB = sb("srcB", [P, TPAD], F32, st)
        srcL = sb("srcL", [P, TPAD], F32, st)
        dstB = sb("dstB", [P, TILES], F32, st)
        srcF = sb("srcF", [P, TPAD], F32, st)
        tmpI = sb("tmpI", [P, TPAD], I32, st)
        junk = sb("junk", [P, TPAD], F32, st)
        junk2 = sb("junk2", [P, STEPS], F32, st)
        cntp = sb("cntp", [P, 2, 32], F32, st)
        cnt = sb("cnt", [P, 2, 32], F32, st)
        tilesI = sb("tilesI", [P, 2, 32], I32, st)
        tiles = sb("tiles", [P, 2, 32], F32, st)
        first = sb("first", [P, 2, 33], F32, st)
        shift = sb("shift", [P, 32], F32, st)
        steps = sb("steps", [P, STEPS], F32, st)
        blk = sb("blk", [P, 2, STEPS], F32, st)
        off = sb("off", [P, STEPS], F32, st)
        seven = sb("seven", [P, 2, STEPS], F32, st)
        before = sb("before", [P, P], F32, st)
        after = sb("after", [P, P], F32, st)
        prev = sb("prev", [P, P], F32, st)
        nxt = sb("nxt", [P, P], F32, st)
        Hr = [sb(f"Hr{h}", [P, U, P], BF16, st) for h in range(RING)]
        Hb = [sb(f"Hb{h}", [P, U, NB], BF16, st) for h in range(RING)]
        HT = [sb(f"HT{h}", [P, W], F32, st) for h in range(RING)]
        eq = sb("eq", [P, U, P], F32, st)
        low = sb("low", [P, W], I32, st)
        row = [sb(f"row{h}", [P, W], I32, st) for h in range(RING)]
        rank = sb("rank", [P, RING, U], F32, st)
        C = sb("C", [P, RING, U, NB], F32, st)
        Cc = sb("Cc", [P, NB], F32, st)
        sel = sb("sel", [P, U, NB], F32, st)
        pos = sb("pos", [P, U], F32, st)
        posI = sb("posI", [P, U], I32, st)
        posA = sb("posA", [P, U], I32, st)
        posB = sb("posB", [P, U], I32, st)
        idx = [sb(f"idx{h}", [P, U], I32, st) for h in range(RING)]
        rbuf = [sb(f"rbuf{h}", [P, U, 4], I32, st) for h in range(RING)]
        ps_cnt = pb("ps_cnt", [P, BANK], banks)
        ps_hist = pb("ps_hist", [P, BANK], banks)
        ps_base = pb("ps_base", [P, BANK], banks)
        ps_new = [pb(f"ps_new{h}", [P, U, NB], banks) for h in range(RING)]
        ps_sel = [pb(f"ps_sel{h}", [P, U, NB], banks) for h in range(RING)]

        s_const = sem("p_const"); s_cchain = sem("p_cchain")
        s_in = sem("p_in"); s_fill = sem("p_fill"); s_fill0 = sem("p_fill0")
        s_v = sem("p_v"); s_cntp = sem("p_cntp"); s_cnt = sem("p_cnt"); s_off = sem("p_off")
        s_rec = sem("p_rec"); s_frec = sem("p_frec")
        s_h1 = sem("p_hist_onehot"); s_h1u = sem("p_hist_used"); s_base0 = sem("p_hist_done")
        s_cs = sem("p_cnt_copied"); s_base = sem("p_base")
        s_oh = sem("p_onehots"); s_new = sem("p_new_counts"); s_C = sem("p_counts_set")
        s_selr = sem("p_sel_ready"); s_idx = sem("p_idx"); s_vl = sem("p_vl"); s_ht = sem("p_turned_onehots")
        s_row = [sem(f"p_row{h}") for h in range(RING)]
        s_rowu = sem("p_row_used")
        s_sc = [sem(f"p_scatter{h}") for h in range(RING)]

        block = banks.enter_context(nc.Block("prepare"))

        @block.sync
        def _(sp):
            sp.dma_start(srcI[:], a["edges_by_partition"]).then_inc(s_in, 16)
            sp.dma_start(dstI[:], a["dst_by_partition"]).then_inc(s_in, 16)
            sp.dma_start(c.x[:], a["x"].rearrange("(b p) d -> p b d", p=P)).then_inc(s_in, 16)
            sp.wait_ge(s_fill0, 2)
            sp.dma_start(c.recS_dram.rearrange("(p s) f -> p (s f)", p=P),
                         c.recS[:, 0:STEPS, :].rearrange("p s f -> p (s f)")).then_inc(s_fill, 16)
            rows = a["src_by_tile"]

            def values(g):
                e0 = some(nc, SP, c.edge0, g * U, U, E)
                for k in range(U):
                    sp.dma_start(frecD[:, ds(g * U + k, 1), :].rearrange("p a f -> p (a f)"),
                                 a["edge_values"][ds(e0[k], P), :]).then_inc(s_frec, 16)

            sp.wait_ge(s_off, 1)
            with sp.Fori(0, TITERS) as i:
                for h in range(RING):
                    values(i * RING + h)
                    sp.wait_ge(s_rowu, (i * RING + h + 1) * U)
                    sp.dma_start(row[h][:], rows[ds((i * RING + h) * W, W)].partition_broadcast(P)
                                 ).then_inc(s_row[h], 16)
            with sp.Fori(TGROUPS, GROUPS) as g:
                values(g)
            sp.wait_ge(s_frec, 16 * STEPS)
            for h in range(RING):
                sp.wait_ge(s_rowu, (TGROUPS + h + 1) * U)
                sp.dma_start(row[h][:], rows[(TGROUPS + h) * W:(TGROUPS + h + 1) * W].partition_broadcast(P)
                             ).then_inc(s_row[h], 16)
            for h in range(RING):
                sp.wait_ge(s_row[h], 16 * (TITERS + 1))

        @block.gpsimd
        def _(pool):
            g = Chain(pool, s_cchain)
            nc.gpsimd.iota(c.iota[:], pattern=[[1, P]], base=0, channel_multiplier=0,
                           allow_small_or_imprecise_dtypes=True).then_inc(s_const, 1)
            nc.gpsimd.iota(c.iota_p[:], pattern=[[0, 1]], base=0, channel_multiplier=1,
                           allow_small_or_imprecise_dtypes=True).then_inc(s_const, 1)
            nc.gpsimd.iota(steps[:], pattern=[[1, STEPS]], base=0, channel_multiplier=0,
                           allow_small_or_imprecise_dtypes=True).then_inc(s_const, 1)
            nc.gpsimd.memset(c.zeros[:], 0.0).then_inc(s_const, 1)
            g.link(nc.gpsimd.memset(c.ident[:], 0.0))
            g.link(nc.gpsimd.memset(prev[:], 0.0))
            g.link(nc.gpsimd.memset(nxt[:], 0.0))
            g.link(nc.gpsimd.memset(c.ones[:], 1.0))
            for t, base in ((c.ident, 0), (prev, 1), (nxt, -1)):
                nc.gpsimd.affine_select(out=t[:], in_=t[:], compare_op=ALU.not_equal, fill=1.0, base=base,
                                        pattern=[[-1, P]], channel_multiplier=1).then_inc(s_const, 1)
            nc.gpsimd.affine_select(out=before[:], in_=c.ones[:], compare_op=ALU.is_gt, fill=0.0, base=0,
                                    pattern=[[-1, P]], channel_multiplier=1).then_inc(s_const, 1)
            nc.gpsimd.affine_select(out=after[:], in_=c.ones[:], compare_op=ALU.is_gt, fill=0.0, base=0,
                                    pattern=[[1, P]], channel_multiplier=-1).then_inc(s_const, 1)
            pool.wait_ge(s_fill, 16)
            with pool.Fori(0, TITERS) as i:
                for h in range(RING):
                    pool.wait_ge(s_idx, i * RING + h + 1)
                    apart(pool, c.s_apart)
                    for k in range(U):
                        last = nc.gpsimd.indirect_dma_start(
                            out=c.recS_dram, out_offset=bass.IndirectOffsetOnAxis(ap=idx[h][:, k:k + 1], axis=0),
                            in_=rbuf[h][:, k, :], in_offset=None)
                        last.then_inc(s_sc[h], 16)
            for h in range(RING):
                pool.wait_ge(s_sc[h], TITERS * U * 16)

        CONSTS = 9

        @block.scalar
        def _(act):
            act.wait_ge(s_off, 1)
            with act.Fori(0, GROUPS) as g:
                e0 = some(nc, ACTIVATION, c.edge0, g * U, U, E)
                for k in range(U):
                    s = g * U + k
                    act.dma_start(recD[:, ds(s, 1), :].rearrange("p a f -> p (a f)"),
                                  a["edges"][ds(e0[k], P), :]).then_inc(s_rec, 16)
            act.wait_ge(s_rec, 16 * STEPS)

        @block.vector
        def _(dve):
            v = Chain(dve, s_v)
            V = nc.vector
            v.link(V.memset(c.recS[:], 0))
            V.memset(c.recS[:, 0:STEPS, 0:1], NONE).then_inc(s_fill0, 2)
            v.link(V.memset(recD[:, STEPS:, :], 0))
            v.link(V.memset(c.locD[:], float(NONE)))
            v.link(V.memset(c.locS[:], float(NONE)))
            v.link(V.memset(cntp[:], 0.0))
            v.link(V.memset(first[:], 0.0))
            dve.wait_ge(s_in, 48)
            dve.wait_ge(s_const, CONSTS)
            src = srcI[:, :, 0]
            v.link(V.tensor_scalar(tmpI[:], src, 7, None, ALU.logical_shift_right))
            v.link(V.tensor_copy(srcB[:], tmpI[:]))
            v.link(V.tensor_scalar(tmpI[:], src, 127, None, ALU.bitwise_and))
            v.link(V.tensor_copy(srcL[:], tmpI[:]))
            v.link(V.tensor_copy(srcF[:], src))
            v.link(V.tensor_scalar(tmpI[:, 0:TILES], dstI[:], 7, None, ALU.logical_shift_right))
            v.link(V.tensor_copy(dstB[:], tmpI[:, 0:TILES]))
            for o, t in ((0, dstB[:]), (1, srcB[:, 0:TILES])):
                for b in range(NB):
                    v.link(V.tensor_scalar(junk[:, 0:TILES], t, float(b), None, ALU.is_equal, ALU.add,
                                           accum_out=cntp[:, o, b:b + 1]))
            V.tensor_copy(junk[:, 0:1], cntp[:, 0, 0:1]).then_inc(s_cntp, 1)
            dve.wait_ge(s_cnt, 1)
            v.link(V.tensor_copy(cnt[:].rearrange("p o b -> p (o b)"), ps_cnt[:, 0:64]))
            v.link(V.tensor_scalar(tilesI[:], cnt[:], float(P - 1), None, ALU.add))
            v.link(V.tensor_scalar(tilesI[:], tilesI[:], 7, None, ALU.logical_shift_right))
            v.link(V.tensor_copy(tiles[:], tilesI[:]))
            for o in range(2):
                v.link(V.tensor_tensor_scan(first[:, o, 1:33], c.ones[:, 0:32], tiles[:, o, :], 0.0, ALU.mult, ALU.add))
            v.link(V.scalar_tensor_tensor(shift[:], tiles[:, 0, :], -float(P), cnt[:, 0, :], ALU.mult, ALU.add))
            v.link(V.memset(blk[:], 0.0))
            v.link(V.memset(seven[:], 0.0))
            v.link(V.tensor_scalar(off[:], steps[:], float(P), None, ALU.mult))
            for b in range(1, NB):
                for o in range(2):
                    v.link(V.scalar_tensor_tensor(blk[:, o, :], steps[:], first[:, o, b:b + 1], blk[:, o, :],
                                                  ALU.is_ge, ALU.add))
                v.link(V.tensor_scalar(junk2[:], steps[:], first[:, 0, b:b + 1], shift[:, b - 1:b],
                                       ALU.is_ge, ALU.mult))
                v.link(V.tensor_tensor(off[:], off[:], junk2[:], ALU.add))
            v.link(V.tensor_scalar(off[:], off[:], float(E), None, ALU.min))
            v.link(V.memset(c.edge0[:, STEPS:], E))
            V.tensor_copy(c.edge0[:, 0:STEPS], off[0:1, :]).then_inc(s_off, 1)
            for k in range(1, 4):
                v.link(V.scalar_tensor_tensor(seven[:], blk[:], 7.0 * k, seven[:], ALU.is_ge, ALU.add))
            v.link(V.tensor_scalar(seven[:], seven[:], float(BANK - 7 * AGG), None, ALU.mult))
            v.link(V.scalar_tensor_tensor(seven[:], blk[:], float(AGG), seven[:], ALU.mult, ALU.add))
            for o, t in ((0, c.blkD), (1, c.blkS)):
                v.link(V.memset(t[:], 0))
                v.link(V.tensor_copy(t[:, 0, 0:STEPS], blk[0:1, o, :]))
                v.link(V.tensor_copy(t[:, 1, 0:STEPS], seven[0:1, o, :]))
            v.link(V.memset(c.prevD[:, 0:1], 0))
            v.link(V.tensor_copy(c.prevD[:, 1:STEPS], blk[0:1, 0, 0:STEPS - 1]))
            dve.sem_inc(s_h1u, RING)
            with dve.Fori(0, TITERS) as i:
                for h in range(RING):
                    at = i * (RING * U) + h * U
                    dve.wait_ge(s_h1u, i * RING + h + 1)
                    V.tensor_tensor(Hb[h][:], bc(c.iota[:, None, 0:NB], [P, U, NB]),
                                    bc(srcB[:, ds(at, U)].unsqueeze(2), [P, U, NB]), ALU.is_equal).then_inc(s_h1, 1)
                    V.tensor_tensor(Hr[h][:], bc(c.iota[:, None, :], [P, U, P]),
                                    bc(srcL[:, ds(at, U)].unsqueeze(2), [P, U, P]), ALU.is_equal).then_inc(s_h1, 1)
            dve.wait_ge(s_base0, 1)
            v.link(V.tensor_copy(junk[:, 0:NB], ps_hist[:, 0:NB]))
            V.tensor_copy(Cc[:], junk[:, 0:NB]).then_inc(s_cs, 1)
            dve.wait_ge(s_base, 1)
            dve.wait_ge(s_cs, 1)
            v.link(V.scalar_tensor_tensor(Cc[:], first[:, 1, 0:NB], float(P), ps_base[:, 0:NB], ALU.mult, ALU.add))

            def block_onehot(g, h):
                V.tensor_tensor(Hb[h][:], bc(c.iota[:, None, 0:NB], [P, U, NB]),
                                bc(srcB[:, ds(g * U, U)].unsqueeze(2), [P, U, NB]), ALU.is_equal).then_inc(s_oh, 1)

            def node_onehot(g, h):
                V.tensor_tensor(Hr[h][:], bc(c.iota[:, None, :], [P, U, P]),
                                bc(srcL[:, ds(g * U, U)].unsqueeze(2), [P, U, P]), ALU.is_equal).then_inc(s_oh, 1)

            def low_bits(h, rows, ch):
                dve.wait_ge(s_row[h], rows)
                return ch.inc(V.tensor_scalar(low[:], row[h][:], 127, None, ALU.bitwise_and))

            def ranks(g, h, tiles):
                for k in tiles:
                    V.scalar_tensor_tensor(eq[:, k, :], row[h][:, k * P:(k + 1) * P], srcF[:, ds(g * U + k, 1)],
                                           before[:], ALU.is_equal, ALU.mult,
                                           accum_out=rank[:, h, k:k + 1]).then_inc(s_rowu, 1)

            def turned_onehot(h, n):
                dve.wait_ge(s_vl, n)
                V.tensor_scalar(HT[h][:], low[:], c.iota_p[:, 0:1], None, ALU.is_equal).then_inc(s_ht, 1)

            def free_positions(h, k, n, ch):
                dve.wait_ge(s_vl, n)
                return ch.inc(V.tensor_tensor(C[:, h, k, :], C[:, h, k - 1, :], ps_new[h][:, k - 1, :], ALU.add))

            def carry_on(h, n):
                dve.wait_ge(s_vl, n)
                V.tensor_tensor(Cc[:], C[:, h, U - 1, :], ps_new[h][:, U - 1, :], ALU.add).then_inc(s_C, 1)

            def sort_groups(i):
                for h in range(RING):
                    g = i * RING + h
                    f = g + RING
                    hn = (h + 1) % RING
                    ch = Chain(dve, s_vl, VSTART + g * VEACH)
                    dve.wait_ge(s_selr, g + 1)
                    t = ch.inc(V.tensor_tensor(sel[:], ps_sel[h][:], Hb[h][:], ALU.mult))
                    dve.wait_ge(s_C, g + 1)
                    n = ch.inc(V.tensor_copy(C[:, hn, 0, :], Cc[:]))
                    dve.wait_ge(s_vl, t)
                    t = ch.inc(V.tensor_reduce(pos[:], sel[:], AX.X, ALU.add))
                    block_onehot(f, h)
                    dve.wait_ge(s_new, g + 2)
                    n = free_positions(hn, 1, n, ch)
                    dve.wait_ge(s_vl, t)
                    t = ch.inc(V.tensor_tensor(posI[:], pos[:], rank[:, h, :], ALU.add))
                    n = free_positions(hn, 2, n, ch)
                    dve.wait_ge(s_vl, t)
                    ch.inc(V.tensor_scalar(posA[:], posI[:], 127, None, ALU.bitwise_and))
                    t = ch.inc(V.tensor_scalar(posB[:], posI[:], 7, None, ALU.logical_shift_right))
                    n = free_positions(hn, 3, n, ch)
                    l = low_bits(h, i * 16 + 32, ch)
                    carry_on(hn, n)
                    if not isinstance(i, int):
                        dve.wait_ge(s_sc[h], i * (16 * U))
                    dve.wait_ge(s_vl, t)
                    r = ch.inc(V.tensor_scalar(rbuf[h][:], srcI[:, ds(g * U, U), :], 1, None, ALU.mult))
                    V.scalar_tensor_tensor(idx[h][:], posA[:], STEPS, posB[:], ALU.mult, ALU.add).then_inc(s_idx, 1)
                    node_onehot(f, h)
                    turned_onehot(h, l)
                    ranks(f, h, range(U))
                    dve.wait_ge(s_rowu, (f + RING + 1) * U)
                    dve.wait_ge(s_vl, r)
                    dve.wait_ge(s_idx, g + 1)
                    assert ch.n == VEACH

            VSTART, VEACH = RING + U, 1 + U + 6
            dve.sem_inc(s_rowu, RING * U)
            ch = Chain(dve, s_vl)
            for h in range(RING):
                block_onehot(h, h)
                node_onehot(h, h)
                turned_onehot(h, low_bits(h, 16, ch))
                ranks(h, h, range(U))
                dve.wait_ge(s_rowu, (h + RING + 1) * U)
                dve.wait_ge(s_ht, h + 1)
            n = ch.inc(V.tensor_copy(C[:, 0, 0, :], Cc[:]))
            dve.wait_ge(s_new, 1)
            for k in range(1, U):
                n = free_positions(0, k, n, ch)
            carry_on(0, n)
            assert ch.n == VSTART
            sort_groups(0)
            with dve.Fori(1, TITERS) as i:
                sort_groups(i)

        @block.tensor
        def _(pe):
            T = nc.tensor
            pe.wait_ge(s_const, CONSTS)
            pe.wait_ge(s_cchain, 4)
            pe.wait_ge(s_cntp, 1)
            T.matmul(ps_cnt[:, 0:64], c.ones[:], cntp[:].rearrange("p o b -> p (o b)"), start=True, stop=True
                     ).then_inc(s_cnt, 1)
            T.matmul(ps_hist[:], c.zeros[:, 0:P], c.zeros[:], start=True, stop=True)
            with pe.Fori(0, TITERS) as i:
                for h in range(RING):
                    pe.wait_ge(s_h1, (i * RING + h + 1) * 2)
                    for k in range(U):
                        last = T.matmul(ps_hist[:, 0:NB], Hr[h][:, k, :], Hb[h][:, k, :], start=False, stop=True,
                                        skip_group_check=True)
                    last.then_inc(s_h1u, 1)
            pe.wait_ge(s_h1u, TGROUPS + RING)
            pe.sem_inc(s_base0, 1)
            pe.wait_ge(s_cs, 1)
            T.matmul(ps_base[:, 0:NB], after[:], Cc[:], start=True, stop=True).then_inc(s_base, 1)
            def new_counts(g, h):
                pe.wait_ge(s_oh, (g + 1) * 2)
                for k in range(U):
                    last = T.matmul(ps_new[h][:, k, :], Hr[h][:, k, :], Hb[h][:, k, :], start=True, stop=True)
                last.then_inc(s_new, 1)

            new_counts(0, 0)
            with pe.Fori(0, TITERS) as i:
                for h in range(RING):
                    g = i * RING + h
                    pe.wait_ge(s_C, g + 1)
                    pe.wait_ge(s_ht, g + 1)
                    for k in range(U):
                        last = T.matmul(ps_sel[h][:, k, :], HT[h][:, k * P:(k + 1) * P], C[:, h, k, :],
                                        start=True, stop=True)
                    last.then_inc(s_selr, 1)
                    new_counts(g + 1, (h + 1) % RING)

        banks.close()
        slots(nc, c, blk, prev, nxt, recD, frecD)


def slots(nc, c, blk, prev, nxt, recD, frecD):
    st = ExitStack()
    sb, pb, sem = c.sb, c.pb, c.sem
    with st:
        node = sb("node", [P, 2, STEPS], F32, st)
        key = sb("key", [P, 2, STEPS], F32, st)
        ok = sb("ok", [P, 2, STEPS], F32, st)
        KT = sb("KT", [Q, 2, W + 1], F32, st)
        ps_key = [pb(f"ps_key{o}", [Q, BANK], st) for o in range(2)]
        ps_edge = pb("ps_edge", [Q, 4], st)
        srcs = sb("srcs", [P, STEPS + U], I32, st)
        LT = sb("LT", [Q, W], F32, st)
        ps_loc = pb("ps_loc", [Q, W], st)
        s_loc = sem("k_loc"); s_lt = sem("k_loc_turned"); s_ltc = sem("k_loc_copied")
        s_out = sem("k_out"); s_srcc = sem("k_srcs"); s_rs = sem("k_records"); s_v = sem("k_v"); s_key = sem("k_key"); s_t = sem("k_turned")
        s_c = sem("k_copied"); s_prev = sem("k_prev"); s_pen = sem("k_pen"); s_nxt = sem("k_next")
        block = st.enter_context(nc.Block("slots"))

        @block.sync
        def _(sp):
            sp.dma_start(c.recS[:, 0:STEPS, :].rearrange("p s f -> p (s f)"),
                         c.recS_dram.rearrange("(p s) f -> p (s f)", p=P)).then_inc(s_rs, 16)
            sp.dma_start(c.val_dram, frecD[:].rearrange("p s f -> p (s f)")).then_inc(s_out, 16)
            sp.wait_ge(s_srcc, 1)
            sp.dma_start(c.src_dram, srcs[:]).then_inc(s_out, 16)
            sp.dma_start(c.loc_dram[STEPS * P:].rearrange("(a f) -> a f", a=1), c.zeros[0:1, :]).then_inc(s_out, 16)
            sp.wait_ge(s_ltc, 1)
            sp.dma_start(c.loc_dram[0:STEPS * P].rearrange("(q f) -> q f", q=Q), LT[:]).then_inc(s_out, 16)
            sp.wait_ge(s_out, 64)

        @block.scalar
        def _(act):
            act.wait_ge(s_lt, 1)
            nc.scalar.copy(LT[:], ps_loc[:]).then_inc(s_ltc, 1)

        @block.vector
        def _(dve):
            V = nc.vector
            v = Chain(dve, s_v)
            V.tensor_copy(srcs[:], recD[:, :, 0]).then_inc(s_srcc, 1)
            v.link(V.tensor_copy(node[:, 0, :], recD[:, 0:STEPS, 1]))
            dve.wait_ge(s_rs, 16)
            v.link(V.tensor_copy(node[:, 1, :], c.recS[:, 0:STEPS, 0]))
            for o, loc in ((0, c.locD), (1, c.locS)):
                v.link(V.scalar_tensor_tensor(loc[:, 0:STEPS], blk[:, o, :], -float(P), node[:, o, :], ALU.mult, ALU.add))
                dve.sem_inc(s_loc, 1)
                v.link(V.tensor_scalar(ok[:, o, :], loc[:, 0:STEPS], 0.0, None, ALU.is_ge))
                v.link(V.scalar_tensor_tensor(ok[:, o, :], loc[:, 0:STEPS], float(P - 1), ok[:, o, :], ALU.is_le, ALU.mult))
                V.scalar_tensor_tensor(key[:, o, :], node[:, o, :], 1.0, ok[:, o, :], ALU.add, ALU.mult
                                       ).then_inc(s_key, 1)
            for o, pen in ((0, c.penD), (1, c.penS)):
                dve.wait_ge(s_t, o + 1)
                V.tensor_copy(KT[:, o, 1:W + 1], ps_key[o][:]).then_inc(s_c, 1)
                dve.wait_ge(s_prev, o + 1)
                v.link(V.tensor_copy(KT[:, o, 0:1], ps_edge[:, o:o + 1]))
                v.link(V.tensor_tensor(pen[:, 0:W], KT[:, o, 1:W + 1], KT[:, o, 0:W], ALU.not_equal))
                V.tensor_scalar(pen[:, 0:W], pen[:, 0:W], -BIG, None, ALU.mult).then_inc(s_pen, 1)
                dve.wait_ge(s_nxt, o + 1)
                v.link(V.tensor_copy(pen[:, W:W + 1], ps_edge[:, 2 + o:3 + o]))

        @block.tensor
        def _(pe):
            T = nc.tensor
            pe.wait_ge(s_loc, 1)
            for j in range(4):
                last = T.transpose(ps_loc[:, j * P:(j + 1) * P], c.locD[:, j:STEPS:4], c.ident[:])
            last.then_inc(s_lt, 1)
            for o, pen in ((0, c.penD), (1, c.penS)):
                pe.wait_ge(s_key, o + 1)
                for j in range(4):
                    last = T.transpose(ps_key[o][:, j * P:(j + 1) * P], key[:, o, j:STEPS:4], c.ident[:])
                last.then_inc(s_t, 1)
            for o, pen in ((0, c.penD), (1, c.penS)):
                pe.wait_ge(s_c, o + 1)
                T.matmul(ps_edge[:, o:o + 1], prev[0:Q, 0:Q], KT[:, o, W:W + 1], start=True, stop=True).then_inc(s_prev, 1)
                pe.wait_ge(s_pen, o + 1)
                T.matmul(ps_edge[:, 2 + o:3 + o], nxt[0:Q, 0:Q], pen[:, 0:1], start=True, stop=True).then_inc(s_nxt, 1)


def kernel(**inputs):
    import numpy as np
    import concourse.bacc as bacc
    from concourse.bass_utils import run_bass_kernel_spmd
    src, dst, typ = (np.asarray(inputs[k]) for k in ("src", "dst", "edge_type_64"))
    f = {k: np.asarray(v) for k, v in inputs.items()}
    full = TILES * P - E
    by_p = np.stack([np.pad(src, (0, full), constant_values=NP - 1), np.pad(dst, (0, full)),
                     np.pad(typ, (0, full)), np.zeros(E + full, src.dtype)], 1).reshape(P, TILES, 4)
    arrays = {
        "edges_by_partition": np.pad(by_p, ((0, 0), (0, TPAD - TILES), (0, 0))),
        "dst_by_partition": np.pad(dst, (0, full), constant_values=NP - 1).reshape(P, TILES),
        "src_by_tile": np.pad(by_p[:, :, 0].T, ((0, TPAD - TILES), (0, 0))).reshape(-1),
        "edges": np.stack([np.pad(v, (0, EPAD - E), constant_values=w)
                           for v, w in ((src, 0), (dst, NONE), (typ, 0), (src, 0))], 1),
        "edge_values": np.pad(np.concatenate([f["edge_weight"][:, None], f["edge_attr_8"]], 1),
                              ((0, EPAD - E), (0, 0))),
        "l0_WT": f["L0_gnn_W"].T,
        "l0_relT": f["L0_gnn_relation_emb"].T,
        "l1_edges": np.pad(f["edge_attr_64"], ((0, EPAD - E), (0, 0))).T,
        **{"l1_" + k: f["L1_gnn_" + k] for k in ("Wk1", "Wk2", "Wk3", "Wv1", "Wv2", "Wv3", "W_logit", "W_out")},
        **{"l2_" + k: f["L2_gnn_" + k] for k in ("W1", "b1", "gamma", "beta", "W2", "b2")},
        **{"l3_WT_" + k: f["L3_gnn_W_" + k].T for k in ("self", "neigh", "var")},
        **{"l3_b_" + k: f["L3_gnn_b_" + k] for k in ("self", "neigh", "var")},
        "x": np.pad(f["x"], ((0, NP - N), (0, 0))),
    }
    nc = bacc.Bacc("TRN2", target_bir_lowering=False, num_devices=1)
    arrays = {k: np.ascontiguousarray(v) for k, v in arrays.items()}
    aps = {k: nc.dram_tensor("in_" + k, v.shape, mybir.dt.from_np(v.dtype), kind="ExternalInput").ap()
           for k, v in arrays.items()}
    out = nc.dram_tensor("out", (NP, D), F32, kind="ExternalOutput").ap()
    program(nc, aps, out)
    r = run_bass_kernel_spmd(nc, [{"in_" + k: v for k, v in arrays.items()}], core_ids=[0])
    return r.results[0]["out"][:N]
```
